# Optimizing a Trainium2 kernel written in Bass

```python
import numpy as np
import jax
import jax.numpy as jnp

def _softmax(x, axis=-1):
    return jax.nn.softmax(x, axis=axis)

def _gelu(x):
    return jax.nn.gelu(x, approximate=True)

def _silu(x):
    return jax.nn.silu(x)

def _sigmoid(x):
    return jax.nn.sigmoid(x)

def _layernorm(x, axis=-1, eps=1e-05):
    m = jnp.mean(x, axis=axis, keepdims=True)
    v = jnp.var(x, axis=axis, keepdims=True)
    return (x - m) / jnp.sqrt(v + eps)

def _scatter_add(tgt, idx, src, axis=0):
    return tgt.at[idx].add(src)

def _segment_sum(src, seg, n):
    return jax.ops.segment_sum(src, seg, n)
kernel_name = 'mk_adj_resnorm_d4_adj_r2_834013'

def setup_inputs(seed: int=0):
    np.random.seed(seed)
    _w = jnp.asarray

    def _rec_inputs():
        import jax
        import jax.numpy as jnp
        _gk = jax.random.key(seed)
        x = -0.000929 + 1 * jax.random.normal(jax.random.fold_in(_gk, 1), (8, 1024, 64), jnp.float32)
        _a = jax.random.bernoulli(jax.random.fold_in(_gk, 2), 0.00195312, (1024, 1024))
        _a = jnp.logical_or(_a, jnp.swapaxes(_a, -1, -2))
        _a = jnp.logical_or(_a, jnp.eye(1024, dtype=bool))
        _af = _a.astype(jnp.float32)
        adj = _af
        return (x, adj)
    x, adj = _rec_inputs()

    def _L0_gnn_setup():
        import jax, jax.numpy as jnp
        import numpy as np
        NEG = -1000000000.0
        key = jax.random.key(seed)
        ks = jax.random.split(key, 14)
        B, N, E, NF, NH = (8, 1024, 64, 64, 64)
        x = jax.random.normal(ks[0], (B, N, NF), dtype=jnp.float32)
        base = jax.nn.one_hot(jax.random.randint(ks[1], (N,), 0, E), E, dtype=jnp.float32)
        extra = (jax.random.uniform(ks[2], (N, E)) < 0.03).astype(jnp.float32)
        H = jnp.clip(base + extra, 0.0, 1.0)
        adj = (jax.random.uniform(ks[3], (N, N)) < 0.01).astype(jnp.float32)
        adj = jnp.clip(adj + jnp.eye(N, dtype=jnp.float32), 0.0, 1.0)
        s_in = 1.0 / np.sqrt(NF)
        s_h = 1.0 / np.sqrt(NH)
        W = jax.random.normal(ks[4], (NF, NH), dtype=jnp.float32) * s_in
        W_ind = jax.random.normal(ks[5], (NF, NH), dtype=jnp.float32) * s_in
        a_node = jax.random.normal(ks[6], (NH,), dtype=jnp.float32) * s_h
        a_gn = jax.random.normal(ks[7], (NH,), dtype=jnp.float32) * s_h
        a_ge = jax.random.normal(ks[8], (NH,), dtype=jnp.float32) * s_h
        fcW = jax.random.normal(ks[9], (NH, 2 * NH), dtype=jnp.float32) * s_h
        fcb = jnp.zeros((2 * NH,), dtype=jnp.float32)
        av = jax.random.normal(ks[10], (2 * NH,), dtype=jnp.float32) / np.sqrt(2 * NH)
        return {'x': x, 'H': H, 'adj': adj, 'nhid': NH, 'W': W, 'W_ind': W_ind, 'a_node': a_node, 'a_gn': a_gn, 'a_ge': a_ge, 'fcW': fcW, 'fcb': fcb, 'av': av}
    _L0_gnn_all = _L0_gnn_setup()
    _L0_gnn_in = {k: v for k, v in _L0_gnn_all.items() if k in ('H', 'W', 'W_ind', 'a_node', 'a_gn', 'a_ge', 'fcW', 'fcb', 'av')}
    del _L0_gnn_all

    def _L1_gnn_setup():
        import jax, jax.numpy as jnp
        import numpy as np
        NEG_INF = -1e+16

        def gat_layer(x, graph, W, b):
            h = x @ W
            s = jnp.einsum('bnd,bmd->bnm', h, h) * graph
            s = jnp.where(s == 0.0, NEG_INF, s)
            a = jax.nn.softmax(s, axis=2)
            return jnp.einsum('bnm,bmd->bnd', a, h) + b
        key = jax.random.key(seed)
        k1, k2, k3, k4, k5, k6 = jax.random.split(key, 6)
        B, N, C_IN, HID, HEADS, C_OUT = (16, 512, 64, 128, 8, 64)
        flow_x = jax.random.normal(k1, (B, N, C_IN), dtype=jnp.float32)
        graph = jax.random.randint(k2, (N, N), 0, 2).astype(jnp.float32)
        Wh = jax.random.normal(k3, (HEADS, C_IN, HID), dtype=jnp.float32)
        bh = jax.random.normal(k4, (HEADS, HID), dtype=jnp.float32)
        W_out = jax.random.normal(k5, (HID * HEADS, C_OUT), dtype=jnp.float32)
        b_out = jax.random.normal(k6, (C_OUT,), dtype=jnp.float32)
        return {'flow_x': flow_x, 'graph': graph, 'Wh': Wh, 'bh': bh, 'W_out': W_out, 'b_out': b_out}
    _L1_gnn_all = _L1_gnn_setup()
    _L1_gnn_in = {k: v for k, v in _L1_gnn_all.items() if k in ('Wh', 'bh', 'W_out', 'b_out')}
    del _L1_gnn_all

    def _L2_gnn_setup():
        import jax, jax.numpy as jnp
        import numpy as np
        MAX_STEPS = 3
        key = jax.random.key(seed)
        ks = jax.random.split(key, 7)
        B, N, D = (1, 4096, 64)
        return {'causal_vars': jax.random.normal(ks[0], (B, N, D), dtype=jnp.float32), 'adj_matrix': jax.random.uniform(ks[1], (N, N), dtype=jnp.float32), 'intervention_value': jax.random.normal(ks[2], (B, D), dtype=jnp.float32), 'W1': jax.random.normal(ks[3], (D, 2 * D), dtype=jnp.float32) * (1.0 / np.sqrt(2 * D)), 'b1': jax.random.normal(ks[4], (D,), dtype=jnp.float32) * 0.01, 'W2': jax.random.normal(ks[5], (D, D), dtype=jnp.float32) * (1.0 / np.sqrt(D)), 'b2': jax.random.normal(ks[6], (D,), dtype=jnp.float32) * 0.01, 'intervention_idx': 0}
    _L2_gnn_all = _L2_gnn_setup()
    _L2_gnn_in = {k: v for k, v in _L2_gnn_all.items() if k in ('intervention_value', 'W1', 'b1', 'W2', 'b2')}
    del _L2_gnn_all

    def _L3_gnn_setup():
        import jax, jax.numpy as jnp
        import numpy as np
        CHEB_K = 3
        EMBED_DIM = 16
        DIM_IN = 64
        DIM_OUT = 64
        key = jax.random.key(seed)
        k1, k2, k3, k4, k5 = jax.random.split(key, 5)
        B, N, C, D = (32, 1024, DIM_IN, EMBED_DIM)
        x = jax.random.normal(k1, (B, N, C), dtype=jnp.float32)
        node_embeddings = jax.random.normal(k2, (N, D), dtype=jnp.float32)
        lap = jax.random.normal(k3, (N, N), dtype=jnp.float32) / jnp.sqrt(jnp.float32(N))
        weights_pool = jax.random.normal(k4, (D, CHEB_K + 1, C, DIM_OUT), dtype=jnp.float32) * 0.05
        bias_pool = jax.random.normal(k5, (D, DIM_OUT), dtype=jnp.float32) * 0.05
        return {'x': x, 'node_embeddings': node_embeddings, 'lap': lap, 'weights_pool': weights_pool, 'bias_pool': bias_pool}
    _L3_gnn_all = _L3_gnn_setup()
    _L3_gnn_in = {k: v for k, v in _L3_gnn_all.items() if k in ('node_embeddings', 'weights_pool', 'bias_pool')}
    del _L3_gnn_all
    return {'x': x, 'adj': adj, 'L0_gnn_H': _L0_gnn_in['H'], 'L0_gnn_W': _L0_gnn_in['W'], 'L0_gnn_W_ind': _L0_gnn_in['W_ind'], 'L0_gnn_a_node': _L0_gnn_in['a_node'], 'L0_gnn_a_gn': _L0_gnn_in['a_gn'], 'L0_gnn_a_ge': _L0_gnn_in['a_ge'], 'L0_gnn_fcW': _L0_gnn_in['fcW'], 'L0_gnn_fcb': _L0_gnn_in['fcb'], 'L0_gnn_av': _L0_gnn_in['av'], 'L1_gnn_Wh': _L1_gnn_in['Wh'], 'L1_gnn_bh': _L1_gnn_in['bh'], 'L1_gnn_W_out': _L1_gnn_in['W_out'], 'L1_gnn_b_out': _L1_gnn_in['b_out'], 'L2_gnn_intervention_value': _L2_gnn_in['intervention_value'], 'L2_gnn_W1': _L2_gnn_in['W1'], 'L2_gnn_b1': _L2_gnn_in['b1'], 'L2_gnn_W2': _L2_gnn_in['W2'], 'L2_gnn_b2': _L2_gnn_in['b2'], 'L3_gnn_node_embeddings': _L3_gnn_in['node_embeddings'], 'L3_gnn_weights_pool': _L3_gnn_in['weights_pool'], 'L3_gnn_bias_pool': _L3_gnn_in['bias_pool']}

def reference(x, adj, L0_gnn_H, L0_gnn_W, L0_gnn_W_ind, L0_gnn_a_node, L0_gnn_a_gn, L0_gnn_a_ge, L0_gnn_fcW, L0_gnn_fcb, L0_gnn_av, L1_gnn_Wh, L1_gnn_bh, L1_gnn_W_out, L1_gnn_b_out, L2_gnn_intervention_value, L2_gnn_W1, L2_gnn_b1, L2_gnn_W2, L2_gnn_b2, L3_gnn_node_embeddings, L3_gnn_weights_pool, L3_gnn_bias_pool):
    import jax
    import jax.numpy as jnp

    def _L0_gnn_ref(x, H, adj, nhid, W, W_ind, a_node, a_gn, a_ge, fcW, fcb, av):
        import jax, jax.numpy as jnp
        import numpy as np
        NEG = -1000000000.0
        h = x @ W
        maskEN = H.T
        s = jax.nn.leaky_relu(h @ a_node, 0.2)
        logits = jnp.where(maskEN[None, :, :] > 0, s[:, None, :], NEG)
        alpha = jax.nn.softmax(logits, axis=-1)
        agg = jnp.einsum('ben,bnf->bef', alpha, h)
        beta = jax.nn.sigmoid((h @ a_gn)[:, None, :] + (agg @ a_ge)[:, :, None])
        all_he = beta[..., None] * h[:, None, :, :] + (1.0 - beta[..., None]) * agg[:, :, None, :]
        deg = jnp.maximum(adj.sum(-1), 1.0)[:, None]
        industry = jnp.einsum('nm,bmf->bnf', adj / deg, x @ W_ind)
        all_he = jax.nn.elu(all_he)
        he = jax.nn.elu(agg)

        def attn_scores(f):
            return jnp.tanh(f @ fcW + fcb) @ av
        se = attn_scores(he)
        logits2 = jnp.where(H[None, :, :] > 0, se[:, None, :], NEG)
        coefs1 = jax.nn.softmax(logits2, axis=-1)
        g = jnp.einsum('bne,benf->bnf', coefs1, all_he)
        pair = jnp.stack([industry, g], axis=2)
        coefs2 = jax.nn.softmax(attn_scores(pair), axis=-1)
        out = jnp.einsum('bnk,bnkf->bnf', coefs2, pair)
        return out

    def _L1_gnn_ref(flow_x, graph, Wh, bh, W_out, b_out):
        import jax, jax.numpy as jnp
        import numpy as np
        NEG_INF = -1e+16

        def gat_layer(x, graph, W, b):
            h = x @ W
            s = jnp.einsum('bnd,bmd->bnm', h, h) * graph
            s = jnp.where(s == 0.0, NEG_INF, s)
            a = jax.nn.softmax(s, axis=2)
            return jnp.einsum('bnm,bmd->bnd', a, h) + b
        heads = jax.vmap(lambda W, b: gat_layer(flow_x, graph, W, b))(Wh, bh)
        H, B, N, D = heads.shape
        cat = jnp.moveaxis(heads, 0, 2).reshape(B, N, H * D)
        x = jax.nn.leaky_relu(cat, negative_slope=0.01)
        out = gat_layer(x, graph, W_out, b_out)
        return jax.nn.leaky_relu(out, negative_slope=0.01)

    def _L2_gnn_ref(causal_vars, adj_matrix, intervention_value, W1, b1, W2, b2, intervention_idx):
        import jax, jax.numpy as jnp
        import numpy as np
        MAX_STEPS = 3
        v = causal_vars.at[:, intervention_idx].set(intervention_value)
        for _ in range(MAX_STEPS):
            effects = jnp.einsum('nm,bmd->bnd', adj_matrix, v)
            h = jnp.concatenate([v, effects], axis=-1)
            h = jax.nn.relu(jnp.einsum('bnk,dk->bnd', h, W1) + b1)
            v = jnp.einsum('bnk,dk->bnd', h, W2) + b2
        return v

    def _L3_gnn_ref(x, node_embeddings, lap, weights_pool, bias_pool):
        import jax, jax.numpy as jnp
        import numpy as np
        CHEB_K = 3
        EMBED_DIM = 16
        DIM_IN = 64
        DIM_OUT = 64
        N = node_embeddings.shape[0]
        support_set = [jnp.eye(N, dtype=x.dtype), lap]
        for _ in range(2, CHEB_K):
            support_set.append(2.0 * lap @ support_set[-1] - support_set[-2])
        apt = jax.nn.softmax(jax.nn.relu(node_embeddings @ node_embeddings.T), axis=1)
        support_set.append(apt)
        supports = jnp.stack(support_set, axis=0)
        weights = jnp.einsum('nd,dkio->nkio', node_embeddings, weights_pool)
        bias = node_embeddings @ bias_pool
        x_g = jnp.einsum('knm,bmc->bknc', supports, x)
        x_g = jnp.transpose(x_g, (0, 2, 1, 3))
        out = jnp.einsum('bnki,nkio->bno', x_g, weights) + bias
        return out
    x = _layernorm(x + _L0_gnn_ref(x, L0_gnn_H, adj, 64, L0_gnn_W, L0_gnn_W_ind, L0_gnn_a_node, L0_gnn_a_gn, L0_gnn_a_ge, L0_gnn_fcW, L0_gnn_fcb, L0_gnn_av), axis=-1)
    x = _layernorm(x + _L1_gnn_ref(x, adj, L1_gnn_Wh, L1_gnn_bh, L1_gnn_W_out, L1_gnn_b_out), axis=-1)
    x = _layernorm(x + _L2_gnn_ref(x, adj, L2_gnn_intervention_value, L2_gnn_W1, L2_gnn_b1, L2_gnn_W2, L2_gnn_b2, 0), axis=-1)
    x = _layernorm(x + _L3_gnn_ref(x, L3_gnn_node_embeddings, adj, L3_gnn_weights_pool, L3_gnn_bias_pool), axis=-1)
    return x

_drawn_inputs = setup_inputs


def setup_inputs(seed=0):
    import zlib

    import numpy as np

    out = dict(_drawn_inputs(seed))
    spreads = {'L0_gnn_fcb': (0.0, 2.0)}
    factors = {'L0_gnn_H': 7.064,
     'L0_gnn_a_node': 3.05,
     'L0_gnn_a_ge': 8.0,
     'L1_gnn_b_out': 7.621,
     'L2_gnn_intervention_value': 30.336,
     'L2_gnn_b1': 8.0,
     'L2_gnn_b2': 8.0,
     'L3_gnn_bias_pool': 6.094,
     'L0_gnn_a_gn': 4.578}
    for name, (base, spread) in spreads.items():
        noise = np.random.default_rng([zlib.crc32(name.encode()), seed]).standard_normal(out[name].shape)
        drawn = base * np.exp(spread * noise) if base else spread * noise
        out[name] = jnp.asarray(drawn.astype(out[name].dtype))
    for name, factor in factors.items():
        out[name] = (out[name] * factor).astype(out[name].dtype)
    return out
```

```python
import concourse.bass as bass
from concourse import mybir
from contextlib import ExitStack

F32 = mybir.dt.float32
F32R = mybir.dt.float32r
BF16 = mybir.dt.bfloat16
ALU = mybir.AluOpType
ACT = mybir.ActivationFunctionType
AX = mybir.AxisListType

P = 128
BATCH, N, C = 8, 1024, 64
NT = N // P
HN = N // 2
HEADS, HC = 8, 128
EDGES = 64
PAIRS = BATCH // 2
MASKED = -1.0e16
NEG = -1.0e9
EPS = 1.0e-5
LOWEST = -3.0e38


def events(bank, names):
    names = names.split()
    assert len(names) <= len(bank)
    return dict(zip(names, bank))


def numbers(sems):
    every = [s.num for s in sems.values()]
    assert every == list(range(every[0], every[0] + len(every)))
    return range(every[0], every[0] + len(every))


def make_identity(pool, tile, zeroed, ready, before):
    pool.memset(tile[:, :], 0.0).then_inc(zeroed, 1)
    pool.wait_ge(zeroed, before + 1)
    pool.affine_select(out=tile[:, :], in_=tile[:, :], compare_op=ALU.not_equal, fill=1.0, base=0,
                       pattern=[[-1, tile.shape[1]]], channel_multiplier=1).then_inc(ready, 1)


def layer_norm_rows(nc, dve, link, y, sq, mean, var, rstd, var_ready, rstd_ready, done):
    groups = y.shape[1]

    def spread(v):
        return v.unsqueeze(2).broadcast_to([P, groups, C])

    link(nc.vector.tensor_reduce(mean, y, AX.X, ALU.add))
    link(nc.vector.tensor_scalar(mean, mean, 1.0 / C, None, ALU.mult))
    link(nc.vector.tensor_tensor(y, y, spread(mean), ALU.subtract))
    link(nc.vector.tensor_tensor(sq, y, y, ALU.mult))
    link(nc.vector.tensor_reduce(var, sq, AX.X, ALU.add))
    nc.vector.tensor_scalar(var, var, 1.0 / C, EPS, ALU.mult, ALU.add).then_inc(var_ready, 1)
    dve.wait_ge(rstd_ready, 1)
    nc.vector.tensor_tensor(y, y, spread(rstd), ALU.mult).then_inc(done, 1)


def transpose_adjacency(nc, bank, io, adjT_dram):
    ctx = ExitStack()
    with ctx:
        adj = ctx.enter_context(nc.sbuf_tensor("a_adj", [P, NT, N], F32))
        adjT = ctx.enter_context(nc.sbuf_tensor("a_adjT", [P, NT, N], F32))
        ident = ctx.enter_context(nc.sbuf_tensor("a_ident", [P, P], F32))
        ps = [ctx.enter_context(nc.psum_tensor(f"a_ps{k}", [P, N], F32)) for k in range(4)]
        e = events(bank, "a_loaded a_zeroed a_ident_ready a_transposed a_copied_even a_copied_odd a_stored")
        with nc.Block() as block:

            @block.sync
            def _(sp):
                for t in range(NT):
                    sp.dma_start(adj[:, t, :], io["adj"][t * P:(t + 1) * P, :]).then_inc(e["a_loaded"], 16)
                for t in range(NT):
                    sp.wait_ge(e["a_copied_even" if t % 2 == 0 else "a_copied_odd"], t // 2 + 1)
                    sp.dma_start(adjT_dram[t * P:(t + 1) * P, :], adjT[:, t, :]).then_inc(e["a_stored"], 16)
                sp.wait_ge(e["a_stored"], 16 * NT)

            @block.gpsimd
            def _(pool):
                make_identity(pool, ident, e["a_zeroed"], e["a_ident_ready"], 0)

            @block.tensor
            def _(pe):
                pe.wait_ge(e["a_ident_ready"], 1)
                pe.wait_ge(e["a_loaded"], 16 * NT)
                for t in range(NT):
                    if t >= 4:
                        pe.wait_ge(e["a_copied_even" if t % 2 == 0 else "a_copied_odd"], t // 2 - 1)
                    for s in range(NT):
                        mm = nc.tensor.transpose(ps[t % 4][:, s * P:(s + 1) * P], adj[:, s, t * P:(t + 1) * P], ident[:, :])
                    mm.then_inc(e["a_transposed"], 1)

            @block.vector
            def _(dve):
                for t in range(0, NT, 2):
                    dve.wait_ge(e["a_transposed"], t + 1)
                    nc.vector.tensor_copy(adjT[:, t, :], ps[t % 4][:, :]).then_inc(e["a_copied_even"], 1)

            @block.scalar
            def _(act):
                for t in range(1, NT, 2):
                    act.wait_ge(e["a_transposed"], t + 1)
                    nc.scalar.activation(adjT[:, t, :], ps[t % 4][:, :], ACT.Copy).then_inc(e["a_copied_odd"], 1)
        nc.all_engine_barrier(sems_to_clear=numbers(e))


def hypergraph_attention(nc, bank, io, adjT_dram, x_in, x_out):
    UNROLL = 4
    ctx = ExitStack()
    with ctx:
        def sb(name, shape, dt=F32):
            return ctx.enter_context(nc.sbuf_tensor(name, shape, dt))

        adjT = sb("h_adjT", [P, NT, N])
        inv_degree = sb("h_inv_degree", [P, N])
        ident = sb("h_ident", [P, P])
        ones = sb("h_ones", [P, P])
        pick = sb("h_pick", [P, EDGES, P], BF16)
        W_diag = sb("h_W_diag", [P, P])
        Wind_diag = sb("h_Wind_diag", [P, P])
        vectors = sb("h_vectors", [P, 3])
        spread3 = sb("h_spread3", [P, 3, P])
        fcW = sb("h_fcW", [P, P])
        fcb = sb("h_fcb", [P, 1])
        av = sb("h_av", [P, 1])
        av_half = sb("h_av_half", [P, 1])
        av_all = sb("h_av_all", [P, P])
        av_pair = sb("h_av_pair", [P, 2, 2, P])
        H_rows = sb("h_H_rows", [P, NT, 2, EDGES])
        mask_rows = sb("h_mask_rows", [P, NT, EDGES])
        fence_rows = sb("h_fence_rows", [P, NT, EDGES])
        maskT = sb("h_maskT", [P, N])
        fenceT = sb("h_fenceT", [P, N])
        x_rows = sb("h_x_rows", [P, NT, 2, C])
        xT = sb("h_xT", [P, N])
        hT = sb("h_hT", [P, N])
        half_hT = sb("h_half_hT", [P, N])
        h_rows = sb("h_h_rows", [P, NT, P])
        ind_rows = sb("h_ind_rows", [P, NT, P])
        indT = sb("h_indT", [P, N])
        gate_h = sb("h_gate_h", [P, N])
        logits = sb("h_logits", [P, N])
        alphaT = sb("h_alphaT", [P, NT, P])
        neg_max = sb("h_neg_max", [P, 1])
        row_sum = sb("h_row_sum", [P, 1])
        row_inv = sb("h_row_inv", [P, 1])
        agg_diag = sb("h_agg_diag", [P, P])
        aggT = sb("h_aggT", [P, EDGES])
        edge_table = sb("h_edge_table", [P, EDGES, 4])
        below = sb("h_below", [P, EDGES])
        above = sb("h_above", [P, EDGES])
        he = sb("h_he", [P, EDGES])
        z_edge = sb("h_z_edge", [P, P])
        se_all = sb("h_se_all", [P, 2, EDGES])
        max2 = sb("h_max2", [P, 2 * NT])
        sum2 = sb("h_sum2", [P, 2 * NT])
        inv2 = sb("h_inv2", [P, 2 * NT])
        coef_rows = sb("h_coef_rows", [P, NT, 2, EDGES])
        coef_rest = sb("h_coef_rest", [P, N])
        coef = sb("h_coef", [P, 3, N], BF16)
        edge_now = [sb(f"h_edge_now{k}", [P, 4]) for k in range(UNROLL)]
        pool_waiter = sb("h_pool_waiter", [P, 1])
        diff = [sb(f"h_diff{k}", [P, N]) for k in range(2)]
        gate = [sb(f"h_gate{k}", [P, N]) for k in range(2)]
        shifted = [sb(f"h_shifted{k}", [P, N]) for k in range(2)]
        expv = [sb(f"h_expv{k}", [P, N]) for k in range(2)]
        reluv = [sb(f"h_reluv{k}", [P, N]) for k in range(2)]
        weighted = [sb(f"h_weighted{k}", [P, N]) for k in range(2)]
        mean = sb("h_mean", [P, 2 * NT])
        var = sb("h_var", [P, 2 * NT])
        rstd = sb("h_rstd", [P, 2 * NT])
        minus_half = sb("h_minus_half", [P, 2 * NT])
        ps_c = [ctx.enter_context(nc.psum_tensor(f"h_ps_c{k}", [P, N], F32)) for k in range(2)]
        ps_g = ctx.enter_context(nc.psum_tensor("h_ps_g", [P, N], F32))
        ps_m = ctx.enter_context(nc.psum_tensor("h_ps_m", [P, N], F32))

        def column(v):
            return v.rearrange("(c o) -> c o", o=1)

        setup = events(bank, "h_w_loaded h_adj_loaded h_zeroed h_ident_ready h_w_zeroed h_ones_ready h_half_ready "
                                "h_HT_ready h_deg_ready h_step")
        with nc.Block() as block:
            e = setup
            WEIGHTS = 16 * 14

            @block.sync
            def _(sp):
                sp.wait_ge(e["h_w_zeroed"], 2)
                for k in range(2):
                    half = slice(k * C, (k + 1) * C)
                    sp.dma_start(W_diag[half, half], io["L0_gnn_W"]).then_inc(e["h_w_loaded"], 16)
                    sp.dma_start(Wind_diag[half, half], io["L0_gnn_W_ind"]).then_inc(e["h_w_loaded"], 16)
                    sp.dma_start(fcW[half, :], io["L0_gnn_fcW"]).then_inc(e["h_w_loaded"], 16)
                    for i, name in enumerate(("L0_gnn_a_node", "L0_gnn_a_gn", "L0_gnn_a_ge")):
                        sp.dma_start(vectors[half, i:i + 1], column(io[name])).then_inc(e["h_w_loaded"], 16)
                sp.dma_start(fcb[:, :], column(io["L0_gnn_fcb"])).then_inc(e["h_w_loaded"], 16)
                sp.dma_start(av[:, :], column(io["L0_gnn_av"])).then_inc(e["h_w_loaded"], 16)
                for k in range(2):
                    sp.dma_start(H_rows[:, :, k, :], io["L0_gnn_H"].rearrange("(t p) e -> p t e", p=P)).then_inc(e["h_adj_loaded"], 16)
                sp.dma_start(adjT[:, :, :], adjT_dram.rearrange("(t p) n -> p t n", p=P)).then_inc(e["h_adj_loaded"], 16)

            @block.gpsimd
            def _(pool):
                nc.gpsimd.memset(W_diag[:, :], 0.0).then_inc(e["h_w_zeroed"], 1)
                nc.gpsimd.memset(Wind_diag[:, :], 0.0).then_inc(e["h_w_zeroed"], 1)
                make_identity(pool, ident, e["h_zeroed"], e["h_ident_ready"], 0)
                nc.gpsimd.memset(minus_half[:, :], -0.5).then_inc(e["h_half_ready"], 1)
                nc.gpsimd.memset(agg_diag[:, :], 0.0).then_inc(e["h_half_ready"], 1)
                nc.gpsimd.memset(edge_table[:, :, :], 0.0).then_inc(e["h_half_ready"], 1)

            @block.tensor
            def _(pe):
                pe.wait_ge(e["h_ident_ready"], 1)
                pe.wait_ge(e["h_adj_loaded"], 48)
                for t in range(NT):
                    mm = nc.tensor.transpose(ps_m[:, t * P:(t + 1) * P], H_rows[:, t, :, :].rearrange("p k e -> p (k e)"), ident[:, :])
                mm.then_inc(e["h_HT_ready"], 1)
                pe.wait_ge(e["h_ones_ready"], 1)
                for m in range(2):
                    cols = slice(m * HN, (m + 1) * HN)
                    for t in range(NT):
                        mm = nc.tensor.matmul(ps_g[:, cols], ones[:, :], adjT[:, t, cols], start=(t == 0), stop=(t == NT - 1))
                mm.then_inc(e["h_deg_ready"], 1)

            @block.vector
            def _(dve):
                done = 0

                def link(ins):
                    nonlocal done
                    done += 1
                    ins.then_inc(e["h_step"], 1)
                    dve.wait_ge(e["h_step"], done)

                nc.vector.memset(ones[:, :], 1.0).then_inc(e["h_ones_ready"], 1)
                link(nc.vector.memset(av_pair[:, :, :, :], 0.0))
                link(nc.vector.memset(spread3[:, :, :], 0.0))
                dve.wait_ge(e["h_ones_ready"], 1)
                dve.wait_ge(e["h_w_loaded"], WEIGHTS)
                link(nc.vector.tensor_scalar(vectors[:, 1:3], vectors[:, 1:3], 0.5, None, ALU.mult))
                for i in range(3):
                    for k in range(2):
                        half = slice(k * C, (k + 1) * C)
                        nc.vector.tensor_scalar(spread3[half, i, half], ones[half, 0:C], vectors[half, i:i + 1], None, ALU.mult)
                link(nc.vector.tensor_scalar(av_half[:, :], av[:, :], 0.5, None, ALU.mult))
                nc.vector.tensor_scalar(av_all[:, :], ones[:, :], av[:, :], None, ALU.mult)
                for k in range(2):
                    half = slice(k * C, (k + 1) * C)
                    nc.vector.tensor_scalar(av_pair[:, 0, k, half], ones[:, 0:C], av_half[:, :], -1.0, ALU.mult, ALU.mult)
                    nc.vector.tensor_scalar(av_pair[:, 1, k, half], ones[:, 0:C], av_half[:, :], None, ALU.mult)
                dve.wait_ge(e["h_ident_ready"], 1)
                for k in range(2):
                    nc.vector.tensor_copy(pick[:, :, k * C:(k + 1) * C],
                                          ident[:, k * EDGES:(k + 1) * EDGES].unsqueeze(2).broadcast_to([P, EDGES, C]))
                dve.wait_ge(e["h_adj_loaded"], 48)
                link(nc.vector.tensor_scalar(mask_rows[:, :, :], H_rows[:, :, 0, :], 0.0, None, ALU.is_gt))
                link(nc.vector.tensor_scalar(fence_rows[:, :, :], mask_rows[:, :, :], -1.0, -NEG, ALU.add, ALU.mult))
                dve.wait_ge(e["h_HT_ready"], 1)
                link(nc.vector.tensor_scalar(maskT[:, :], ps_m[:, :], 0.0, None, ALU.is_gt))
                link(nc.vector.tensor_scalar(fenceT[:, :], maskT[:, :], -1.0, -NEG, ALU.add, ALU.mult))
                dve.wait_ge(e["h_deg_ready"], 1)
                link(nc.vector.tensor_scalar(inv_degree[:, :], ps_g[:, :], 1.0, None, ALU.max))
                link(nc.vector.reciprocal(inv_degree[:, :], inv_degree[:, :]))
        nc.all_engine_barrier(sems_to_clear=numbers(setup))

        e = events(bank, "h_x_loaded h_xT_ready h_xT_copied h_hT_ready h_hT_copied h_rows_ready h_rows_copied "
                            "h_irows_ready h_irows_copied h_s_ready h_s_copied h_a_masked h_a_exp h_a_inv h_aT_ready "
                            "h_aT_copied h_agg_ready h_agg_scaled h_aggT_ready h_aggT_copied h_gateh_ready h_gateh_copied "
                            "h_gatee_ready h_gatee_copied h_he_below h_he_exp h_he_ready h_z_ready h_z_tanh h_se_ready "
                            "h_se_copied h_c_shifted h_c_exp h_c_ready h_cT_ready h_c_high h_c_parts h_ind_ready h_ind_copied "
                            "h_half_made h_chain")
        loop = events(bank, "h_edge_copied h_diff_ready h_turn h_gate_ready h_shift_ready h_exp_ready h_relu_ready "
                               "h_f_ready h_w_ready h_spread_ready h_added")
        post = events(bank, "h_g_ready h_za_ready h_za_tanh h_zb_ready h_zb_tanh h_d_ready h_d_tanh h_o_ready "
                               "h_oT_ready h_norm h_var_ready h_rstd_ready h_y_done h_stored")
        x_pairs = x_in.rearrange("(q k) (t p) c -> q k p t c", k=2, p=P)
        y_pairs = x_out.rearrange("(q k) (t p) c -> q k p t c", k=2, p=P)

        with nc.Fori(0, PAIRS) as pair:
            with nc.Block() as block:

                @block.sync
                def _(sp):
                    for k in range(2):
                        sp.dma_start(x_rows[:, :, k, :], x_pairs[pair, k]).then_inc(e["h_x_loaded"], 16)
                    sp.wait_ge(e["h_x_loaded"], 32)

                @block.tensor
                def _(pe):
                    pe.wait_ge(e["h_x_loaded"], 32)
                    for t in range(NT):
                        mm = nc.tensor.transpose(ps_m[:, t * P:(t + 1) * P], x_rows[:, t, :, :].rearrange("p k c -> p (k c)"), ident[:, :])
                    mm.then_inc(e["h_xT_ready"], 1)
                    pe.wait_ge(e["h_xT_copied"], 1)
                    for m in range(2):
                        cols = slice(m * HN, (m + 1) * HN)
                        mm = nc.tensor.matmul(ps_c[0][:, cols], W_diag[:, :], xT[:, cols], start=True, stop=True)
                    mm.then_inc(e["h_hT_ready"], 1)
                    for t in range(NT):
                        mm = nc.tensor.matmul(ps_c[1][:, t * P:(t + 1) * P], xT[:, t * P:(t + 1) * P], W_diag[:, :], start=True, stop=True)
                    mm.then_inc(e["h_rows_ready"], 1)
                    for t in range(NT):
                        mm = nc.tensor.matmul(ps_g[:, t * P:(t + 1) * P], xT[:, t * P:(t + 1) * P], Wind_diag[:, :], start=True, stop=True)
                    mm.then_inc(e["h_irows_ready"], 1)
                    pe.wait_ge(e["h_hT_copied"], 1)
                    for m in range(2):
                        cols = slice(m * HN, (m + 1) * HN)
                        mm = nc.tensor.matmul(ps_m[:, cols], spread3[:, 0, :], hT[:, cols], start=True, stop=True)
                    mm.then_inc(e["h_s_ready"], 1)
                    for m in range(2):
                        cols = slice(m * HN, (m + 1) * HN)
                        mm = nc.tensor.matmul(ps_c[0][:, cols], spread3[:, 1, :], hT[:, cols], start=True, stop=True)
                    mm.then_inc(e["h_gateh_ready"], 1)
                    pe.wait_ge(e["h_irows_copied"], 1)
                    for m in range(2):
                        cols = slice(m * HN, (m + 1) * HN)
                        for t in range(NT):
                            mm = nc.tensor.matmul(ps_g[:, cols], ind_rows[:, t, :], adjT[:, t, cols], start=(t == 0), stop=(t == NT - 1))
                    mm.then_inc(e["h_ind_ready"], 1)
                    pe.wait_ge(e["h_a_exp"], 1)
                    pe.wait_ge(e["h_rows_copied"], 1)
                    for t in range(NT):
                        mm = nc.tensor.transpose(ps_c[1][:, t * P:(t + 1) * P], logits[:, t * P:(t + 1) * P], ident[:, :])
                    mm.then_inc(e["h_aT_ready"], 1)
                    pe.wait_ge(e["h_aT_copied"], 1)
                    for t in range(NT):
                        mm = nc.tensor.matmul(ps_m[:, 0:P], alphaT[:, t, :], h_rows[:, t, :], start=(t == 0), stop=(t == NT - 1))
                    mm.then_inc(e["h_agg_ready"], 1)
                    pe.wait_ge(e["h_agg_scaled"], 2)
                    nc.tensor.transpose(ps_c[1][:, 0:P], agg_diag[:, :], ident[:, :]).then_inc(e["h_aggT_ready"], 1)
                    pe.wait_ge(e["h_aggT_copied"], 2)
                    nc.tensor.matmul(ps_m[:, 0:EDGES], spread3[:, 2, :], aggT[:, :], start=True, stop=True).then_inc(e["h_gatee_ready"], 1)
                    pe.wait_ge(e["h_he_ready"], 1)
                    for k in range(2):
                        half = slice(k * C, (k + 1) * C)
                        mm = nc.tensor.matmul(ps_c[1][:, k * HN:k * HN + EDGES], fcW[half, :], he[half, :], start=True, stop=True)
                    mm.then_inc(e["h_z_ready"], 1)
                    pe.wait_ge(e["h_z_tanh"], 1)
                    pe.wait_ge(e["h_gatee_copied"], 1)
                    nc.tensor.matmul(ps_m[:, 0:P], av_all[:, :], z_edge[:, :], start=True, stop=True).then_inc(e["h_se_ready"], 1)
                    pe.wait_ge(e["h_c_ready"], 1)
                    for t in range(NT):
                        mm = nc.tensor.transpose(ps_c[1][:, t * P:(t + 1) * P], coef_rows[:, t, :, :].rearrange("p k e -> p (k e)"), ident[:, :])
                    mm.then_inc(e["h_cT_ready"], 1)

                @block.scalar
                def _(act):
                    act.wait_ge(e["h_xT_ready"], 1)
                    nc.scalar.activation(xT[:, :], ps_m[:, :], ACT.Copy).then_inc(e["h_xT_copied"], 1)
                    act.wait_ge(e["h_rows_ready"], 1)
                    nc.scalar.activation(h_rows[:, :, :], ps_c[1][:, :].rearrange("p (t c) -> p t c", c=P), ACT.Copy).then_inc(e["h_rows_copied"], 1)
                    act.wait_ge(e["h_irows_ready"], 1)
                    nc.scalar.activation(ind_rows[:, :, :], ps_g[:, :].rearrange("p (t c) -> p t c", c=P), ACT.Copy).then_inc(e["h_irows_copied"], 1)
                    act.wait_ge(e["h_s_ready"], 1)
                    nc.scalar.activation(logits[:, :], ps_m[:, :], ACT.Copy).then_inc(e["h_s_copied"], 1)
                    act.wait_ge(e["h_gateh_ready"], 1)
                    nc.scalar.activation(gate_h[:, :], ps_c[0][:, :], ACT.Copy).then_inc(e["h_gateh_copied"], 1)
                    act.wait_ge(e["h_a_masked"], 1)
                    nc.scalar.activation(logits[:, :], logits[:, :], ACT.Exp, bias=neg_max[:, :], accum_out=row_sum[:, :]).then_inc(e["h_a_exp"], 1)
                    act.wait_ge(e["h_aT_ready"], 1)
                    nc.scalar.activation(alphaT[:, :, :], ps_c[1][:, :].rearrange("p (t c) -> p t c", c=P), ACT.Copy).then_inc(e["h_aT_copied"], 1)
                    act.wait_ge(e["h_he_below"], 1)
                    nc.scalar.activation(below[:, :], below[:, :], ACT.Exp).then_inc(e["h_he_exp"], 1)
                    act.wait_ge(e["h_gatee_ready"], 1)
                    nc.scalar.activation(edge_table[:, :, 0], ps_m[:, 0:EDGES], ACT.Copy).then_inc(e["h_gatee_copied"], 1)
                    act.wait_ge(e["h_z_ready"], 1)
                    nc.scalar.activation(z_edge[:, :].rearrange("p (k e) -> p k e", k=2), ps_c[1][:, :].rearrange("p (k e) -> p k e", k=2)[:, :, 0:EDGES], ACT.Tanh, bias=fcb[:, :]).then_inc(e["h_z_tanh"], 1)
                    act.wait_ge(e["h_se_ready"], 1)
                    nc.scalar.activation(se_all[:, :, :], ps_m[:, 0:P].rearrange("p (k e) -> p k e", k=2), ACT.Copy).then_inc(e["h_se_copied"], 1)
                    act.wait_ge(e["h_c_shifted"], 1)
                    nc.scalar.activation(coef_rows[:, :, :, :], coef_rows[:, :, :, :], ACT.Exp).then_inc(e["h_c_exp"], 1)
                    act.wait_ge(e["h_cT_ready"], 1)
                    nc.scalar.activation(coef[:, 0, :], ps_c[1][:, :], ACT.Copy).then_inc(e["h_c_high"], 1)

                @block.vector
                def _(dve):
                    done = 0

                    def link(ins):
                        nonlocal done
                        done += 1
                        ins.then_inc(e["h_chain"], 1)
                        dve.wait_ge(e["h_chain"], done)

                    dve.wait_ge(e["h_hT_ready"], 1)
                    nc.vector.tensor_copy(hT[:, :], ps_c[0][:, :]).then_inc(e["h_hT_copied"], 1)
                    dve.wait_ge(e["h_s_copied"], 1)
                    link(nc.vector.scalar_tensor_tensor(logits[:, :], logits[:, :], 0.2, logits[:, :], ALU.mult, ALU.max))
                    link(nc.vector.tensor_tensor(logits[:, :], logits[:, :], maskT[:, :], ALU.mult))
                    link(nc.vector.tensor_tensor(logits[:, :], logits[:, :], fenceT[:, :], ALU.add))
                    nc.vector.tensor_reduce(neg_max[:, :], logits[:, :], AX.X, ALU.max, negate=True).then_inc(e["h_a_masked"], 1)
                    dve.wait_ge(e["h_hT_copied"], 1)
                    nc.vector.tensor_scalar(half_hT[:, :], hT[:, :], 0.5, None, ALU.mult).then_inc(e["h_half_made"], 1)
                    dve.wait_ge(e["h_a_exp"], 1)
                    nc.vector.reciprocal(row_inv[:, :], row_sum[:, :]).then_inc(e["h_a_inv"], 1)
                    dve.wait_ge(e["h_ind_ready"], 1)
                    nc.vector.tensor_tensor(indT[:, :], ps_g[:, :], inv_degree[:, :], ALU.mult).then_inc(e["h_ind_copied"], 1)
                    dve.wait_ge(e["h_agg_ready"], 1)
                    dve.wait_ge(e["h_a_inv"], 1)
                    for k in range(2):
                        half = slice(k * C, (k + 1) * C)
                        nc.vector.tensor_scalar(agg_diag[half, half], ps_m[half, half], row_inv[half, :], None, ALU.mult).then_inc(e["h_agg_scaled"], 1)
                    dve.wait_ge(e["h_aggT_ready"], 1)
                    for k in range(2):
                        half = slice(k * C, (k + 1) * C)
                        nc.vector.tensor_copy(aggT[half, :], ps_c[1][half, half]).then_inc(e["h_aggT_copied"], 1)
                    dve.wait_ge(e["h_aggT_copied"], 2)
                    nc.vector.tensor_scalar(below[:, :], aggT[:, :], 0.0, None, ALU.min).then_inc(e["h_he_below"], 1)
                    link(nc.vector.tensor_scalar(above[:, :], aggT[:, :], 0.0, None, ALU.max))
                    link(nc.vector.tensor_copy(edge_table[:, :, 1], aggT[:, :]))
                    link(nc.vector.tensor_scalar(edge_table[:, :, 2], aggT[:, :], 0.5, None, ALU.mult))
                    dve.wait_ge(e["h_he_exp"], 1)
                    nc.vector.scalar_tensor_tensor(he[:, :], below[:, :], -1.0, above[:, :], ALU.add, ALU.add).then_inc(e["h_he_ready"], 1)
                    dve.wait_ge(e["h_se_copied"], 1)
                    rows = coef_rows[:, :, :, :]
                    for k in range(2):
                        link(nc.vector.tensor_tensor(coef_rows[:, :, k, :], mask_rows[:, :, :],
                                                     se_all[:, k, :].unsqueeze(1).broadcast_to([P, NT, EDGES]), ALU.mult))
                        link(nc.vector.tensor_tensor(coef_rows[:, :, k, :], coef_rows[:, :, k, :], fence_rows[:, :, :], ALU.add))
                    flat = rows.rearrange("p t k e -> p (t k) e")
                    link(nc.vector.tensor_reduce(max2[:, :], flat, AX.X, ALU.max))
                    nc.vector.tensor_tensor(flat, flat, max2[:, :].unsqueeze(2).broadcast_to([P, 2 * NT, EDGES]), ALU.subtract).then_inc(e["h_c_shifted"], 1)
                    dve.wait_ge(e["h_c_exp"], 1)
                    link(nc.vector.tensor_reduce(sum2[:, :], flat, AX.X, ALU.add))
                    link(nc.vector.reciprocal(inv2[:, :], sum2[:, :]))
                    nc.vector.tensor_tensor(flat, flat, inv2[:, :].unsqueeze(2).broadcast_to([P, 2 * NT, EDGES]), ALU.mult).then_inc(e["h_c_ready"], 1)
                    dve.wait_ge(e["h_c_high"], 1)
                    link(nc.vector.tensor_tensor(coef_rest[:, :], ps_c[1][:, :], coef[:, 0, :], ALU.subtract))
                    link(nc.vector.tensor_copy(coef[:, 1, :], coef_rest[:, :]))
                    link(nc.vector.tensor_tensor(coef[:, 2, :], coef_rest[:, :], coef[:, 1, :], ALU.subtract))
            nc.all_engine_barrier(sems_to_clear=numbers(e))

            with nc.Block() as block:
                f = loop

                def rounds(eng, step):
                    for j in range(UNROLL):
                        step(j, j)
                    with eng.Fori(1, EDGES // UNROLL - 1) as turn:
                        for j in range(UNROLL):
                            step(UNROLL * turn + j, j)
                    for j in range(UNROLL):
                        step(EDGES - UNROLL + j, j)

                def past(edge, least):
                    return not isinstance(edge, int) or edge >= least

                @block.gpsimd
                def _(pool):
                    nc.gpsimd.tensor_tensor(pool_waiter[:, :], ident[:, 0:1], ident[:, 0:1], ALU.add).then_inc(f["h_turn"], 1)

                    def step(edge, j):
                        if past(edge, UNROLL):
                            pool.wait_ge(f["h_turn"], edge - UNROLL + 1)
                            pool.wait_ge(f["h_relu_ready"], edge - UNROLL + 1)
                            nc.gpsimd.tensor_tensor(pool_waiter[:, :], ident[:, 0:1], ident[:, 0:1], ALU.add).then_inc(f["h_turn"], 1)
                        nc.gpsimd.tensor_copy(edge_now[j][:, :], edge_table[:, edge, :]).then_inc(f["h_edge_copied"], 1)
                        pool.wait_ge(f["h_edge_copied"], edge + 1)
                        if past(edge, 2):
                            pool.wait_ge(f["h_shift_ready"], edge - 1)
                        nc.gpsimd.tensor_tensor(diff[j % 2][:, :], half_hT[:, :], edge_now[j][:, 2:3].broadcast_to([P, N]),
                                                ALU.subtract).then_inc(f["h_diff_ready"], 1)
                    rounds(pool, step)

                @block.scalar
                def _(act):
                    def make_gate(edge, j):
                        act.wait_ge(f["h_edge_copied"], edge + 1)
                        if past(edge, 2):
                            act.wait_ge(f["h_shift_ready"], edge - 1)
                        nc.scalar.activation(gate[j % 2][:, :], gate_h[:, :], ACT.Tanh, bias=edge_now[j % UNROLL][:, 0:1]).then_inc(f["h_gate_ready"], 1)

                    def functions(edge, j):
                        act.wait_ge(f["h_shift_ready"], edge + 1)
                        if past(edge, 2):
                            act.wait_ge(f["h_f_ready"], edge - 1)
                        agg = edge_now[j % UNROLL][:, 1:2]
                        nc.scalar.activation(expv[j % 2][:, :], shifted[j % 2][:, :], ACT.Exp, bias=agg).then_inc(f["h_exp_ready"], 1)
                        nc.scalar.activation(reluv[j % 2][:, :], shifted[j % 2][:, :], ACT.Relu, bias=agg).then_inc(f["h_relu_ready"], 1)

                    def step(edge, j):
                        if not isinstance(edge, int) or edge + 2 < EDGES:
                            make_gate(edge + 2, j + 2)
                        if not isinstance(edge, int) or edge + 1 < EDGES:
                            functions(edge + 1, j + 1)

                    make_gate(0, 0)
                    make_gate(1, 1)
                    functions(0, 0)
                    rounds(act, step)

                @block.vector
                def _(dve):
                    def shift(edge, j):
                        dve.wait_ge(f["h_diff_ready"], edge + 1)
                        dve.wait_ge(f["h_gate_ready"], edge + 1)
                        if past(edge, 2):
                            dve.wait_ge(f["h_relu_ready"], edge - 1)
                        nc.vector.scalar_tensor_tensor(shifted[j % 2][:, :], gate[j % 2][:, :], 1.0, diff[j % 2][:, :],
                                                       ALU.add, ALU.mult).then_inc(f["h_shift_ready"], 1)

                    def step(edge, j):
                        if not isinstance(edge, int) or edge + 1 < EDGES:
                            shift(edge + 1, j + 1)
                        dve.wait_ge(f["h_relu_ready"], edge + 1)
                        nc.vector.scalar_tensor_tensor(reluv[j % 2][:, :], expv[j % 2][:, :], 1.0, reluv[j % 2][:, :],
                                                       ALU.min, ALU.add).then_inc(f["h_w_ready"], 1)
                        dve.wait_ge(f["h_w_ready"], edge + 1)
                        dve.wait_ge(f["h_spread_ready"], edge + 1)
                        if past(edge, 2):
                            dve.wait_ge(f["h_added"], edge - 1)
                        nc.vector.tensor_tensor(weighted[j % 2][:, :], reluv[j % 2][:, :], ps_c[j % 2][:, :], ALU.mult).then_inc(f["h_f_ready"], 1)

                    shift(0, 0)
                    rounds(dve, step)

                @block.tensor
                def _(pe):
                    def spread(edge, j):
                        for m in range(2):
                            cols = slice(m * HN, (m + 1) * HN)
                            for part in range(3):
                                mm = nc.tensor.matmul(ps_c[j % 2][:, cols], pick[:, edge, :], coef[:, part, cols],
                                                      start=(part == 0), stop=(part == 2))
                        mm.then_inc(f["h_spread_ready"], 1)

                    def step(edge, j):
                        pe.wait_ge(f["h_f_ready"], edge + 1)
                        first = isinstance(edge, int) and edge == 0
                        last = isinstance(edge, int) and edge == EDGES - 1
                        for m in range(2):
                            cols = slice(m * HN, (m + 1) * HN)
                            mm = nc.tensor.matmul(ps_g[:, cols], ident[:, :], weighted[j % 2][:, cols], start=first, stop=last)
                        mm.then_inc(f["h_added"], 1)
                        if not isinstance(edge, int) or edge + 2 < EDGES:
                            spread(edge + 2, j + 2)

                    spread(0, 0)
                    spread(1, 1)
                    rounds(pe, step)
            nc.all_engine_barrier(sems_to_clear=numbers(loop))

            with nc.Block() as block:
                q = post
                gT, outT, d_tanh = diff[0], diff[1], gate[0]
                zt = [[shifted[0], shifted[1]], [expv[0], expv[1]]]
                y = weighted[0][:, :].rearrange("p (t c) -> p t c", c=C)
                sq = weighted[1][:, :].rearrange("p (t c) -> p t c", c=C)

                @block.vector
                def _(dve):
                    nc.vector.tensor_scalar(gT[:, :], ps_g[:, :], -1.0, None, ALU.add).then_inc(q["h_g_ready"], 1)
                    dve.wait_ge(q["h_g_ready"], 1)
                    nc.vector.tensor_tensor(outT[:, :], gT[:, :], indT[:, :], ALU.subtract).then_inc(q["h_g_ready"], 1)
                    done = 0

                    def link(ins):
                        nonlocal done
                        done += 1
                        ins.then_inc(q["h_norm"], 1)
                        dve.wait_ge(q["h_norm"], done)

                    dve.wait_ge(q["h_d_tanh"], 1)
                    dve.wait_ge(q["h_g_ready"], 2)
                    link(nc.vector.scalar_tensor_tensor(outT[:, :], d_tanh[:, :], 1.0, outT[:, :], ALU.add, ALU.mult))
                    nc.vector.scalar_tensor_tensor(outT[:, :], outT[:, :], 0.5, indT[:, :], ALU.mult, ALU.add).then_inc(q["h_o_ready"], 1)
                    dve.wait_ge(q["h_oT_ready"], 1)
                    link(nc.vector.tensor_tensor(y, ps_c[0][:, :].rearrange("p (t c) -> p t c", c=C),
                                                 x_rows[:, :, :, :].rearrange("p t k c -> p (t k) c"), ALU.add))
                    layer_norm_rows(nc, dve, link, y, sq, mean[:, :], var[:, :], rstd[:, :], q["h_var_ready"], q["h_rstd_ready"], q["h_y_done"])

                @block.gpsimd
                def _(pool):
                    pool.wait_ge(q["h_var_ready"], 1)
                    nc.gpsimd.tensor_tensor(rstd[:, :], var[:, :], minus_half[:, :], ALU.pow).then_inc(q["h_rstd_ready"], 1)

                @block.tensor
                def _(pe):
                    for k in range(2):
                        half = slice(k * C, (k + 1) * C)
                        if k == 1:
                            pe.wait_ge(q["h_za_tanh"], 1)
                        for m in range(2):
                            cols = slice(m * HN, (m + 1) * HN)
                            mm = nc.tensor.matmul(ps_c[0][:, cols], fcW[half, :], indT[half, cols], start=True, stop=True)
                        mm.then_inc(q["h_za_ready"], 1)
                        if k == 0:
                            pe.wait_ge(q["h_g_ready"], 1)
                        else:
                            pe.wait_ge(q["h_zb_tanh"], 1)
                        for m in range(2):
                            cols = slice(m * HN, (m + 1) * HN)
                            mm = nc.tensor.matmul(ps_c[1][:, cols], fcW[half, :], gT[half, cols], start=True, stop=True)
                        mm.then_inc(q["h_zb_ready"], 1)
                    pe.wait_ge(q["h_za_tanh"], 2)
                    pe.wait_ge(q["h_zb_tanh"], 2)
                    for m in range(2):
                        cols = slice(m * HN, (m + 1) * HN)
                        for i in range(4):
                            kind, k = i // 2, i % 2
                            mm = nc.tensor.matmul(ps_m[:, cols], av_pair[:, kind, k, :], zt[kind][k][:, cols], start=(i == 0), stop=(i == 3))
                    mm.then_inc(q["h_d_ready"], 1)
                    pe.wait_ge(q["h_o_ready"], 1)
                    for t in range(NT):
                        mm = nc.tensor.transpose(ps_c[0][:, t * P:(t + 1) * P], outT[:, t * P:(t + 1) * P], ident[:, :])
                    mm.then_inc(q["h_oT_ready"], 1)

                @block.scalar
                def _(act):
                    for k in range(2):
                        act.wait_ge(q["h_za_ready"], k + 1)
                        nc.scalar.activation(zt[0][k][:, :], ps_c[0][:, :], ACT.Tanh, bias=fcb[:, :]).then_inc(q["h_za_tanh"], 1)
                        act.wait_ge(q["h_zb_ready"], k + 1)
                        nc.scalar.activation(zt[1][k][:, :], ps_c[1][:, :], ACT.Tanh, bias=fcb[:, :]).then_inc(q["h_zb_tanh"], 1)
                    act.wait_ge(q["h_d_ready"], 1)
                    nc.scalar.activation(d_tanh[:, :], ps_m[:, :], ACT.Tanh).then_inc(q["h_d_tanh"], 1)

                @block.sync
                def _(sp):
                    sp.wait_ge(q["h_y_done"], 1)
                    for k in range(2):
                        sp.dma_start(y_pairs[pair, k], weighted[0][:, :].rearrange("p (t k c) -> p t k c", k=2, c=C)[:, :, k, :]).then_inc(q["h_stored"], 16)
                    sp.wait_ge(q["h_stored"], 32)
            nc.all_engine_barrier(sems_to_clear=numbers(post))


def multi_head_gat(nc, bank, io, x_in, x_out):
    ctx = ExitStack()
    with ctx:
        def sb(name, shape, dt=F32):
            return ctx.enter_context(nc.sbuf_tensor(name, shape, dt))

        def pb(name, shape):
            return ctx.enter_context(nc.psum_tensor(name, shape, F32))

        ident = sb("g_ident", [P, P])
        ident_bf = sb("g_ident_bf", [P, P], BF16)
        ident2 = sb("g_ident2", [P, C])
        graph = sb("g_graph", [P, NT, N])
        fence = sb("g_fence", [P, NT, N], BF16)
        w_head = sb("g_w_head", [P, HEADS, HC])
        A_table = sb("g_A_table", [P, HEADS, 2, P], F32R)
        W_table = sb("g_W_table", [P, HEADS, 2 * P + 1])
        b_out_row = sb("g_b_out_row", [P, C])
        A_cur = [sb(f"g_A_cur{k}", [P, 2, P], F32R) for k in range(2)]
        W_cur = [sb(f"g_W_cur{k}", [P, 2 * P + 1]) for k in range(2)]
        x_rows = sb("g_x_rows", [P, NT, 2 * C])
        moving_hi = sb("g_moving_hi", [P, N], F32R)
        moving_lo = sb("g_moving_lo", [P, N], F32R)
        moving_hl = sb("g_moving_hl", [P, N], F32R)
        value_hl = sb("g_value_hl", [P, NT, P], F32R)
        query = [sb(f"g_query{k}", [P, N], F32R) for k in range(2)]
        scores = [sb(f"g_scores{k}", [P, N]) for k in range(2)]
        row_max = [sb(f"g_row_max{k}", [P, 1]) for k in range(2)]
        waiter = sb("g_waiter", [P, 1])
        pool_waiter = sb("g_pool_waiter", [P, 1])
        neg_max = [sb(f"g_neg_max{k}", [P, 1]) for k in range(2)]
        probs = [sb(f"g_probs{k}", [P, N]) for k in range(2)]
        row_sum = sb("g_row_sum", [P, NT])
        row_inv = sb("g_row_inv", [P, NT])
        pt_hi = [sb(f"g_pt_hi{k}", [P, NT, HN], F32R) for k in range(2)]
        pt_lo = [sb(f"g_pt_lo{k}", [P, NT, HN], F32R) for k in range(2)]
        mixed = sb("g_mixed", [P, HN])
        mixed_n = sb("g_mixed_n", [P, HN])
        cat_b = sb("g_cat_b", [P, HN])
        cat = sb("g_cat", [P, HN])
        hidden = sb("g_hidden", [P, N])
        y = sb("g_y", [P, NT, C])
        sq = sb("g_sq", [P, NT, C])
        mean = sb("g_mean", [P, NT])
        var = sb("g_var", [P, NT])
        rstd = sb("g_rstd", [P, NT])
        minus_half = sb("g_minus_half", [P, NT])

        ps_s = [pb(f"g_ps_s{k}", [P, N]) for k in range(2)]
        ps_t = [pb(f"g_ps_t{k}", [P, HN]) for k in range(2)]
        ps_u = pb("g_ps_u", [P, HN])
        ps_x = pb("g_ps_x", [P, HN])

        setup = events(bank, "g_loaded g_zeroed g_ident_ready g_ident2_ready g_graph_zero "
                                "g_fence_ready g_graph_ready g_wT_ready g_wT_copied g_A_ready "
                                "g_A_high g_A_rest g_W_packed g_half_ready")
        with nc.Block() as block:
            e = setup

            @block.sync
            def _(sp):
                sp.dma_start(graph[:, :, :], io["adj"].rearrange("(t p) m -> p t m", p=P)).then_inc(e["g_loaded"], 16)
                for k in range(2):
                    half = slice(k * C, (k + 1) * C)
                    sp.dma_start(w_head[half, :, :], io["L1_gnn_Wh"].rearrange("h c d -> c h d")).then_inc(e["g_loaded"], 16)
                    sp.dma_start(W_table[:, :, P + k * C:P + (k + 1) * C],
                                 io["L1_gnn_W_out"].rearrange("(h d) c -> d h c", d=HC)).then_inc(e["g_loaded"], 16)
                sp.dma_start(W_table[:, :, 2 * P:2 * P + 1],
                             io["L1_gnn_bh"].rearrange("h (d o) -> d h o", o=1),
                             allow_slow_non_contiguous=True).then_inc(e["g_loaded"], 16)
                sp.dma_start(b_out_row[:, :], io["L1_gnn_b_out"].partition_broadcast(P)).then_inc(e["g_loaded"], 16)

            @block.gpsimd
            def _(pool):
                make_identity(pool, ident, e["g_zeroed"], e["g_ident_ready"], 0)
                make_identity(pool, ident_bf, e["g_zeroed"], e["g_ident_ready"], 1)
                nc.gpsimd.memset(minus_half[:, :], -0.5).then_inc(e["g_half_ready"], 1)

            @block.vector
            def _(dve):
                dve.wait_ge(e["g_ident_ready"], 2)
                nc.vector.tensor_tensor(ident2[:, :], ident[:, 0:C], ident[:, C:2 * C], ALU.add).then_inc(e["g_ident2_ready"], 1)
                dve.wait_ge(e["g_loaded"], 16 * 7)
                for t in range(NT):
                    nc.vector.tensor_scalar(scores[t % 2][:, :], graph[:, t, :], 0.0, None, ALU.is_equal).then_inc(e["g_graph_zero"], 1)
                    dve.wait_ge(e["g_graph_zero"], t + 1)
                    nc.vector.tensor_scalar(fence[:, t, :], scores[t % 2][:, :], MASKED, None, ALU.mult).then_inc(e["g_fence_ready"], 1)
                    nc.vector.tensor_tensor(graph[:, t, :], graph[:, t, :], scores[t % 2][:, :], ALU.add).then_inc(e["g_graph_ready"], 1)
                    dve.wait_ge(e["g_graph_ready"], t + 1)
                nc.vector.tensor_copy(W_table[:, :, 0:P], w_head[:, :, :]).then_inc(e["g_W_packed"], 1)
                dve.wait_ge(e["g_wT_ready"], 1)
                nc.vector.tensor_copy(scores[0][:, :], ps_s[0][:, :]).then_inc(e["g_wT_copied"], 1)
                dve.wait_ge(e["g_A_ready"], 1)
                for h in range(HEADS):
                    nc.vector.tensor_copy(A_table[:, h, 0, :], ps_s[1][:, h * P:(h + 1) * P]).then_inc(e["g_A_high"], 1)
                    dve.wait_ge(e["g_A_high"], h + 1)
                    nc.vector.tensor_tensor(A_table[:, h, 1, :], ps_s[1][:, h * P:(h + 1) * P],
                                            A_table[:, h, 0, :].bitcast(F32), ALU.subtract).then_inc(e["g_A_rest"], 1)

            @block.tensor
            def _(pe):
                pe.wait_ge(e["g_loaded"], 16 * 7)
                pe.wait_ge(e["g_ident_ready"], 2)
                for h in range(HEADS):
                    mm = nc.tensor.transpose(ps_s[0][:, h * P:(h + 1) * P], w_head[:, h, :], ident[:, :])
                mm.then_inc(e["g_wT_ready"], 1)
                pe.wait_ge(e["g_wT_copied"], 1)
                for h in range(HEADS):
                    wT = scores[0][:, h * P:(h + 1) * P]
                    mm = nc.tensor.matmul(ps_s[1][:, h * P:(h + 1) * P], wT, wT, start=True, stop=True)
                mm.then_inc(e["g_A_ready"], 1)
        nc.all_engine_barrier(sems_to_clear=numbers(setup))

        e = events(bank, "g_x_loaded g_xT_ready g_x_high g_x_rest g_x_stacked g_v_high g_v_rest "
                            "g_s_ready g_m_ready g_t_ready g_p_ready g_pt_ready g_hi_ready g_lo_ready g_u_ready "
                            "g_ut_ready g_ri_ready g_rb_ready g_un_ready g_cat_ready g_vb_ready g_v_ready g_hp_ready "
                            "g_hacc_ready g_y_ready g_yr_ready g_y2_ready g_wa_ready g_ww_ready g_turn "
                            "g_h_split g_hT_ready g_out_ready g_norm g_var_ready g_rstd_ready g_y_done g_stored")
        LAST = HEADS
        xin = x_in.rearrange("b (t p) c -> b p t c", p=P)
        xout = x_out.rearrange("b (t p) c -> b p t c", p=P)

        with nc.Fori(0, BATCH) as b:
            with nc.Block() as block:

                @block.sync
                def _(sp):
                    for k in range(2):
                        sp.dma_start(x_rows[:, :, k * C:(k + 1) * C], xin[b]).then_inc(e["g_x_loaded"], 16)
                    sp.wait_ge(e["g_y_done"], 1)
                    sp.dma_start(xout[b], y[:, :, :]).then_inc(e["g_stored"], 16)
                    sp.wait_ge(e["g_stored"], 16)

                @block.gpsimd
                def _(pool):
                    def weights(h, k):
                        later = not isinstance(h, int) or h >= 2
                        if later:
                            pool.wait_ge(e["g_turn"], 2 * h - 3)
                            pool.wait_ge(e["g_y_ready"], 2 * h - 2)
                            nc.gpsimd.tensor_tensor(pool_waiter[:, :], ident[:, 0:1], ident[:, 0:1], ALU.add).then_inc(e["g_turn"], 1)
                        nc.gpsimd.tensor_copy(A_cur[k][:, :, :], A_table[:, h, :, :]).then_inc(e["g_wa_ready"], 1)
                        if later:
                            pool.wait_ge(e["g_turn"], 2 * h - 2)
                            pool.wait_ge(e["g_hp_ready"], 2 * h - 2)
                            nc.gpsimd.tensor_tensor(pool_waiter[:, :], ident[:, 0:1], ident[:, 0:1], ALU.add).then_inc(e["g_turn"], 1)
                        nc.gpsimd.tensor_copy(W_cur[k][:, :], W_table[:, h, :]).then_inc(e["g_ww_ready"], 1)

                    nc.gpsimd.tensor_tensor(pool_waiter[:, :], ident[:, 0:1], ident[:, 0:1], ALU.add).then_inc(e["g_turn"], 1)
                    weights(0, 0)
                    weights(1, 1)
                    with pool.Fori(1, HEADS // 2) as pair:
                        weights(2 * pair, 0)
                        weights(2 * pair + 1, 1)
                    pool.wait_ge(e["g_var_ready"], 1)
                    nc.gpsimd.tensor_tensor(rstd[:, :], var[:, :], minus_half[:, :], ALU.pow).then_inc(e["g_rstd_ready"], 1)

                @block.tensor
                def _(pe):
                    def score(h, i, k):
                        n = 8 * h + i
                        if i == 0 and not (isinstance(h, int) and h == LAST):
                            pe.wait_ge(e["g_y2_ready"], 2 * h + 2)
                        if not isinstance(n, int) or n >= 2:
                            pe.wait_ge(e["g_t_ready"], n - 1)
                        for m in range(2):
                            cols = slice(m * HN, (m + 1) * HN)
                            rows = slice(i * P, (i + 1) * P)
                            nc.tensor.matmul(ps_s[i % 2][:, cols], ident_bf[:, :], fence[:, i, cols], start=True, stop=False)
                            nc.tensor.matmul(ps_s[i % 2][:, cols], query[k][:, rows], moving_hi[:, cols], start=False, stop=False)
                            mm = nc.tensor.matmul(ps_s[i % 2][:, cols], query[k][:, rows], moving_lo[:, cols], start=False, stop=True)
                        mm.then_inc(e["g_s_ready"], 1)

                    def transpose(h, i):
                        n = 8 * h + i
                        pe.wait_ge(e["g_p_ready"], n + 1)
                        for a in range(2):
                            if not isinstance(n, int) or n >= 1:
                                pe.wait_ge(e["g_lo_ready"], 2 * n + a - 1)
                            for j in range(4):
                                m = 4 * a + j
                                mm = nc.tensor.transpose(ps_t[a][:, j * P:(j + 1) * P],
                                                         probs[i % 2][:, m * P:(m + 1) * P], ident[:, :])
                            mm.then_inc(e["g_pt_ready"], 1)

                    def mix(h, half, chunk):
                        if chunk == 0:
                            pe.wait_ge(e["g_lo_ready"], 16 * h + 8 * half + 8)
                            if not (isinstance(h, int) and 2 * h + half == 0):
                                pe.wait_ge(e["g_ut_ready"], 2 * h + half)
                        for j in (2 * chunk, 2 * chunk + 1):
                            nc.tensor.matmul(ps_u[:, :], value_hl[:, j, :], pt_hi[half][:, j, :], start=(j == 0), stop=False)
                            mm = nc.tensor.matmul(ps_u[:, :], value_hl[:, j, :], pt_lo[half][:, j, :], start=False, stop=(j == NT - 1))
                        if chunk == 3:
                            mm.then_inc(e["g_u_ready"], 1)

                    def queries(h, half, k):
                        pe.wait_ge(e["g_wa_ready"], h + 1)
                        cols = slice(half * HN, (half + 1) * HN)
                        nc.tensor.matmul(ps_x[:, :], A_cur[k][:, 0, :], moving_hl[:, cols], start=True, stop=False)
                        nc.tensor.matmul(ps_x[:, :], A_cur[k][:, 1, :], moving_hl[:, cols], start=False, stop=True).then_inc(e["g_y_ready"], 1)

                    def spread_inverse(h, half):
                        pe.wait_ge(e["g_ri_ready"], 2 * h + half + 1)
                        for j in range(4):
                            i = 4 * half + j
                            mm = nc.tensor.matmul(ps_x[:, j * P:(j + 1) * P], row_inv[:, i:i + 1].broadcast_to([P, P]), ident[:, :],
                                                  start=True, stop=True)
                        mm.then_inc(e["g_rb_ready"], 1)

                    def project(h, half, k):
                        pe.wait_ge(e["g_ww_ready"], h + 1)
                        pe.wait_ge(e["g_un_ready"], 2 * h + half + 1)
                        nc.tensor.matmul(ps_x[:, :], W_cur[k][:, 0:P], mixed_n[:, :], start=True, stop=True).then_inc(e["g_cat_ready"], 1)

                    def project_out(h, half, k):
                        pe.wait_ge(e["g_v_ready"], 2 * h + half + 1)
                        nc.tensor.matmul(ps_x[:, :], W_cur[k][:, P:2 * P], cat[:, :], start=True, stop=True).then_inc(e["g_hp_ready"], 1)

                    def head(h, k, first=False, last=False):
                        for i in range(NT):
                            transpose(h, i)
                            if i + 2 < NT:
                                score(h, i + 2, k)
                            elif not last:
                                score(h + 1, i + 2 - NT, 1 - k)
                            if i >= 4:
                                mix(h, 0, i - 4)
                            elif not first:
                                mix(h - 1, 1, i)
                            if i == 0 and not first:
                                pe.wait_ge(e["g_hacc_ready"], 2 * h)
                                pe.wait_ge(e["g_y2_ready"], 2 * h + 2)
                                spread_inverse(h - 1, 0)
                            if i == 1 and not first:
                                project(h - 1, 0, 1 - k)
                            if i == 2 and not first:
                                project_out(h - 1, 0, 1 - k)
                            if i == 3 and not last:
                                if first:
                                    pe.wait_ge(e["g_y2_ready"], 2)
                                else:
                                    pe.wait_ge(e["g_hacc_ready"], 2 * h + 1)
                                queries(h + 1, 0, 1 - k)
                            if i == 4 and not last:
                                pe.wait_ge(e["g_y2_ready"], 2 * h + 3)
                                queries(h + 1, 1, 1 - k)
                            if i == 5 and not first:
                                if last:
                                    pe.wait_ge(e["g_hacc_ready"], 2 * h + 1)
                                else:
                                    pe.wait_ge(e["g_y2_ready"], 2 * h + 4)
                                spread_inverse(h - 1, 1)
                            if i == 6 and not first:
                                project(h - 1, 1, 1 - k)
                            if i == 7 and not first:
                                project_out(h - 1, 1, 1 - k)

                    pe.wait_ge(e["g_x_loaded"], 32)
                    for t in range(NT):
                        mm = nc.tensor.transpose(ps_s[0][:, t * P:(t + 1) * P], x_rows[:, t, :], ident[:, :])
                    mm.then_inc(e["g_xT_ready"], 1)
                    pe.wait_ge(e["g_x_stacked"], 2)
                    pe.wait_ge(e["g_v_rest"], 1)
                    queries(0, 0, 0)
                    pe.wait_ge(e["g_y2_ready"], 1)
                    queries(0, 1, 0)
                    score(0, 0, 0)
                    score(0, 1, 0)
                    head(0, 0, first=True)
                    with pe.Fori(0, HEADS // 2 - 1) as pair:
                        head(2 * pair + 1, 1)
                        head(2 * pair + 2, 0)
                    head(HEADS - 1, 1, last=True)
                    for half in range(2):
                        if half == 1:
                            for chunk in range(4):
                                mix(HEADS - 1, 1, chunk)
                        pe.wait_ge(e["g_hacc_ready"], 2 * HEADS + half)
                        spread_inverse(HEADS - 1, half)
                        project(HEADS - 1, half, 1)
                        project_out(HEADS - 1, half, 1)

                    pe.wait_ge(e["g_hacc_ready"], 2 * HEADS + 2)
                    for t in range(NT):
                        mm = nc.tensor.transpose(ps_s[0][:, t * P:(t + 1) * P], hidden[:, t * P:(t + 1) * P], ident[:, :])
                    mm.then_inc(e["g_hT_ready"], 1)
                    pe.wait_ge(e["g_h_split"], 3)
                    pe.wait_ge(e["g_v_rest"], 2)
                    score(LAST, 0, 0)
                    score(LAST, 1, 0)
                    for i in range(NT):
                        transpose(LAST, i)
                        if i + 2 < NT:
                            score(LAST, i + 2, 0)
                        if i >= 4:
                            mix(LAST, 0, i - 4)
                    for half in range(2):
                        if half == 1:
                            for chunk in range(4):
                                mix(LAST, 1, chunk)
                        pe.wait_ge(e["g_ut_ready"], 2 * LAST + half + 1)
                        if half == 1:
                            pe.wait_ge(e["g_out_ready"], 1)
                        for j in range(4):
                            mm = nc.tensor.matmul(ps_x[:, j * C:(j + 1) * C], mixed[:, j * P:(j + 1) * P], ident2[:, :],
                                                  start=True, stop=True)
                        mm.then_inc(e["g_rb_ready"], 1)

                @block.scalar
                def _(act):
                    def exponentials(h, i):
                        n = 8 * h + i
                        act.wait_ge(e["g_t_ready"], n + 1)
                        if not isinstance(n, int) or n >= 2:
                            act.wait_ge(e["g_pt_ready"], 2 * n - 2)
                        if i % 4 == 0 and not (isinstance(h, int) and h == 0):
                            act.wait_ge(e["g_ri_ready"], 2 * h - 1 + i // 4)
                        nc.scalar.activation(probs[i % 2][:, :], scores[i % 2][:, :], ACT.Exp, bias=neg_max[i % 2][:, :],
                                             accum_out=row_sum[:, i:i + 1]).then_inc(e["g_p_ready"], 1)

                    def high(h, i):
                        n = 8 * h + i
                        half, j = i // 4, i % 4
                        for a in range(2):
                            if j == 0 and a == 0 and not (isinstance(h, int) and h == 0):
                                act.wait_ge(e["g_u_ready"], 2 * h - 1 + half)
                            act.wait_ge(e["g_pt_ready"], 2 * n + a + 1)
                            nc.scalar.activation(pt_hi[half][:, 4 * a:4 * a + 4, j * P:(j + 1) * P],
                                                 ps_t[a][:, :].rearrange("p (m n) -> p m n", n=P), ACT.Copy).then_inc(e["g_hi_ready"], 1)

                    def take_mixed(h, half):
                        act.wait_ge(e["g_u_ready"], 2 * h + half + 1)
                        nc.scalar.activation(mixed[:, :], ps_u[:, :], ACT.Copy).then_inc(e["g_ut_ready"], 1)

                    def add_bias(h, half, k):
                        act.wait_ge(e["g_cat_ready"], 2 * h + half + 1)
                        nc.scalar.activation(cat_b[:, :], ps_x[:, :], ACT.Identity, bias=W_cur[k][:, 2 * P:2 * P + 1]).then_inc(e["g_vb_ready"], 1)

                    def round_queries(h, half, k):
                        act.wait_ge(e["g_y_ready"], 2 * h + half + 1)
                        nc.scalar.activation(query[k][:, half * HN:(half + 1) * HN], ps_x[:, :], ACT.Copy).then_inc(e["g_yr_ready"], 1)

                    def head(h, k, first=False, last=False):
                        for i in range(NT):
                            high(h, i)
                            if i + 1 < NT:
                                exponentials(h, i + 1)
                            elif not last:
                                exponentials(h + 1, 0)
                            if i == 0 and not first:
                                take_mixed(h - 1, 0)
                            if i == 1 and not first:
                                add_bias(h - 1, 0, 1 - k)
                            if i == 3 and not last:
                                round_queries(h + 1, 0, 1 - k)
                            if i == 4 and not first:
                                take_mixed(h - 1, 1)
                            if i == 4 and not last:
                                round_queries(h + 1, 1, 1 - k)
                            if i == 6 and not first:
                                add_bias(h - 1, 1, 1 - k)

                    act.wait_ge(e["g_xT_ready"], 1)
                    nc.scalar.activation(moving_hi[:, :], ps_s[0][:, :], ACT.Copy).then_inc(e["g_x_high"], 1)
                    round_queries(0, 0, 0)
                    round_queries(0, 1, 0)
                    exponentials(0, 0)
                    head(0, 0, first=True)
                    with act.Fori(0, HEADS // 2 - 1) as pair:
                        head(2 * pair + 1, 1)
                        head(2 * pair + 2, 0)
                    head(HEADS - 1, 1, last=True)
                    for half in range(2):
                        take_mixed(HEADS - 1, half)
                        add_bias(HEADS - 1, half, 1)

                    act.wait_ge(e["g_hacc_ready"], 2 * HEADS + 2)
                    nc.scalar.activation(moving_hi[:, :], hidden[:, :], ACT.Copy).then_inc(e["g_h_split"], 1)
                    exponentials(LAST, 0)
                    for i in range(NT):
                        high(LAST, i)
                        if i + 1 < NT:
                            exponentials(LAST, i + 1)
                    for half in range(2):
                        act.wait_ge(e["g_u_ready"], 2 * LAST + half + 1)
                        if half == 1:
                            act.wait_ge(e["g_rb_ready"], 2 * HEADS + 1)
                        nc.scalar.activation(mixed[:, :], ps_u[:, :], ACT.Copy).then_inc(e["g_ut_ready"], 1)

                @block.vector
                def _(dve):
                    def mask_and_max(h, i):
                        n = 8 * h + i
                        if not isinstance(n, int) or n >= 2:
                            dve.wait_ge(e["g_p_ready"], n - 1)
                        dve.wait_ge(e["g_s_ready"], n + 1)
                        nc.vector.memset(waiter[:, :], 0.0)
                        nc.vector.tensor_tensor_reduce(out=scores[i % 2][:, :], in0=ps_s[i % 2][:, :], in1=graph[:, i, :],
                                                       scale=1.0, scalar=LOWEST, op0=ALU.mult, op1=ALU.max,
                                                       accum_out=row_max[i % 2][:, :]).then_inc(e["g_m_ready"], 1)
                        dve.wait_ge(e["g_m_ready"], n + 1)
                        nc.vector.tensor_scalar(neg_max[i % 2][:, :], row_max[i % 2][:, :], -1.0, None, ALU.mult).then_inc(e["g_t_ready"], 1)

                    def rest(h, i):
                        n = 8 * h + i
                        half, j = i // 4, i % 4
                        for a in range(2):
                            dve.wait_ge(e["g_hi_ready"], 2 * n + a + 1)
                            into = (slice(None), slice(4 * a, 4 * a + 4), slice(j * P, (j + 1) * P))
                            nc.vector.tensor_tensor(pt_lo[half][into], ps_t[a][:, :].rearrange("p (m n) -> p m n", n=P),
                                                    pt_hi[half][into].bitcast(F32), ALU.subtract).then_inc(e["g_lo_ready"], 1)

                    def inverse(h, half):
                        dve.wait_ge(e["g_p_ready"], 8 * h + 4 * half + 4)
                        if not (isinstance(h, int) and h == 0):
                            dve.wait_ge(e["g_rb_ready"], 2 * h - 1 + half)
                        cols = slice(4 * half, 4 * half + 4)
                        nc.vector.reciprocal(row_inv[:, cols], row_sum[:, cols]).then_inc(e["g_ri_ready"], 1)

                    def scale_mixed(h, half):
                        dve.wait_ge(e["g_ut_ready"], 2 * h + half + 1)
                        dve.wait_ge(e["g_rb_ready"], 2 * h + half + 1)
                        nc.vector.tensor_tensor(mixed_n[:, :], mixed[:, :], ps_x[:, :], ALU.mult).then_inc(e["g_un_ready"], 1)

                    def leaky(h, half):
                        dve.wait_ge(e["g_vb_ready"], 2 * h + half + 1)
                        nc.vector.scalar_tensor_tensor(cat[:, :], cat_b[:, :], 0.01, cat_b[:, :], ALU.mult, ALU.max).then_inc(e["g_v_ready"], 1)

                    def collect(h, half):
                        dve.wait_ge(e["g_hp_ready"], 2 * h + half + 1)
                        cols = slice(half * HN, (half + 1) * HN)
                        dve.wait_ge(e["g_hacc_ready"], 2 * h + half + 1)
                        nc.vector.tensor_tensor(hidden[:, cols], hidden[:, cols], ps_x[:, :], ALU.add).then_inc(e["g_hacc_ready"], 1)

                    def rest_of_queries(h, half, k):
                        dve.wait_ge(e["g_yr_ready"], 2 * h + half + 1)
                        cols = slice(half * HN, (half + 1) * HN)
                        nc.vector.tensor_tensor(query[k][C:P, cols], ps_x[C:P, :], query[k][C:P, cols].bitcast(F32),
                                                ALU.subtract).then_inc(e["g_y2_ready"], 1)

                    def head(h, k, first=False, last=False):
                        for i in range(NT):
                            if i + 1 < NT:
                                mask_and_max(h, i + 1)
                            elif not last:
                                mask_and_max(h + 1, 0)
                            rest(h, i)
                            if i == 0 and not first:
                                scale_mixed(h - 1, 0)
                            if i == 1 and not first:
                                leaky(h - 1, 0)
                            if i == 2 and not first:
                                collect(h - 1, 0)
                            if i == 3:
                                inverse(h, 0)
                            if i == 3 and not last:
                                rest_of_queries(h + 1, 0, 1 - k)
                            if i == 4 and not last:
                                rest_of_queries(h + 1, 1, 1 - k)
                            if i == 5 and not first:
                                scale_mixed(h - 1, 1)
                            if i == 6 and not first:
                                leaky(h - 1, 1)
                            if i == 7 and not first:
                                collect(h - 1, 1)
                            if i == 7:
                                inverse(h, 1)

                    for half in range(2):
                        nc.vector.memset(hidden[:, half * HN:(half + 1) * HN], 0.0).then_inc(e["g_hacc_ready"], 1)
                    dve.wait_ge(e["g_x_high"], 1)
                    nc.vector.tensor_tensor(moving_lo[:, :], ps_s[0][:, :], moving_hi[:, :].bitcast(F32), ALU.subtract).then_inc(e["g_x_rest"], 1)
                    nc.vector.tensor_copy(moving_hl[0:C, :], moving_hi[0:C, :].bitcast(F32)).then_inc(e["g_x_stacked"], 1)
                    dve.wait_ge(e["g_x_rest"], 1)
                    nc.vector.tensor_copy(moving_hl[C:P, :], moving_lo[C:P, :].bitcast(F32)).then_inc(e["g_x_stacked"], 1)
                    dve.wait_ge(e["g_x_loaded"], 32)
                    nc.vector.tensor_copy(value_hl[:, :, 0:C], x_rows[:, :, 0:C]).then_inc(e["g_v_high"], 1)
                    dve.wait_ge(e["g_v_high"], 1)
                    nc.vector.tensor_tensor(value_hl[:, :, C:P], x_rows[:, :, C:P], value_hl[:, :, 0:C].bitcast(F32),
                                            ALU.subtract).then_inc(e["g_v_rest"], 1)
                    rest_of_queries(0, 0, 0)
                    rest_of_queries(0, 1, 0)
                    mask_and_max(0, 0)
                    head(0, 0, first=True)
                    with dve.Fori(0, HEADS // 2 - 1) as pair:
                        head(2 * pair + 1, 1)
                        head(2 * pair + 2, 0)
                    head(HEADS - 1, 1, last=True)
                    for half in range(2):
                        scale_mixed(HEADS - 1, half)
                        leaky(HEADS - 1, half)
                        collect(HEADS - 1, half)

                    dve.wait_ge(e["g_h_split"], 1)
                    nc.vector.tensor_tensor(moving_lo[:, :], hidden[:, :], moving_hi[:, :].bitcast(F32), ALU.subtract).then_inc(e["g_x_rest"], 1)
                    nc.vector.tensor_copy(query[0][0:C, :], moving_hi[0:C, :].bitcast(F32)).then_inc(e["g_h_split"], 1)
                    dve.wait_ge(e["g_x_rest"], 2)
                    nc.vector.tensor_copy(query[0][C:P, :], moving_lo[C:P, :].bitcast(F32)).then_inc(e["g_h_split"], 1)
                    dve.wait_ge(e["g_hT_ready"], 1)
                    hT = ps_s[0][:, :].rearrange("p (t c) -> p t c", c=P)
                    nc.vector.tensor_copy(value_hl[:, :, 0:C], hT[:, :, 0:C]).then_inc(e["g_v_high"], 1)
                    dve.wait_ge(e["g_v_high"], 2)
                    nc.vector.tensor_tensor(value_hl[:, :, C:P], hT[:, :, C:P], value_hl[:, :, 0:C].bitcast(F32),
                                            ALU.subtract).then_inc(e["g_v_rest"], 1)
                    mask_and_max(LAST, 0)
                    for i in range(NT):
                        if i + 1 < NT:
                            mask_and_max(LAST, i + 1)
                        rest(LAST, i)
                        if i == 3:
                            inverse(LAST, 0)
                    inverse(LAST, 1)

                    done = 0
                    for half in range(2):
                        tiles = slice(4 * half, 4 * half + 4)
                        dve.wait_ge(e["g_rb_ready"], 2 * HEADS + half + 1)
                        dve.wait_ge(e["g_ri_ready"], 2 * LAST + half + 1)
                        nc.vector.tensor_tensor(y[:, tiles, :], ps_x[:, 0:4 * C].rearrange("p (t c) -> p t c", c=C),
                                                row_inv[:, tiles].unsqueeze(2).broadcast_to([P, 4, C]), ALU.mult).then_inc(e["g_out_ready"], 1)
                    dve.wait_ge(e["g_out_ready"], 2)

                    def link(ins):
                        nonlocal done
                        done += 1
                        ins.then_inc(e["g_norm"], 1)
                        dve.wait_ge(e["g_norm"], done)

                    bias = b_out_row[:, :].unsqueeze(1).broadcast_to([P, NT, C])
                    link(nc.vector.tensor_tensor(y[:, :, :], y[:, :, :], bias, ALU.add))
                    link(nc.vector.scalar_tensor_tensor(y[:, :, :], y[:, :, :], 0.01, y[:, :, :], ALU.mult, ALU.max))
                    link(nc.vector.tensor_tensor(y[:, :, :], y[:, :, :], x_rows[:, :, 0:C], ALU.add))
                    layer_norm_rows(nc, dve, link, y[:, :, :], sq[:, :, :], mean[:, :], var[:, :], rstd[:, :],
                                    e["g_var_ready"], e["g_rstd_ready"], e["g_y_done"])
            nc.all_engine_barrier(sems_to_clear=numbers(e))


def causal_steps(nc, bank, io, adjT_dram, x_in, x_out):
    STEPS = 3
    ctx = ExitStack()
    with ctx:
        def sb(name, shape, dt=F32):
            return ctx.enter_context(nc.sbuf_tensor(name, shape, dt))

        adjT = sb("c_adjT", [P, NT, N])
        ident = sb("c_ident", [P, P])
        w_stage = sb("c_w_stage", [C, 3, P])
        w_diag = sb("c_w_diag", [P, 3, P])
        b1 = sb("c_b1", [P, 1])
        b2 = sb("c_b2", [P, 1])
        b2_row = sb("c_b2_row", [P, P])
        x_rows = sb("c_x_rows", [P, NT, BATCH, C])
        v_rows = sb("c_v_rows", [P, NT, BATCH, C])
        vT = sb("c_vT", [P, PAIRS, N])
        effect = [sb(f"c_effect{k}", [P, N]) for k in range(2)]
        hidden = [sb(f"c_hidden{k}", [P, N]) for k in range(2)]
        sq = sb("c_sq", [P, NT * BATCH, C])
        mean = sb("c_mean", [P, NT * BATCH])
        var = sb("c_var", [P, NT * BATCH])
        rstd = sb("c_rstd", [P, NT * BATCH])
        minus_half = sb("c_minus_half", [P, NT * BATCH])
        ps_e = [ctx.enter_context(nc.psum_tensor(f"c_ps_e{k}", [P, N], F32)) for k in range(2)]
        ps_h = ctx.enter_context(nc.psum_tensor("c_ps_h", [P, N], F32))
        ps_v = ctx.enter_context(nc.psum_tensor("c_ps_v", [P, N], F32))

        def columns(p):
            return v_rows[:, :, 2 * p:2 * p + 2, :]

        setup = events(bank, "c_w_loaded c_adj_loaded c_x_loaded c_v_loaded c_zeroed c_ident_ready c_w_zeroed "
                                "c_wT_ready c_w_ready c_half_ready c_vT_ready c_vT_copied c_intervened")
        with nc.Block() as block:
            e = setup

            @block.sync
            def _(sp):
                xr = x_in.rearrange("b (t p) c -> p t b c", p=P)
                for t in range(NT):
                    sp.dma_start(x_rows[:, t, :, :], xr[:, t, :, :]).then_inc(e["c_x_loaded"], 16)
                    sp.dma_start(v_rows[:, t, :, :], xr[:, t, :, :]).then_inc(e["c_v_loaded"], 16)
                for k in range(2):
                    half = slice(k * C, (k + 1) * C)
                    for i, src in enumerate((io["L2_gnn_W1"][:, 0:C], io["L2_gnn_W1"][:, C:2 * C], io["L2_gnn_W2"])):
                        sp.dma_start(w_stage[:, i, half], src).then_inc(e["c_w_loaded"], 16)
                    sp.dma_start(b1[half, :], io["L2_gnn_b1"].rearrange("(c o) -> c o", o=1)).then_inc(e["c_w_loaded"], 16)
                    sp.dma_start(b2[half, :], io["L2_gnn_b2"].rearrange("(c o) -> c o", o=1)).then_inc(e["c_w_loaded"], 16)
                    sp.dma_start(b2_row[:, half], io["L2_gnn_b2"].partition_broadcast(P)).then_inc(e["c_w_loaded"], 16)
                sp.wait_ge(e["c_v_loaded"], 16 * NT)
                for b in range(BATCH):
                    sp.dma_start(v_rows[0:1, 0, b, :], io["L2_gnn_intervention_value"]).then_inc(e["c_intervened"], 16)
                sp.dma_start(adjT[:, :, :], adjT_dram.rearrange("(t p) n -> p t n", p=P)).then_inc(e["c_adj_loaded"], 16)
                sp.wait_ge(e["c_adj_loaded"], 16)
                sp.wait_ge(e["c_x_loaded"], 16 * NT)

            @block.gpsimd
            def _(pool):
                make_identity(pool, ident, e["c_zeroed"], e["c_ident_ready"], 0)
                nc.gpsimd.memset(w_diag[:, :, :], 0.0).then_inc(e["c_w_zeroed"], 1)
                nc.gpsimd.memset(minus_half[:, :], -0.5).then_inc(e["c_half_ready"], 1)

            @block.tensor
            def _(pe):
                pe.wait_ge(e["c_ident_ready"], 1)
                pe.wait_ge(e["c_w_loaded"], 16 * 12)
                for i in range(3):
                    mm = nc.tensor.transpose(ps_h[:, i * C:(i + 1) * C], w_stage[:, i, :], ident[0:C, 0:C])
                mm.then_inc(e["c_wT_ready"], 1)
                pe.wait_ge(e["c_intervened"], 16 * BATCH)
                for p in range(PAIRS):
                    if p >= 2:
                        pe.wait_ge(e["c_vT_copied"], p - 1)
                    for t in range(NT):
                        mm = nc.tensor.transpose(ps_e[p % 2][:, t * P:(t + 1) * P],
                                                 v_rows[:, t, 2 * p:2 * p + 2, :].rearrange("p b c -> p (b c)"), ident[:, :])
                    mm.then_inc(e["c_vT_ready"], 1)

            @block.vector
            def _(dve):
                dve.wait_ge(e["c_w_zeroed"], 1)
                dve.wait_ge(e["c_wT_ready"], 1)
                for k in range(2):
                    half = slice(k * C, (k + 1) * C)
                    nc.vector.tensor_copy(w_diag[half, :, half], ps_h[half, 0:3 * C].rearrange("p (i c) -> p i c", c=C)).then_inc(e["c_w_ready"], 1)
                for p in range(PAIRS):
                    dve.wait_ge(e["c_vT_ready"], p + 1)
                    nc.vector.tensor_copy(vT[:, p, :], ps_e[p % 2][:, :]).then_inc(e["c_vT_copied"], 1)
        nc.all_engine_barrier(sems_to_clear=numbers(setup))

        e = events(bank, "c_effect_ready c_effect_copied c_hidden_ready c_hidden_copied c_next_ready "
                            "c_next_copied c_rows_ready c_rows_copied c_norm c_var_ready c_rstd_ready c_y_done c_stored")
        with nc.Fori(0, STEPS) as step:
            with nc.Block() as block:

                @block.tensor
                def _(pe):
                    for u in range(PAIRS + 2):
                        if u < PAIRS:
                            if u >= 2:
                                pe.wait_ge(e["c_effect_copied"], u - 1)
                            for m in range(2):
                                cols = slice(m * HN, (m + 1) * HN)
                                for t in range(NT):
                                    mm = nc.tensor.matmul(ps_e[u % 2][:, cols], v_rows[:, t, 2 * u:2 * u + 2, :].rearrange("p b c -> p (b c)"),
                                                          adjT[:, t, cols], start=(t == 0), stop=(t == NT - 1))
                            mm.then_inc(e["c_effect_ready"], 1)
                        if u >= 2:
                            p = u - 2
                            pe.wait_ge(e["c_hidden_copied"], p + 1)
                            if p >= 1:
                                pe.wait_ge(e["c_rows_copied"], p)
                            for m in range(2):
                                cols = slice(m * HN, (m + 1) * HN)
                                mm = nc.tensor.matmul(ps_v[:, cols], w_diag[:, 2, :], hidden[p % 2][:, cols], start=True, stop=True)
                            mm.then_inc(e["c_next_ready"], 1)
                            pe.wait_ge(e["c_next_copied"], p + 1)
                            for t in range(NT):
                                mm = nc.tensor.matmul(ps_v[:, t * P:(t + 1) * P], hidden[p % 2][:, t * P:(t + 1) * P], w_diag[:, 2, :],
                                                      start=True, stop=True)
                            mm.then_inc(e["c_rows_ready"], 1)
                        if 1 <= u <= PAIRS:
                            p = u - 1
                            pe.wait_ge(e["c_effect_copied"], p + 1)
                            if p >= 1:
                                pe.wait_ge(e["c_hidden_copied"], p)
                            for m in range(2):
                                cols = slice(m * HN, (m + 1) * HN)
                                nc.tensor.matmul(ps_h[:, cols], w_diag[:, 0, :], vT[:, p, cols], start=True, stop=False)
                                mm = nc.tensor.matmul(ps_h[:, cols], w_diag[:, 1, :], effect[p % 2][:, cols], start=False, stop=True)
                            mm.then_inc(e["c_hidden_ready"], 1)

                @block.scalar
                def _(act):
                    for p in range(PAIRS):
                        act.wait_ge(e["c_hidden_ready"], p + 1)
                        if p >= 2:
                            act.wait_ge(e["c_rows_ready"], p - 1)
                        nc.scalar.activation(hidden[p % 2][:, :], ps_h[:, :], ACT.Relu, bias=b1[:, :]).then_inc(e["c_hidden_copied"], 1)
                        act.wait_ge(e["c_next_ready"], p + 1)
                        nc.scalar.activation(vT[:, p, :], ps_v[:, :], ACT.Identity, bias=b2[:, :]).then_inc(e["c_next_copied"], 1)

                @block.vector
                def _(dve):
                    def take_effect(p):
                        dve.wait_ge(e["c_effect_ready"], p + 1)
                        if p >= 2:
                            dve.wait_ge(e["c_hidden_ready"], p - 1)
                        nc.vector.tensor_copy(effect[p % 2][:, :], ps_e[p % 2][:, :]).then_inc(e["c_effect_copied"], 1)

                    take_effect(0)
                    take_effect(1)
                    for p in range(PAIRS):
                        if p + 2 < PAIRS:
                            take_effect(p + 2)
                        dve.wait_ge(e["c_rows_ready"], p + 1)
                        nc.vector.tensor_tensor(columns(p).rearrange("p t b c -> p t (b c)"), ps_v[:, :].rearrange("p (t c) -> p t c", c=P),
                                                b2_row[:, :].unsqueeze(1).broadcast_to([P, NT, P]), ALU.add).then_inc(e["c_rows_copied"], 1)
            nc.all_engine_barrier(sems_to_clear=numbers(e))

        with nc.Block() as block:
            v_all = v_rows[:, :, :, :].rearrange("p t b c -> p (t b) c")

            @block.vector
            def _(dve):
                done = 0

                def link(ins):
                    nonlocal done
                    done += 1
                    ins.then_inc(e["c_norm"], 1)
                    dve.wait_ge(e["c_norm"], done)

                link(nc.vector.tensor_tensor(v_all, v_all, x_rows[:, :, :, :].rearrange("p t b c -> p (t b) c"), ALU.add))
                layer_norm_rows(nc, dve, link, v_all, sq[:, :, :], mean[:, :], var[:, :], rstd[:, :],
                                e["c_var_ready"], e["c_rstd_ready"], e["c_y_done"])

            @block.gpsimd
            def _(pool):
                pool.wait_ge(e["c_var_ready"], 1)
                nc.gpsimd.tensor_tensor(rstd[:, :], var[:, :], minus_half[:, :], ALU.pow).then_inc(e["c_rstd_ready"], 1)

            @block.sync
            def _(sp):
                sp.wait_ge(e["c_y_done"], 1)
                for t in range(NT):
                    sp.dma_start(x_out.rearrange("b (t p) c -> p t b c", p=P)[:, t, :, :], v_rows[:, t, :, :]).then_inc(e["c_stored"], 16)
                sp.wait_ge(e["c_stored"], 16 * NT)
        nc.all_engine_barrier(sems_to_clear=numbers(e))


def adaptive_chebyshev(nc, bank, io, adjT_dram, x_in, x_out):
    D = io["L3_gnn_node_embeddings"].shape[1]
    ctx = ExitStack()
    with ctx:
        def sb(name, shape, dt=F32):
            return ctx.enter_context(nc.sbuf_tensor(name, shape, dt))

        adjT = sb("k_adjT", [P, NT, N])
        aptT = sb("k_aptT", [P, NT, N])
        ident = sb("k_ident", [P, P])
        embed = sb("k_embed", [P, NT, D])
        embedT = sb("k_embedT", [D, N])
        pool_w = sb("k_pool_w", [P, 2, D, C])
        pool_b = sb("k_pool_b", [D, C])
        bias = sb("k_bias", [P, NT, C])
        g01 = sb("k_g01", [P, NT, BATCH, 2, C])
        g23 = sb("k_g23", [P, NT, BATCH, 2, C])
        relu = sb("k_relu", [P, N])
        probs = [sb(f"k_probs{k}", [P, N]) for k in range(2)]
        row_max = sb("k_row_max", [P, NT])
        row_sum = sb("k_row_sum", [P, NT])
        row_inv = sb("k_row_inv", [P, NT])
        stage = [sb(f"k_stage{k}", [P, 2, BATCH, P]) for k in range(2)]
        gT = [sb(f"k_gT{k}", [P, 2, P]) for k in range(2)]
        mixed = [probs[0], probs[1]]
        y = sb("k_y", [P, 2, BATCH, C])
        sq = sb("k_sq", [P, 2 * BATCH, C])
        mean = sb("k_mean", [P, 2 * BATCH])
        var = sb("k_var", [P, 2 * BATCH])
        rstd = sb("k_rstd", [P, 2 * BATCH])
        minus_half = sb("k_minus_half", [P, 2 * BATCH])
        ps_a = [ctx.enter_context(nc.psum_tensor(f"k_ps_a{k}", [P, N], F32)) for k in range(2)]
        ps_b = [ctx.enter_context(nc.psum_tensor(f"k_ps_b{k}", [P, HN], F32)) for k in range(2)]

        setup = events(bank, "k_adj_loaded k_x_loaded k_e_loaded k_w_loaded k_zeroed k_ident_ready k_half_ready "
                                "k_eT_ready k_eT_copied k_bias_ready k_bias_copied k_s_ready k_relu_ready k_max_ready "
                                "k_p_ready k_pt_ready k_pt_copied k_inv_ready k_x1_ready k_x1_copied k_x2_ready "
                                "k_x2_copied k_x3_ready k_x3_copied")
        with nc.Block() as block:
            e = setup

            @block.sync
            def _(sp):
                sp.dma_start(embed[:, :, :], io["L3_gnn_node_embeddings"].rearrange("(t p) d -> p t d", p=P)).then_inc(e["k_e_loaded"], 16)
                for t in range(NT):
                    sp.dma_start(g01[:, t, :, 0, :], x_in.rearrange("b (t p) c -> p t b c", p=P)[:, t, :, :]).then_inc(e["k_x_loaded"], 16)
                sp.dma_start(adjT[:, :, :], adjT_dram.rearrange("(t p) n -> p t n", p=P)).then_inc(e["k_adj_loaded"], 16)
                for k in range(4):
                    sp.dma_start(pool_w[(k % 2) * C:(k % 2 + 1) * C, k // 2, :, :],
                                 io["L3_gnn_weights_pool"][:, k, :, :].rearrange("d i o -> i d o")).then_inc(e["k_w_loaded"], 16)
                sp.dma_start(pool_b[:, :], io["L3_gnn_bias_pool"]).then_inc(e["k_w_loaded"], 16)
                sp.wait_ge(e["k_w_loaded"], 16 * 5)

            @block.gpsimd
            def _(pool):
                make_identity(pool, ident, e["k_zeroed"], e["k_ident_ready"], 0)
                nc.gpsimd.memset(minus_half[:, :], -0.5).then_inc(e["k_half_ready"], 1)

            @block.tensor
            def _(pe):
                pe.wait_ge(e["k_ident_ready"], 1)
                pe.wait_ge(e["k_e_loaded"], 16)
                for t in range(NT):
                    mm = nc.tensor.transpose(ps_a[0][0:D, t * P:(t + 1) * P], embed[:, t, :], ident[:, :])
                mm.then_inc(e["k_eT_ready"], 1)
                pe.wait_ge(e["k_eT_copied"], 1)
                pe.wait_ge(e["k_w_loaded"], 16 * 5)
                for t in range(NT):
                    mm = nc.tensor.matmul(ps_b[0][:, t * C:(t + 1) * C], embedT[:, t * P:(t + 1) * P], pool_b[:, :], start=True, stop=True)
                mm.then_inc(e["k_bias_ready"], 1)
                for t in range(NT + 1):
                    if t < NT:
                        if t >= 1:
                            pe.wait_ge(e["k_relu_ready"], t)
                        for m in range(2):
                            cols = slice(m * HN, (m + 1) * HN)
                            mm = nc.tensor.matmul(ps_a[0][:, cols], embedT[:, t * P:(t + 1) * P], embedT[:, cols], start=True, stop=True)
                        mm.then_inc(e["k_s_ready"], 1)
                    if t >= 1:
                        pe.wait_ge(e["k_p_ready"], t)
                        if t >= 2:
                            pe.wait_ge(e["k_pt_copied"], t - 1)
                        for s in range(NT):
                            mm = nc.tensor.transpose(ps_a[1][:, s * P:(s + 1) * P], probs[(t - 1) % 2][:, s * P:(s + 1) * P], ident[:, :])
                        mm.then_inc(e["k_pt_ready"], 1)

                def apply(matrixT, source, ready, copied, before):
                    for t in range(NT):
                        if before + t >= 2:
                            pe.wait_ge(*copied(t))
                        for s in range(NT):
                            mm = nc.tensor.matmul(ps_b[t % 2][:, :], matrixT[:, s, t * P:(t + 1) * P], source(s),
                                                  start=(s == 0), stop=(s == NT - 1))
                        mm.then_inc(ready, 1)

                pe.wait_ge(e["k_adj_loaded"], 16)
                pe.wait_ge(e["k_x_loaded"], 16 * NT)
                pe.wait_ge(e["k_bias_copied"], 1)
                apply(adjT, lambda s: g01[:, s, :, 0, :], e["k_x1_ready"], lambda t: (e["k_x1_copied"], t - 1), 0)
                pe.wait_ge(e["k_x1_copied"], NT)
                apply(adjT, lambda s: g01[:, s, :, 1, :], e["k_x2_ready"], lambda t: (e["k_x2_copied"], t - 1), 0)
                pe.wait_ge(e["k_x2_copied"], NT)
                pe.wait_ge(e["k_pt_copied"], NT)
                apply(aptT, lambda s: g01[:, s, :, 0, :], e["k_x3_ready"], lambda t: (e["k_x3_copied"], t - 1), 0)

            @block.scalar
            def _(act):
                act.wait_ge(e["k_eT_ready"], 1)
                nc.scalar.activation(embedT[:, :], ps_a[0][0:D, :], ACT.Copy).then_inc(e["k_eT_copied"], 1)
                for t in range(NT):
                    act.wait_ge(e["k_s_ready"], t + 1)
                    if t >= 1:
                        act.wait_ge(e["k_p_ready"], t)
                    nc.scalar.activation(relu[:, :], ps_a[0][:, :], ACT.Relu).then_inc(e["k_relu_ready"], 1)
                    act.wait_ge(e["k_max_ready"], t + 1)
                    if t >= 2:
                        act.wait_ge(e["k_pt_ready"], t - 1)
                    nc.scalar.activation(probs[t % 2][:, :], relu[:, :], ACT.Exp, bias=row_max[:, t:t + 1],
                                         accum_out=row_sum[:, t:t + 1]).then_inc(e["k_p_ready"], 1)
                for t in range(NT):
                    act.wait_ge(e["k_x1_ready"], t + 1)
                    nc.scalar.activation(g01[:, t, :, 1, :], ps_b[t % 2][:, :].rearrange("p (b c) -> p b c", c=C), ACT.Copy).then_inc(e["k_x1_copied"], 1)
                act.wait_ge(e["k_inv_ready"], 1)
                for t in range(NT):
                    act.wait_ge(e["k_x3_ready"], t + 1)
                    nc.scalar.activation(g23[:, t, :, 1, :], ps_b[t % 2][:, :].rearrange("p (b c) -> p b c", c=C), ACT.Copy,
                                         scale=row_inv[:, t:t + 1]).then_inc(e["k_x3_copied"], 1)

            @block.vector
            def _(dve):
                dve.wait_ge(e["k_bias_ready"], 1)
                nc.vector.tensor_copy(bias[:, :, :], ps_b[0][:, :].rearrange("p (t c) -> p t c", c=C)).then_inc(e["k_bias_copied"], 1)
                for t in range(NT):
                    dve.wait_ge(e["k_relu_ready"], t + 1)
                    nc.vector.tensor_reduce(row_max[:, t:t + 1], relu[:, :], AX.X, ALU.max, negate=True).then_inc(e["k_max_ready"], 1)
                    if t >= 1:
                        dve.wait_ge(e["k_pt_ready"], t)
                        nc.vector.tensor_copy(aptT[:, :, (t - 1) * P:t * P], ps_a[1][:, :].rearrange("p (s n) -> p s n", n=P)).then_inc(e["k_pt_copied"], 1)
                dve.wait_ge(e["k_pt_ready"], NT)
                nc.vector.tensor_copy(aptT[:, :, (NT - 1) * P:NT * P], ps_a[1][:, :].rearrange("p (s n) -> p s n", n=P)).then_inc(e["k_pt_copied"], 1)
                dve.wait_ge(e["k_p_ready"], NT)
                nc.vector.reciprocal(row_inv[:, :], row_sum[:, :]).then_inc(e["k_inv_ready"], 1)
                for t in range(NT):
                    dve.wait_ge(e["k_x2_ready"], t + 1)
                    nc.vector.scalar_tensor_tensor(g23[:, t, :, 0, :], ps_b[t % 2][:, :].rearrange("p (b c) -> p b c", c=C), 2.0,
                                                   g01[:, t, :, 0, :], ALU.mult, ALU.subtract).then_inc(e["k_x2_copied"], 1)
        nc.all_engine_barrier(sems_to_clear=numbers(setup))

        e = events(bank, "k_staged k_gT_ready k_gT_copied k_z_ready k_z_scaled k_sum_ready k_norm k_var_ready "
                            "k_rstd_ready k_y_done k_stored")
        UNITS = 2 * BATCH
        yT = x_out.rearrange("b (t p) c -> t p b c", p=P)
        with nc.Fori(0, NT // 2) as turn:
            with nc.Block() as block:

                @block.gpsimd
                def _(pool):
                    for k in range(2):
                        nc.gpsimd.tensor_copy(stage[k][:, 0, :, :], g01[:, 2 * turn + k, :, :, :].rearrange("p b k c -> p b (k c)")).then_inc(e["k_staged"], 1)
                        nc.gpsimd.tensor_copy(stage[k][:, 1, :, :], g23[:, 2 * turn + k, :, :, :].rearrange("p b k c -> p b (k c)")).then_inc(e["k_staged"], 1)
                    pool.wait_ge(e["k_var_ready"], 1)
                    nc.gpsimd.tensor_tensor(rstd[:, :], var[:, :], minus_half[:, :], ALU.pow).then_inc(e["k_rstd_ready"], 1)

                @block.tensor
                def _(pe):
                    for u in range(UNITS + 1):
                        if u < UNITS:
                            k, b = u // BATCH, u % BATCH
                            pe.wait_ge(e["k_staged"], 2 * k + 2)
                            if u >= 2:
                                pe.wait_ge(e["k_gT_copied"], u - 1)
                            for q in range(2):
                                mm = nc.tensor.transpose(ps_b[u % 2][:, q * P:(q + 1) * P], stage[k][:, q, b, :], ident[:, :])
                            mm.then_inc(e["k_gT_ready"], 1)
                        if u >= 1:
                            w = u - 1
                            pe.wait_ge(e["k_gT_copied"], w + 1)
                            if w >= 2:
                                pe.wait_ge(e["k_z_scaled"], w - 1)
                            for m in range(2):
                                cols = slice(m * HN, (m + 1) * HN)
                                for q in range(2):
                                    mm = nc.tensor.matmul(ps_a[w % 2][:, cols], gT[w % 2][:, q, :],
                                                          pool_w[:, q, m * D // 2:(m + 1) * D // 2, :].rearrange("p d o -> p (d o)"),
                                                          start=(q == 0), stop=(q == 1))
                            mm.then_inc(e["k_z_ready"], 1)

                @block.scalar
                def _(act):
                    for u in range(UNITS):
                        act.wait_ge(e["k_gT_ready"], u + 1)
                        if u >= 2:
                            act.wait_ge(e["k_z_ready"], u - 1)
                        nc.scalar.activation(gT[u % 2][:, :, :], ps_b[u % 2][:, 0:2 * P].rearrange("p (q n) -> p q n", n=P), ACT.Copy).then_inc(e["k_gT_copied"], 1)

                @block.vector
                def _(dve):
                    for u in range(UNITS):
                        k, b = u // BATCH, u % BATCH
                        dve.wait_ge(e["k_z_ready"], u + 1)
                        if u >= 2:
                            dve.wait_ge(e["k_sum_ready"], u - 1)
                        nc.vector.tensor_tensor(mixed[u % 2][:, :].rearrange("p (d o) -> p d o", o=C),
                                                ps_a[u % 2][:, :].rearrange("p (d o) -> p d o", o=C),
                                                embed[:, 2 * turn + k, :].unsqueeze(2).broadcast_to([P, D, C]), ALU.mult).then_inc(e["k_z_scaled"], 1)
                        dve.wait_ge(e["k_z_scaled"], u + 1)
                        nc.vector.tensor_reduce(y[:, k, b, :], mixed[u % 2][:, :].rearrange("p (d o) -> p o d", o=C), AX.X, ALU.add).then_inc(e["k_sum_ready"], 1)
                    done = 0

                    def link(ins):
                        nonlocal done
                        done += 1
                        ins.then_inc(e["k_norm"], 1)
                        dve.wait_ge(e["k_norm"], done)

                    dve.wait_ge(e["k_sum_ready"], UNITS)
                    for k in range(2):
                        link(nc.vector.tensor_tensor(y[:, k, :, :], y[:, k, :, :],
                                                     bias[:, 2 * turn + k, :].unsqueeze(1).broadcast_to([P, BATCH, C]), ALU.add))
                        link(nc.vector.tensor_tensor(y[:, k, :, :], y[:, k, :, :], g01[:, 2 * turn + k, :, 0, :], ALU.add))
                    layer_norm_rows(nc, dve, link, y[:, :, :, :].rearrange("p k b c -> p (k b) c"), sq[:, :, :], mean[:, :], var[:, :],
                                    rstd[:, :], e["k_var_ready"], e["k_rstd_ready"], e["k_y_done"])

                @block.sync
                def _(sp):
                    sp.wait_ge(e["k_y_done"], 1)
                    for k in range(2):
                        sp.dma_start(yT[2 * turn + k], y[:, k, :, :]).then_inc(e["k_stored"], 16)
                    sp.wait_ge(e["k_stored"], 32)
            nc.all_engine_barrier(sems_to_clear=numbers(e))


def adjacency_network(nc, io, out):
    adjT = nc.dram_tensor("adjT", (N, N), F32, kind="Internal").ap()
    x1, x2, x3 = (nc.dram_tensor(f"x{i}", (BATCH, N, C), F32, kind="Internal").ap() for i in (1, 2, 3))
    with ExitStack() as ctx:
        bank = [ctx.enter_context(nc.semaphore(f"signal{i}")) for i in range(60)]
        transpose_adjacency(nc, bank, io, adjT)
        hypergraph_attention(nc, bank, io, adjT, io["x"], x1)
        multi_head_gat(nc, bank, io, x1, x2)
        causal_steps(nc, bank, io, adjT, x2, x3)
        adaptive_chebyshev(nc, bank, io, adjT, x3, out)


_INS = ['x', 'adj', 'L0_gnn_H', 'L0_gnn_W', 'L0_gnn_W_ind', 'L0_gnn_a_node', 'L0_gnn_a_gn', 'L0_gnn_a_ge',
        'L0_gnn_fcW', 'L0_gnn_fcb', 'L0_gnn_av', 'L1_gnn_Wh', 'L1_gnn_bh', 'L1_gnn_W_out', 'L1_gnn_b_out',
        'L2_gnn_intervention_value', 'L2_gnn_W1', 'L2_gnn_b1', 'L2_gnn_W2', 'L2_gnn_b2',
        'L3_gnn_node_embeddings', 'L3_gnn_weights_pool', 'L3_gnn_bias_pool']


def kernel(**inputs):
    import numpy as _np
    import concourse.bacc as _bacc
    from concourse import mybir as _mybir
    from concourse.bass_utils import run_bass_kernel_spmd as _run

    nc = _bacc.Bacc("TRN2", target_bir_lowering=False, num_devices=1)
    arrays, io = {}, {}
    for name in _INS:
        a = _np.ascontiguousarray(inputs[name])
        arrays[f"in_{name}"] = a
        io[name] = nc.dram_tensor(f"in_{name}", a.shape, _mybir.dt.from_np(a.dtype), kind="ExternalInput").ap()
    out = nc.dram_tensor("out_0", (BATCH, N, C), F32, kind="ExternalOutput").ap()
    adjacency_network(nc, io, out)
    r = _run(nc, [arrays], core_ids=[0])
    return r.results[0]["out_0"]
```

```python
import concourse.bass as bass
from concourse import mybir
from contextlib import ExitStack

F32 = mybir.dt.float32
F32R = mybir.dt.float32r
BF16 = mybir.dt.bfloat16
ALU = mybir.AluOpType
ACT = mybir.ActivationFunctionType
AX = mybir.AxisListType

P = 128
BATCH, N, C = 8, 1024, 64
NT = N // P
HN = N // 2
HEADS, HC = 8, 128
EDGES = 64
PAIRS = BATCH // 2
MASKED = -1.0e16
NEG = -1.0e9
EPS = 1.0e-5
LOWEST = -3.0e38


def events(bank, names):
    names = names.split()
    assert len(names) <= len(bank)
    return dict(zip(names, bank))


def numbers(sems):
    every = [s.num for s in sems.values()]
    assert every == list(range(every[0], every[0] + len(every)))
    return range(every[0], every[0] + len(every))


def make_identity(pool, tile, zeroed, ready, before):
    pool.memset(tile[:, :], 0.0).then_inc(zeroed, 1)
    pool.wait_ge(zeroed, before + 1)
    pool.affine_select(out=tile[:, :], in_=tile[:, :], compare_op=ALU.not_equal, fill=1.0, base=0,
                       pattern=[[-1, tile.shape[1]]], channel_multiplier=1).then_inc(ready, 1)


def layer_norm_rows(nc, dve, link, y, sq, mean, var, rstd, var_ready, rstd_ready, done):
    groups = y.shape[1]

    def spread(v):
        return v.unsqueeze(2).broadcast_to([P, groups, C])

    link(nc.vector.tensor_reduce(mean, y, AX.X, ALU.add))
    link(nc.vector.tensor_scalar(mean, mean, 1.0 / C, None, ALU.mult))
    link(nc.vector.tensor_tensor(y, y, spread(mean), ALU.subtract))
    link(nc.vector.tensor_tensor(sq, y, y, ALU.mult))
    link(nc.vector.tensor_reduce(var, sq, AX.X, ALU.add))
    nc.vector.tensor_scalar(var, var, 1.0 / C, EPS, ALU.mult, ALU.add).then_inc(var_ready, 1)
    dve.wait_ge(rstd_ready, 1)
    nc.vector.tensor_tensor(y, y, spread(rstd), ALU.mult).then_inc(done, 1)


def transpose_adjacency(nc, bank, io, adjT_dram):
    ctx = ExitStack()
    with ctx:
        adj = ctx.enter_context(nc.sbuf_tensor("a_adj", [P, NT, N], F32))
        adjT = ctx.enter_context(nc.sbuf_tensor("a_adjT", [P, NT, N], F32))
        ident = ctx.enter_context(nc.sbuf_tensor("a_ident", [P, P], F32))
        ps = [ctx.enter_context(nc.psum_tensor(f"a_ps{k}", [P, N], F32)) for k in range(4)]
        e = events(bank, "a_loaded a_zeroed a_ident_ready a_transposed a_copied_even a_copied_odd a_stored")
        with nc.Block() as block:

            @block.sync
            def _(sp):
                for t in range(NT):
                    sp.dma_start(adj[:, t, :], io["adj"][t * P:(t + 1) * P, :]).then_inc(e["a_loaded"], 16)
                for t in range(NT):
                    sp.wait_ge(e["a_copied_even" if t % 2 == 0 else "a_copied_odd"], t // 2 + 1)
                    sp.dma_start(adjT_dram[t * P:(t + 1) * P, :], adjT[:, t, :]).then_inc(e["a_stored"], 16)
                sp.wait_ge(e["a_stored"], 16 * NT)

            @block.gpsimd
            def _(pool):
                make_identity(pool, ident, e["a_zeroed"], e["a_ident_ready"], 0)

            @block.tensor
            def _(pe):
                pe.wait_ge(e["a_ident_ready"], 1)
                pe.wait_ge(e["a_loaded"], 16 * NT)
                for t in range(NT):
                    if t >= 4:
                        pe.wait_ge(e["a_copied_even" if t % 2 == 0 else "a_copied_odd"], t // 2 - 1)
                    for s in range(NT):
                        mm = nc.tensor.transpose(ps[t % 4][:, s * P:(s + 1) * P], adj[:, s, t * P:(t + 1) * P], ident[:, :])
                    mm.then_inc(e["a_transposed"], 1)

            @block.vector
            def _(dve):
                for t in range(0, NT, 2):
                    dve.wait_ge(e["a_transposed"], t + 1)
                    nc.vector.tensor_copy(adjT[:, t, :], ps[t % 4][:, :]).then_inc(e["a_copied_even"], 1)

            @block.scalar
            def _(act):
                for t in range(1, NT, 2):
                    act.wait_ge(e["a_transposed"], t + 1)
                    nc.scalar.activation(adjT[:, t, :], ps[t % 4][:, :], ACT.Copy).then_inc(e["a_copied_odd"], 1)
        nc.all_engine_barrier(sems_to_clear=numbers(e))


def hypergraph_attention(nc, bank, io, adjT_dram, x_in, x_out):
    UNROLL = 4
    ctx = ExitStack()
    with ctx:
        def sb(name, shape, dt=F32):
            return ctx.enter_context(nc.sbuf_tensor(name, shape, dt))

        adjT = sb("h_adjT", [P, NT, N])
        inv_degree = sb("h_inv_degree", [P, N])
        ident = sb("h_ident", [P, P])
        ones = sb("h_ones", [P, P])
        pick = sb("h_pick", [P, EDGES, P], BF16)
        W_diag = sb("h_W_diag", [P, P])
        Wind_diag = sb("h_Wind_diag", [P, P])
        vectors = sb("h_vectors", [P, 3])
        spread3 = sb("h_spread3", [P, 3, P])
        fcW = sb("h_fcW", [P, P])
        fcb = sb("h_fcb", [P, 1])
        av = sb("h_av", [P, 1])
        av_half = sb("h_av_half", [P, 1])
        av_all = sb("h_av_all", [P, P])
        av_pair = sb("h_av_pair", [P, 2, 2, P])
        H_rows = sb("h_H_rows", [P, NT, 2, EDGES])
        mask_rows = sb("h_mask_rows", [P, NT, EDGES])
        fence_rows = sb("h_fence_rows", [P, NT, EDGES])
        maskT = sb("h_maskT", [P, N])
        fenceT = sb("h_fenceT", [P, N])
        x_rows = sb("h_x_rows", [P, NT, 2, C])
        xT = sb("h_xT", [P, N])
        hT = sb("h_hT", [P, N])
        half_hT = sb("h_half_hT", [P, N])
        h_rows = sb("h_h_rows", [P, NT, P])
        ind_rows = sb("h_ind_rows", [P, NT, P])
        indT = sb("h_indT", [P, N])
        gate_h = sb("h_gate_h", [P, N])
        logits = sb("h_logits", [P, N])
        alphaT = sb("h_alphaT", [P, NT, P])
        neg_max = sb("h_neg_max", [P, 1])
        row_sum = sb("h_row_sum", [P, 1])
        row_inv = sb("h_row_inv", [P, 1])
        agg_diag = sb("h_agg_diag", [P, P])
        aggT = sb("h_aggT", [P, EDGES])
        edge_table = sb("h_edge_table", [P, EDGES, 4])
        below = sb("h_below", [P, EDGES])
        above = sb("h_above", [P, EDGES])
        he = sb("h_he", [P, EDGES])
        z_edge = sb("h_z_edge", [P, P])
        se_all = sb("h_se_all", [P, 2, EDGES])
        max2 = sb("h_max2", [P, 2 * NT])
        sum2 = sb("h_sum2", [P, 2 * NT])
        inv2 = sb("h_inv2", [P, 2 * NT])
        coef_rows = sb("h_coef_rows", [P, NT, 2, EDGES])
        coef_rest = sb("h_coef_rest", [P, N])
        coef = sb("h_coef", [P, 3, N], BF16)
        edge_now = [sb(f"h_edge_now{k}", [P, 4]) for k in range(UNROLL)]
        pool_waiter = sb("h_pool_waiter", [P, 1])
        diff = [sb(f"h_diff{k}", [P, N]) for k in range(2)]
        gate = [sb(f"h_gate{k}", [P, N]) for k in range(2)]
        shifted = [sb(f"h_shifted{k}", [P, N]) for k in range(2)]
        expv = [sb(f"h_expv{k}", [P, N]) for k in range(2)]
        reluv = [sb(f"h_reluv{k}", [P, N]) for k in range(2)]
        weighted = [sb(f"h_weighted{k}", [P, N]) for k in range(2)]
        mean = sb("h_mean", [P, 2 * NT])
        var = sb("h_var", [P, 2 * NT])
        rstd = sb("h_rstd", [P, 2 * NT])
        minus_half = sb("h_minus_half", [P, 2 * NT])
        ps_c = [ctx.enter_context(nc.psum_tensor(f"h_ps_c{k}", [P, N], F32)) for k in range(2)]
        ps_g = ctx.enter_context(nc.psum_tensor("h_ps_g", [P, N], F32))
        ps_m = ctx.enter_context(nc.psum_tensor("h_ps_m", [P, N], F32))

        def column(v):
            return v.rearrange("(c o) -> c o", o=1)

        setup = events(bank, "h_w_loaded h_adj_loaded h_zeroed h_ident_ready h_w_zeroed h_ones_ready h_half_ready "
                                "h_HT_ready h_deg_ready h_step")
        with nc.Block() as block:
            e = setup
            WEIGHTS = 16 * 14

            @block.sync
            def _(sp):
                sp.wait_ge(e["h_w_zeroed"], 2)
                for k in range(2):
                    half = slice(k * C, (k + 1) * C)
                    sp.dma_start(W_diag[half, half], io["L0_gnn_W"]).then_inc(e["h_w_loaded"], 16)
                    sp.dma_start(Wind_diag[half, half], io["L0_gnn_W_ind"]).then_inc(e["h_w_loaded"], 16)
                    sp.dma_start(fcW[half, :], io["L0_gnn_fcW"]).then_inc(e["h_w_loaded"], 16)
                    for i, name in enumerate(("L0_gnn_a_node", "L0_gnn_a_gn", "L0_gnn_a_ge")):
                        sp.dma_start(vectors[half, i:i + 1], column(io[name])).then_inc(e["h_w_loaded"], 16)
                sp.dma_start(fcb[:, :], column(io["L0_gnn_fcb"])).then_inc(e["h_w_loaded"], 16)
                sp.dma_start(av[:, :], column(io["L0_gnn_av"])).then_inc(e["h_w_loaded"], 16)
                for k in range(2):
                    sp.dma_start(H_rows[:, :, k, :], io["L0_gnn_H"].rearrange("(t p) e -> p t e", p=P)).then_inc(e["h_adj_loaded"], 16)
                sp.dma_start(adjT[:, :, :], adjT_dram.rearrange("(t p) n -> p t n", p=P)).then_inc(e["h_adj_loaded"], 16)

            @block.gpsimd
            def _(pool):
                nc.gpsimd.memset(W_diag[:, :], 0.0).then_inc(e["h_w_zeroed"], 1)
                nc.gpsimd.memset(Wind_diag[:, :], 0.0).then_inc(e["h_w_zeroed"], 1)
                make_identity(pool, ident, e["h_zeroed"], e["h_ident_ready"], 0)
                nc.gpsimd.memset(minus_half[:, :], -0.5).then_inc(e["h_half_ready"], 1)
                nc.gpsimd.memset(agg_diag[:, :], 0.0).then_inc(e["h_half_ready"], 1)
                nc.gpsimd.memset(edge_table[:, :, :], 0.0).then_inc(e["h_half_ready"], 1)

            @block.tensor
            def _(pe):
                pe.wait_ge(e["h_ident_ready"], 1)
                pe.wait_ge(e["h_adj_loaded"], 48)
                for t in range(NT):
                    mm = nc.tensor.transpose(ps_m[:, t * P:(t + 1) * P], H_rows[:, t, :, :].rearrange("p k e -> p (k e)"), ident[:, :])
                mm.then_inc(e["h_HT_ready"], 1)
                pe.wait_ge(e["h_ones_ready"], 1)
                for m in range(2):
                    cols = slice(m * HN, (m + 1) * HN)
                    for t in range(NT):
                        mm = nc.tensor.matmul(ps_g[:, cols], ones[:, :], adjT[:, t, cols], start=(t == 0), stop=(t == NT - 1))
                mm.then_inc(e["h_deg_ready"], 1)

            @block.vector
            def _(dve):
                done = 0

                def link(ins):
                    nonlocal done
                    done += 1
                    ins.then_inc(e["h_step"], 1)
                    dve.wait_ge(e["h_step"], done)

                nc.vector.memset(ones[:, :], 1.0).then_inc(e["h_ones_ready"], 1)
                link(nc.vector.memset(av_pair[:, :, :, :], 0.0))
                link(nc.vector.memset(spread3[:, :, :], 0.0))
                dve.wait_ge(e["h_ones_ready"], 1)
                dve.wait_ge(e["h_w_loaded"], WEIGHTS)
                link(nc.vector.tensor_scalar(vectors[:, 1:3], vectors[:, 1:3], 0.5, None, ALU.mult))
                for i in range(3):
                    for k in range(2):
                        half = slice(k * C, (k + 1) * C)
                        nc.vector.tensor_scalar(spread3[half, i, half], ones[half, 0:C], vectors[half, i:i + 1], None, ALU.mult)
                link(nc.vector.tensor_scalar(av_half[:, :], av[:, :], 0.5, None, ALU.mult))
                nc.vector.tensor_scalar(av_all[:, :], ones[:, :], av[:, :], None, ALU.mult)
                for k in range(2):
                    half = slice(k * C, (k + 1) * C)
                    nc.vector.tensor_scalar(av_pair[:, 0, k, half], ones[:, 0:C], av_half[:, :], -1.0, ALU.mult, ALU.mult)
                    nc.vector.tensor_scalar(av_pair[:, 1, k, half], ones[:, 0:C], av_half[:, :], None, ALU.mult)
                dve.wait_ge(e["h_ident_ready"], 1)
                for k in range(2):
                    nc.vector.tensor_copy(pick[:, :, k * C:(k + 1) * C],
                                          ident[:, k * EDGES:(k + 1) * EDGES].unsqueeze(2).broadcast_to([P, EDGES, C]))
                dve.wait_ge(e["h_adj_loaded"], 48)
                link(nc.vector.tensor_scalar(mask_rows[:, :, :], H_rows[:, :, 0, :], 0.0, None, ALU.is_gt))
                link(nc.vector.tensor_scalar(fence_rows[:, :, :], mask_rows[:, :, :], -1.0, -NEG, ALU.add, ALU.mult))
                dve.wait_ge(e["h_HT_ready"], 1)
                link(nc.vector.tensor_scalar(maskT[:, :], ps_m[:, :], 0.0, None, ALU.is_gt))
                link(nc.vector.tensor_scalar(fenceT[:, :], maskT[:, :], -1.0, -NEG, ALU.add, ALU.mult))
                dve.wait_ge(e["h_deg_ready"], 1)
                link(nc.vector.tensor_scalar(inv_degree[:, :], ps_g[:, :], 1.0, None, ALU.max))
                link(nc.vector.reciprocal(inv_degree[:, :], inv_degree[:, :]))
        nc.all_engine_barrier(sems_to_clear=numbers(setup))

        e = events(bank, "h_x_loaded h_xT_ready h_xT_copied h_hT_ready h_hT_copied h_rows_ready h_rows_copied "
                            "h_irows_ready h_irows_copied h_s_ready h_s_copied h_a_masked h_a_exp h_a_inv h_aT_ready "
                            "h_aT_copied h_agg_ready h_agg_scaled h_aggT_ready h_aggT_copied h_gateh_ready h_gateh_copied "
                            "h_gatee_ready h_gatee_copied h_he_below h_he_exp h_he_ready h_z_ready h_z_tanh h_se_ready "
                            "h_se_copied h_c_shifted h_c_exp h_c_ready h_cT_ready h_c_high h_c_parts h_ind_ready h_ind_copied "
                            "h_half_made h_chain")
        loop = events(bank, "h_edge_copied h_diff_ready h_turn h_gate_ready h_shift_ready h_exp_ready h_relu_ready "
                               "h_f_ready h_w_ready h_spread_ready h_added")
        post = events(bank, "h_g_ready h_za_ready h_za_tanh h_zb_ready h_zb_tanh h_d_ready h_d_tanh h_o_ready "
                               "h_oT_ready h_norm h_var_ready h_rstd_ready h_y_done h_stored")
        x_pairs = x_in.rearrange("(q k) (t p) c -> q k p t c", k=2, p=P)
        y_pairs = x_out.rearrange("(q k) (t p) c -> q k p t c", k=2, p=P)

        with nc.Fori(0, PAIRS) as pair:
            with nc.Block() as block:

                @block.sync
                def _(sp):
                    for k in range(2):
                        sp.dma_start(x_rows[:, :, k, :], x_pairs[pair, k]).then_inc(e["h_x_loaded"], 16)
                    sp.wait_ge(e["h_x_loaded"], 32)

                @block.tensor
                def _(pe):
                    pe.wait_ge(e["h_x_loaded"], 32)
                    for t in range(NT):
                        mm = nc.tensor.transpose(ps_m[:, t * P:(t + 1) * P], x_rows[:, t, :, :].rearrange("p k c -> p (k c)"), ident[:, :])
                    mm.then_inc(e["h_xT_ready"], 1)
                    pe.wait_ge(e["h_xT_copied"], 1)
                    for m in range(2):
                        cols = slice(m * HN, (m + 1) * HN)
                        mm = nc.tensor.matmul(ps_c[0][:, cols], W_diag[:, :], xT[:, cols], start=True, stop=True)
                    mm.then_inc(e["h_hT_ready"], 1)
                    for t in range(NT):
                        mm = nc.tensor.matmul(ps_c[1][:, t * P:(t + 1) * P], xT[:, t * P:(t + 1) * P], W_diag[:, :], start=True, stop=True)
                    mm.then_inc(e["h_rows_ready"], 1)
                    for t in range(NT):
                        mm = nc.tensor.matmul(ps_g[:, t * P:(t + 1) * P], xT[:, t * P:(t + 1) * P], Wind_diag[:, :], start=True, stop=True)
                    mm.then_inc(e["h_irows_ready"], 1)
                    pe.wait_ge(e["h_hT_copied"], 1)
                    for m in range(2):
                        cols = slice(m * HN, (m + 1) * HN)
                        mm = nc.tensor.matmul(ps_m[:, cols], spread3[:, 0, :], hT[:, cols], start=True, stop=True)
                    mm.then_inc(e["h_s_ready"], 1)
                    for m in range(2):
                        cols = slice(m * HN, (m + 1) * HN)
                        mm = nc.tensor.matmul(ps_c[0][:, cols], spread3[:, 1, :], hT[:, cols], start=True, stop=True)
                    mm.then_inc(e["h_gateh_ready"], 1)
                    pe.wait_ge(e["h_irows_copied"], 1)
                    for m in range(2):
                        cols = slice(m * HN, (m + 1) * HN)
                        for t in range(NT):
                            mm = nc.tensor.matmul(ps_g[:, cols], ind_rows[:, t, :], adjT[:, t, cols], start=(t == 0), stop=(t == NT - 1))
                    mm.then_inc(e["h_ind_ready"], 1)
                    pe.wait_ge(e["h_a_exp"], 1)
                    pe.wait_ge(e["h_rows_copied"], 1)
                    for t in range(NT):
                        mm = nc.tensor.transpose(ps_c[1][:, t * P:(t + 1) * P], logits[:, t * P:(t + 1) * P], ident[:, :])
                    mm.then_inc(e["h_aT_ready"], 1)
                    pe.wait_ge(e["h_aT_copied"], 1)
                    for t in range(NT):
                        mm = nc.tensor.matmul(ps_m[:, 0:P], alphaT[:, t, :], h_rows[:, t, :], start=(t == 0), stop=(t == NT - 1))
                    mm.then_inc(e["h_agg_ready"], 1)
                    pe.wait_ge(e["h_agg_scaled"], 2)
                    nc.tensor.transpose(ps_c[1][:, 0:P], agg_diag[:, :], ident[:, :]).then_inc(e["h_aggT_ready"], 1)
                    pe.wait_ge(e["h_aggT_copied"], 2)
                    nc.tensor.matmul(ps_m[:, 0:EDGES], spread3[:, 2, :], aggT[:, :], start=True, stop=True).then_inc(e["h_gatee_ready"], 1)
                    pe.wait_ge(e["h_he_ready"], 1)
                    for k in range(2):
                        half = slice(k * C, (k + 1) * C)
                        mm = nc.tensor.matmul(ps_c[1][:, k * HN:k * HN + EDGES], fcW[half, :], he[half, :], start=True, stop=True)
                    mm.then_inc(e["h_z_ready"], 1)
                    pe.wait_ge(e["h_z_tanh"], 1)
                    pe.wait_ge(e["h_gatee_copied"], 1)
                    nc.tensor.matmul(ps_m[:, 0:P], av_all[:, :], z_edge[:, :], start=True, stop=True).then_inc(e["h_se_ready"], 1)
                    pe.wait_ge(e["h_c_ready"], 1)
                    for t in range(NT):
                        mm = nc.tensor.transpose(ps_c[1][:, t * P:(t + 1) * P], coef_rows[:, t, :, :].rearrange("p k e -> p (k e)"), ident[:, :])
                    mm.then_inc(e["h_cT_ready"], 1)

                @block.scalar
                def _(act):
                    act.wait_ge(e["h_xT_ready"], 1)
                    nc.scalar.activation(xT[:, :], ps_m[:, :], ACT.Copy).then_inc(e["h_xT_copied"], 1)
                    act.wait_ge(e["h_rows_ready"], 1)
                    nc.scalar.activation(h_rows[:, :, :], ps_c[1][:, :].rearrange("p (t c) -> p t c", c=P), ACT.Copy).then_inc(e["h_rows_copied"], 1)
                    act.wait_ge(e["h_irows_ready"], 1)
                    nc.scalar.activation(ind_rows[:, :, :], ps_g[:, :].rearrange("p (t c) -> p t c", c=P), ACT.Copy).then_inc(e["h_irows_copied"], 1)
                    act.wait_ge(e["h_s_ready"], 1)
                    nc.scalar.activation(logits[:, :], ps_m[:, :], ACT.Copy).then_inc(e["h_s_copied"], 1)
                    act.wait_ge(e["h_gateh_ready"], 1)
                    nc.scalar.activation(gate_h[:, :], ps_c[0][:, :], ACT.Copy).then_inc(e["h_gateh_copied"], 1)
                    act.wait_ge(e["h_a_masked"], 1)
                    nc.scalar.activation(logits[:, :], logits[:, :], ACT.Exp, bias=neg_max[:, :], accum_out=row_sum[:, :]).then_inc(e["h_a_exp"], 1)
                    act.wait_ge(e["h_aT_ready"], 1)
                    nc.scalar.activation(alphaT[:, :, :], ps_c[1][:, :].rearrange("p (t c) -> p t c", c=P), ACT.Copy).then_inc(e["h_aT_copied"], 1)
                    act.wait_ge(e["h_he_below"], 1)
                    nc.scalar.activation(below[:, :], below[:, :], ACT.Exp).then_inc(e["h_he_exp"], 1)
                    act.wait_ge(e["h_gatee_ready"], 1)
                    nc.scalar.activation(edge_table[:, :, 0], ps_m[:, 0:EDGES], ACT.Copy).then_inc(e["h_gatee_copied"], 1)
                    act.wait_ge(e["h_z_ready"], 1)
                    nc.scalar.activation(z_edge[:, :].rearrange("p (k e) -> p k e", k=2), ps_c[1][:, :].rearrange("p (k e) -> p k e", k=2)[:, :, 0:EDGES], ACT.Tanh, bias=fcb[:, :]).then_inc(e["h_z_tanh"], 1)
                    act.wait_ge(e["h_se_ready"], 1)
                    nc.scalar.activation(se_all[:, :, :], ps_m[:, 0:P].rearrange("p (k e) -> p k e", k=2), ACT.Copy).then_inc(e["h_se_copied"], 1)
                    act.wait_ge(e["h_c_shifted"], 1)
                    nc.scalar.activation(coef_rows[:, :, :, :], coef_rows[:, :, :, :], ACT.Exp).then_inc(e["h_c_exp"], 1)
                    act.wait_ge(e["h_cT_ready"], 1)
                    nc.scalar.activation(coef[:, 0, :], ps_c[1][:, :], ACT.Copy).then_inc(e["h_c_high"], 1)

                @block.vector
                def _(dve):
                    done = 0

                    def link(ins):
                        nonlocal done
                        done += 1
                        ins.then_inc(e["h_chain"], 1)
                        dve.wait_ge(e["h_chain"], done)

                    dve.wait_ge(e["h_hT_ready"], 1)
                    nc.vector.tensor_copy(hT[:, :], ps_c[0][:, :]).then_inc(e["h_hT_copied"], 1)
                    dve.wait_ge(e["h_s_copied"], 1)
                    link(nc.vector.scalar_tensor_tensor(logits[:, :], logits[:, :], 0.2, logits[:, :], ALU.mult, ALU.max))
                    link(nc.vector.tensor_tensor(logits[:, :], logits[:, :], maskT[:, :], ALU.mult))
                    link(nc.vector.tensor_tensor(logits[:, :], logits[:, :], fenceT[:, :], ALU.add))
                    nc.vector.tensor_reduce(neg_max[:, :], logits[:, :], AX.X, ALU.max, negate=True).then_inc(e["h_a_masked"], 1)
                    dve.wait_ge(e["h_hT_copied"], 1)
                    nc.vector.tensor_scalar(half_hT[:, :], hT[:, :], 0.5, None, ALU.mult).then_inc(e["h_half_made"], 1)
                    dve.wait_ge(e["h_a_exp"], 1)
                    nc.vector.reciprocal(row_inv[:, :], row_sum[:, :]).then_inc(e["h_a_inv"], 1)
                    dve.wait_ge(e["h_ind_ready"], 1)
                    nc.vector.tensor_tensor(indT[:, :], ps_g[:, :], inv_degree[:, :], ALU.mult).then_inc(e["h_ind_copied"], 1)
                    dve.wait_ge(e["h_agg_ready"], 1)
                    dve.wait_ge(e["h_a_inv"], 1)
                    for k in range(2):
                        half = slice(k * C, (k + 1) * C)
                        nc.vector.tensor_scalar(agg_diag[half, half], ps_m[half, half], row_inv[half, :], None, ALU.mult).then_inc(e["h_agg_scaled"], 1)
                    dve.wait_ge(e["h_aggT_ready"], 1)
                    for k in range(2):
                        half = slice(k * C, (k + 1) * C)
                        nc.vector.tensor_copy(aggT[half, :], ps_c[1][half, half]).then_inc(e["h_aggT_copied"], 1)
                    dve.wait_ge(e["h_aggT_copied"], 2)
                    nc.vector.tensor_scalar(below[:, :], aggT[:, :], 0.0, None, ALU.min).then_inc(e["h_he_below"], 1)
                    link(nc.vector.tensor_scalar(above[:, :], aggT[:, :], 0.0, None, ALU.max))
                    link(nc.vector.tensor_copy(edge_table[:, :, 1], aggT[:, :]))
                    link(nc.vector.tensor_scalar(edge_table[:, :, 2], aggT[:, :], 0.5, None, ALU.mult))
                    dve.wait_ge(e["h_he_exp"], 1)
                    nc.vector.scalar_tensor_tensor(he[:, :], below[:, :], -1.0, above[:, :], ALU.add, ALU.add).then_inc(e["h_he_ready"], 1)
                    dve.wait_ge(e["h_se_copied"], 1)
                    rows = coef_rows[:, :, :, :]
                    for k in range(2):
                        link(nc.vector.tensor_tensor(coef_rows[:, :, k, :], mask_rows[:, :, :],
                                                     se_all[:, k, :].unsqueeze(1).broadcast_to([P, NT, EDGES]), ALU.mult))
                        link(nc.vector.tensor_tensor(coef_rows[:, :, k, :], coef_rows[:, :, k, :], fence_rows[:, :, :], ALU.add))
                    flat = rows.rearrange("p t k e -> p (t k) e")
                    link(nc.vector.tensor_reduce(max2[:, :], flat, AX.X, ALU.max))
                    nc.vector.tensor_tensor(flat, flat, max2[:, :].unsqueeze(2).broadcast_to([P, 2 * NT, EDGES]), ALU.subtract).then_inc(e["h_c_shifted"], 1)
                    dve.wait_ge(e["h_c_exp"], 1)
                    link(nc.vector.tensor_reduce(sum2[:, :], flat, AX.X, ALU.add))
                    link(nc.vector.reciprocal(inv2[:, :], sum2[:, :]))
                    nc.vector.tensor_tensor(flat, flat, inv2[:, :].unsqueeze(2).broadcast_to([P, 2 * NT, EDGES]), ALU.mult).then_inc(e["h_c_ready"], 1)
                    dve.wait_ge(e["h_c_high"], 1)
                    link(nc.vector.tensor_tensor(coef_rest[:, :], ps_c[1][:, :], coef[:, 0, :], ALU.subtract))
                    link(nc.vector.tensor_copy(coef[:, 1, :], coef_rest[:, :]))
                    link(nc.vector.tensor_tensor(coef[:, 2, :], coef_rest[:, :], coef[:, 1, :], ALU.subtract))
            nc.all_engine_barrier(sems_to_clear=numbers(e))

            with nc.Block() as block:
                f = loop

                def rounds(eng, step):
                    for j in range(UNROLL):
                        step(j, j)
                    with eng.Fori(1, EDGES // UNROLL - 1) as turn:
                        for j in range(UNROLL):
                            step(UNROLL * turn + j, j)
                    for j in range(UNROLL):
                        step(EDGES - UNROLL + j, j)

                def past(edge, least):
                    return not isinstance(edge, int) or edge >= least

                @block.gpsimd
                def _(pool):
                    nc.gpsimd.tensor_tensor(pool_waiter[:, :], ident[:, 0:1], ident[:, 0:1], ALU.add).then_inc(f["h_turn"], 1)

                    def step(edge, j):
                        if past(edge, UNROLL):
                            pool.wait_ge(f["h_turn"], edge - UNROLL + 1)
                            pool.wait_ge(f["h_relu_ready"], edge - UNROLL + 1)
                            nc.gpsimd.tensor_tensor(pool_waiter[:, :], ident[:, 0:1], ident[:, 0:1], ALU.add).then_inc(f["h_turn"], 1)
                        nc.gpsimd.tensor_copy(edge_now[j][:, :], edge_table[:, edge, :]).then_inc(f["h_edge_copied"], 1)
                        pool.wait_ge(f["h_edge_copied"], edge + 1)
                        if past(edge, 2):
                            pool.wait_ge(f["h_shift_ready"], edge - 1)
                        nc.gpsimd.tensor_tensor(diff[j % 2][:, :], half_hT[:, :], edge_now[j][:, 2:3].broadcast_to([P, N]),
                                                ALU.subtract).then_inc(f["h_diff_ready"], 1)
                    rounds(pool, step)

                @block.scalar
                def _(act):
                    def make_gate(edge, j):
                        act.wait_ge(f["h_edge_copied"], edge + 1)
                        if past(edge, 2):
                            act.wait_ge(f["h_shift_ready"], edge - 1)
                        nc.scalar.activation(gate[j % 2][:, :], gate_h[:, :], ACT.Tanh, bias=edge_now[j % UNROLL][:, 0:1]).then_inc(f["h_gate_ready"], 1)

                    def functions(edge, j):
                        act.wait_ge(f["h_shift_ready"], edge + 1)
                        if past(edge, 2):
                            act.wait_ge(f["h_f_ready"], edge - 1)
                        agg = edge_now[j % UNROLL][:, 1:2]
                        nc.scalar.activation(expv[j % 2][:, :], shifted[j % 2][:, :], ACT.Exp, bias=agg).then_inc(f["h_exp_ready"], 1)
                        nc.scalar.activation(reluv[j % 2][:, :], shifted[j % 2][:, :], ACT.Relu, bias=agg).then_inc(f["h_relu_ready"], 1)

                    def step(edge, j):
                        if not isinstance(edge, int) or edge + 2 < EDGES:
                            make_gate(edge + 2, j + 2)
                        if not isinstance(edge, int) or edge + 1 < EDGES:
                            functions(edge + 1, j + 1)

                    make_gate(0, 0)
                    make_gate(1, 1)
                    functions(0, 0)
                    rounds(act, step)

                @block.vector
                def _(dve):
                    def shift(edge, j):
                        dve.wait_ge(f["h_diff_ready"], edge + 1)
                        dve.wait_ge(f["h_gate_ready"], edge + 1)
                        if past(edge, 2):
                            dve.wait_ge(f["h_relu_ready"], edge - 1)
                        nc.vector.scalar_tensor_tensor(shifted[j % 2][:, :], gate[j % 2][:, :], 1.0, diff[j % 2][:, :],
                                                       ALU.add, ALU.mult).then_inc(f["h_shift_ready"], 1)

                    def step(edge, j):
                        if not isinstance(edge, int) or edge + 1 < EDGES:
                            shift(edge + 1, j + 1)
                        dve.wait_ge(f["h_relu_ready"], edge + 1)
                        nc.vector.scalar_tensor_tensor(reluv[j % 2][:, :], expv[j % 2][:, :], 1.0, reluv[j % 2][:, :],
                                                       ALU.min, ALU.add).then_inc(f["h_w_ready"], 1)
                        dve.wait_ge(f["h_w_ready"], edge + 1)
                        dve.wait_ge(f["h_spread_ready"], edge + 1)
                        if past(edge, 2):
                            dve.wait_ge(f["h_added"], edge - 1)
                        nc.vector.tensor_tensor(weighted[j % 2][:, :], reluv[j % 2][:, :], ps_c[j % 2][:, :], ALU.mult).then_inc(f["h_f_ready"], 1)

                    shift(0, 0)
                    rounds(dve, step)

                @block.tensor
                def _(pe):
                    def spread(edge, j):
                        for m in range(2):
                            cols = slice(m * HN, (m + 1) * HN)
                            for part in range(3):
                                mm = nc.tensor.matmul(ps_c[j % 2][:, cols], pick[:, edge, :], coef[:, part, cols],
                                                      start=(part == 0), stop=(part == 2))
                        mm.then_inc(f["h_spread_ready"], 1)

                    def step(edge, j):
                        pe.wait_ge(f["h_f_ready"], edge + 1)
                        first = isinstance(edge, int) and edge == 0
                        last = isinstance(edge, int) and edge == EDGES - 1
                        for m in range(2):
                            cols = slice(m * HN, (m + 1) * HN)
                            mm = nc.tensor.matmul(ps_g[:, cols], ident[:, :], weighted[j % 2][:, cols], start=first, stop=last)
                        mm.then_inc(f["h_added"], 1)
                        if not isinstance(edge, int) or edge + 2 < EDGES:
                            spread(edge + 2, j + 2)

                    spread(0, 0)
                    spread(1, 1)
                    rounds(pe, step)
            nc.all_engine_barrier(sems_to_clear=numbers(loop))

            with nc.Block() as block:
                q = post
                gT, outT, d_tanh = diff[0], diff[1], gate[0]
                zt = [[shifted[0], shifted[1]], [expv[0], expv[1]]]
                y = weighted[0][:, :].rearrange("p (t c) -> p t c", c=C)
                sq = weighted[1][:, :].rearrange("p (t c) -> p t c", c=C)

                @block.vector
                def _(dve):
                    nc.vector.tensor_scalar(gT[:, :], ps_g[:, :], -1.0, None, ALU.add).then_inc(q["h_g_ready"], 1)
                    dve.wait_ge(q["h_g_ready"], 1)
                    nc.vector.tensor_tensor(outT[:, :], gT[:, :], indT[:, :], ALU.subtract).then_inc(q["h_g_ready"], 1)
                    done = 0

                    def link(ins):
                        nonlocal done
                        done += 1
                        ins.then_inc(q["h_norm"], 1)
                        dve.wait_ge(q["h_norm"], done)

                    dve.wait_ge(q["h_d_tanh"], 1)
                    dve.wait_ge(q["h_g_ready"], 2)
                    link(nc.vector.scalar_tensor_tensor(outT[:, :], d_tanh[:, :], 1.0, outT[:, :], ALU.add, ALU.mult))
                    nc.vector.scalar_tensor_tensor(outT[:, :], outT[:, :], 0.5, indT[:, :], ALU.mult, ALU.add).then_inc(q["h_o_ready"], 1)
                    dve.wait_ge(q["h_oT_ready"], 1)
                    link(nc.vector.tensor_tensor(y, ps_c[0][:, :].rearrange("p (t c) -> p t c", c=C),
                                                 x_rows[:, :, :, :].rearrange("p t k c -> p (t k) c"), ALU.add))
                    layer_norm_rows(nc, dve, link, y, sq, mean[:, :], var[:, :], rstd[:, :], q["h_var_ready"], q["h_rstd_ready"], q["h_y_done"])

                @block.gpsimd
                def _(pool):
                    pool.wait_ge(q["h_var_ready"], 1)
                    nc.gpsimd.tensor_tensor(rstd[:, :], var[:, :], minus_half[:, :], ALU.pow).then_inc(q["h_rstd_ready"], 1)

                @block.tensor
                def _(pe):
                    for k in range(2):
                        half = slice(k * C, (k + 1) * C)
                        if k == 1:
                            pe.wait_ge(q["h_za_tanh"], 1)
                        for m in range(2):
                            cols = slice(m * HN, (m + 1) * HN)
                            mm = nc.tensor.matmul(ps_c[0][:, cols], fcW[half, :], indT[half, cols], start=True, stop=True)
                        mm.then_inc(q["h_za_ready"], 1)
                        if k == 0:
                            pe.wait_ge(q["h_g_ready"], 1)
                        else:
                            pe.wait_ge(q["h_zb_tanh"], 1)
                        for m in range(2):
                            cols = slice(m * HN, (m + 1) * HN)
                            mm = nc.tensor.matmul(ps_c[1][:, cols], fcW[half, :], gT[half, cols], start=True, stop=True)
                        mm.then_inc(q["h_zb_ready"], 1)
                    pe.wait_ge(q["h_za_tanh"], 2)
                    pe.wait_ge(q["h_zb_tanh"], 2)
                    for m in range(2):
                        cols = slice(m * HN, (m + 1) * HN)
                        for i in range(4):
                            kind, k = i // 2, i % 2
                            mm = nc.tensor.matmul(ps_m[:, cols], av_pair[:, kind, k, :], zt[kind][k][:, cols], start=(i == 0), stop=(i == 3))
                    mm.then_inc(q["h_d_ready"], 1)
                    pe.wait_ge(q["h_o_ready"], 1)
                    for t in range(NT):
                        mm = nc.tensor.transpose(ps_c[0][:, t * P:(t + 1) * P], outT[:, t * P:(t + 1) * P], ident[:, :])
                    mm.then_inc(q["h_oT_ready"], 1)

                @block.scalar
                def _(act):
                    for k in range(2):
                        act.wait_ge(q["h_za_ready"], k + 1)
                        nc.scalar.activation(zt[0][k][:, :], ps_c[0][:, :], ACT.Tanh, bias=fcb[:, :]).then_inc(q["h_za_tanh"], 1)
                        act.wait_ge(q["h_zb_ready"], k + 1)
                        nc.scalar.activation(zt[1][k][:, :], ps_c[1][:, :], ACT.Tanh, bias=fcb[:, :]).then_inc(q["h_zb_tanh"], 1)
                    act.wait_ge(q["h_d_ready"], 1)
                    nc.scalar.activation(d_tanh[:, :], ps_m[:, :], ACT.Tanh).then_inc(q["h_d_tanh"], 1)

                @block.sync
                def _(sp):
                    sp.wait_ge(q["h_y_done"], 1)
                    for k in range(2):
                        sp.dma_start(y_pairs[pair, k], weighted[0][:, :].rearrange("p (t k c) -> p t k c", k=2, c=C)[:, :, k, :]).then_inc(q["h_stored"], 16)
                    sp.wait_ge(q["h_stored"], 32)
            nc.all_engine_barrier(sems_to_clear=numbers(post))


def multi_head_gat(nc, bank, io, x_in, x_out):
    ctx = ExitStack()
    with ctx:
        def sb(name, shape, dt=F32):
            return ctx.enter_context(nc.sbuf_tensor(name, shape, dt))

        def pb(name, shape):
            return ctx.enter_context(nc.psum_tensor(name, shape, F32))

        ident = sb("g_ident", [P, P])
        ident_bf = sb("g_ident_bf", [P, P], BF16)
        ident2 = sb("g_ident2", [P, C])
        graph = sb("g_graph", [P, NT, N])
        fence = sb("g_fence", [P, NT, N], BF16)
        A_table = sb("g_A_table", [P, HEADS, 2, P], F32R)
        W_table = sb("g_W_table", [P, HEADS, 2 * P + 1])
        b_out_row = sb("g_b_out_row", [P, C])
        A_cur = [sb(f"g_A_cur{k}", [P, 2, P], F32R) for k in range(2)]
        W_cur = [sb(f"g_W_cur{k}", [P, 2 * P + 1]) for k in range(2)]
        x_rows = sb("g_x_rows", [P, NT, 2 * C])
        x_again = sb("g_x_again", [P, NT, C])
        moving_hi = sb("g_moving_hi", [P, N], F32R)
        moving_lo = sb("g_moving_lo", [P, N], F32R)
        moving_hl = sb("g_moving_hl", [P, N], F32R)
        value_hl = sb("g_value_hl", [P, NT, P], F32R)
        query = [sb(f"g_query{k}", [P, N], F32R) for k in range(2)]
        other_hi = sb("g_other_hi", [P, N], F32R)
        other_lo = sb("g_other_lo", [P, N], F32R)
        other_hl = sb("g_other_hl", [P, N], F32R)
        other_value = sb("g_other_value", [P, NT, P], F32R)
        SLOTS = 4
        tile = [sb(f"g_tile{k}", [P, N]) for k in range(SLOTS)]
        row_max = [sb(f"g_row_max{k}", [P, 1]) for k in range(SLOTS)]
        neg_max = [sb(f"g_neg_max{k}", [P, 1]) for k in range(SLOTS)]
        waiter = sb("g_waiter", [P, 1])
        pool_waiter = sb("g_pool_waiter", [P, 1])
        row_sum = sb("g_row_sum", [P, NT])
        row_inv = sb("g_row_inv", [P, NT])
        pt_hi = [sb(f"g_pt_hi{k}", [P, NT, HN], F32R) for k in range(2)]
        pt_lo = [sb(f"g_pt_lo{k}", [P, NT, HN], F32R) for k in range(2)]
        mixed = sb("g_mixed", [P, HN])
        mixed_n = sb("g_mixed_n", [P, HN])
        cat = sb("g_cat", [P, HN])
        hidden = sb("g_hidden", [P, N])
        y = sb("g_y", [P, NT, C])
        sq = x_again
        mean = sb("g_mean", [P, NT])
        var = sb("g_var", [P, NT])
        rstd = sb("g_rstd", [P, NT])
        minus_half = sb("g_minus_half", [P, NT])

        ps_s = [pb(f"g_ps_s{k}", [P, N]) for k in range(2)]
        ps_t = [pb(f"g_ps_t{k}", [P, HN]) for k in range(2)]
        ps_u = pb("g_ps_u", [P, HN])
        ps_x = pb("g_ps_x", [P, HN])

        w_head = tile[2][:, :].rearrange("p (h d) -> p h d", d=HC)
        setup = events(bank, "g_loaded g_zeroed g_ident_ready g_ident2_ready g_graph_zero "
                                "g_fence_ready g_graph_ready g_wT_ready g_wT_copied g_A_ready "
                                "g_A_high g_A_rest g_W_packed g_half_ready")
        with nc.Block() as block:
            e = setup

            @block.sync
            def _(sp):
                sp.dma_start(graph[:, :, :], io["adj"].rearrange("(t p) m -> p t m", p=P)).then_inc(e["g_loaded"], 16)
                for k in range(2):
                    half = slice(k * C, (k + 1) * C)
                    sp.dma_start(w_head[half, :, :], io["L1_gnn_Wh"].rearrange("h c d -> c h d")).then_inc(e["g_loaded"], 16)
                    sp.dma_start(W_table[:, :, P + k * C:P + (k + 1) * C],
                                 io["L1_gnn_W_out"].rearrange("(h d) c -> d h c", d=HC)).then_inc(e["g_loaded"], 16)
                sp.dma_start(W_table[:, :, 2 * P:2 * P + 1],
                             io["L1_gnn_bh"].rearrange("h (d o) -> d h o", o=1),
                             allow_slow_non_contiguous=True).then_inc(e["g_loaded"], 16)
                sp.dma_start(b_out_row[:, :], io["L1_gnn_b_out"].partition_broadcast(P)).then_inc(e["g_loaded"], 16)

            @block.gpsimd
            def _(pool):
                make_identity(pool, ident, e["g_zeroed"], e["g_ident_ready"], 0)
                make_identity(pool, ident_bf, e["g_zeroed"], e["g_ident_ready"], 1)
                nc.gpsimd.memset(minus_half[:, :], -0.5).then_inc(e["g_half_ready"], 1)

            @block.vector
            def _(dve):
                dve.wait_ge(e["g_ident_ready"], 2)
                nc.vector.tensor_tensor(ident2[:, :], ident[:, 0:C], ident[:, C:2 * C], ALU.add).then_inc(e["g_ident2_ready"], 1)
                dve.wait_ge(e["g_loaded"], 16 * 7)
                for t in range(NT):
                    nc.vector.tensor_scalar(tile[t % 2][:, :], graph[:, t, :], 0.0, None, ALU.is_equal).then_inc(e["g_graph_zero"], 1)
                    dve.wait_ge(e["g_graph_zero"], t + 1)
                    nc.vector.tensor_scalar(fence[:, t, :], tile[t % 2][:, :], MASKED, None, ALU.mult).then_inc(e["g_fence_ready"], 1)
                    nc.vector.tensor_tensor(graph[:, t, :], graph[:, t, :], tile[t % 2][:, :], ALU.add).then_inc(e["g_graph_ready"], 1)
                nc.vector.tensor_copy(W_table[:, :, 0:P], w_head).then_inc(e["g_W_packed"], 1)
                dve.wait_ge(e["g_wT_ready"], 1)
                nc.vector.tensor_copy(tile[0][:, :], ps_s[0][:, :]).then_inc(e["g_wT_copied"], 1)
                dve.wait_ge(e["g_A_ready"], 1)
                for h in range(HEADS):
                    nc.vector.tensor_copy(A_table[:, h, 0, :], ps_s[1][:, h * P:(h + 1) * P]).then_inc(e["g_A_high"], 1)
                    dve.wait_ge(e["g_A_high"], h + 1)
                    nc.vector.tensor_tensor(A_table[:, h, 1, :], ps_s[1][:, h * P:(h + 1) * P],
                                            A_table[:, h, 0, :].bitcast(F32), ALU.subtract).then_inc(e["g_A_rest"], 1)

            @block.tensor
            def _(pe):
                pe.wait_ge(e["g_loaded"], 16 * 7)
                pe.wait_ge(e["g_ident_ready"], 2)
                for h in range(HEADS):
                    mm = nc.tensor.transpose(ps_s[0][:, h * P:(h + 1) * P], w_head[:, h, :], ident[:, :])
                mm.then_inc(e["g_wT_ready"], 1)
                pe.wait_ge(e["g_wT_copied"], 1)
                for h in range(HEADS):
                    wT = tile[0][:, h * P:(h + 1) * P]
                    mm = nc.tensor.matmul(ps_s[1][:, h * P:(h + 1) * P], wT, wT, start=True, stop=True)
                mm.then_inc(e["g_A_ready"], 1)
        nc.all_engine_barrier(sems_to_clear=numbers(setup))

        names = ("g_x_loaded g_r_loaded g_xT_ready g_x_high g_x_rest g_o_stacked g_main_hi g_main_lo g_main_hl g_v_high g_v_rest "
                 "g_s_ready g_m_ready g_t_ready g_p_ready g_pt_ready g_hi_ready g_lo_ready g_u_ready "
                 "g_ut_ready g_ri_ready g_rb_ready g_un_ready g_cat_ready g_vb_ready g_v_ready g_hp_ready "
                 "g_hacc_ready g_y_ready g_yr_ready g_y2_ready g_wa_ready g_ww_ready g_turn "
                 "g_h_high g_h_rest g_hT_ready g_hT_copied g_o_ready g_o_used g_norm g_square g_var_ready g_rstd_ready "
                 "g_y_done g_stored")
        e = events(bank, names)
        AHEAD = 2
        NEXT = HEADS
        xin = x_in.rearrange("b (t p) c -> b p t c", p=P)
        xout = x_out.rearrange("b (t p) c -> b p t c", p=P)

        def is_out(h):
            return isinstance(h, str)

        def is_int(h, number):
            return isinstance(h, int) and h == number

        def load_x(sp, b):
            for k in range(2):
                sp.dma_start(x_rows[:, :, k * C:(k + 1) * C], xin[b]).then_inc(e["g_x_loaded"], 16)

        def transpose_x(half):
            for j in range(4):
                mm = nc.tensor.transpose(ps_x[:, j * P:(j + 1) * P], x_rows[:, 4 * half + j, :], ident[:, :])
            mm.then_inc(e["g_xT_ready"], 1)

        def x_high(act, half):
            act.wait_ge(e["g_xT_ready"], half + 1)
            nc.scalar.activation(other_hi[:, half * HN:(half + 1) * HN], ps_x[:, :], ACT.Copy).then_inc(e["g_x_high"], 1)

        def x_rest(dve, half):
            cols = slice(half * HN, (half + 1) * HN)
            dve.wait_ge(e["g_x_high"], half + 1)
            nc.vector.tensor_tensor(other_lo[:, cols], ps_x[:, :], other_hi[:, cols].bitcast(F32), ALU.subtract).then_inc(e["g_x_rest"], 1)

        def stack_other(pool, turn, prior, prior_count):
            pool.wait_ge(prior, prior_count)
            nc.gpsimd.tensor_copy(other_hl[0:C, :], other_hi[0:C, :].bitcast(F32)).then_inc(e["g_o_stacked"], 1)
            pool.wait_ge(e["g_o_stacked"], 2 * turn + 1)
            nc.gpsimd.tensor_copy(other_hl[C:P, :], other_lo[C:P, :].bitcast(F32)).then_inc(e["g_o_stacked"], 1)
            pool.wait_ge(e["g_o_stacked"], 2 * turn + 2)

        def query_product(k, half, moving):
            cols = slice(half * HN, (half + 1) * HN)
            nc.tensor.matmul(ps_x[:, :], A_cur[k][:, 0, :], moving[:, cols], start=True, stop=False)
            nc.tensor.matmul(ps_x[:, :], A_cur[k][:, 1, :], moving[:, cols], start=False, stop=True).then_inc(e["g_y_ready"], 1)

        def query_high(k, half):
            nc.scalar.activation(query[k][:, half * HN:(half + 1) * HN], ps_x[:, :], ACT.Copy).then_inc(e["g_yr_ready"], 1)

        def query_rest(k, half):
            cols = slice(half * HN, (half + 1) * HN)
            nc.vector.tensor_tensor(query[k][C:P, cols], ps_x[C:P, :], query[k][C:P, cols].bitcast(F32),
                                    ALU.subtract).then_inc(e["g_y2_ready"], 1)

        with nc.Block() as block:

            @block.sync
            def _(sp):
                load_x(sp, 0)

            @block.gpsimd
            def _(pool):
                nc.gpsimd.tensor_copy(A_cur[0][:, :, :], A_table[:, 0, :, :]).then_inc(e["g_wa_ready"], 1)
                pool.wait_ge(e["g_x_rest"], 2)
                stack_other(pool, 0, e["g_wa_ready"], 1)

            @block.tensor
            def _(pe):
                pe.wait_ge(e["g_x_loaded"], 32)
                transpose_x(0)
                pe.wait_ge(e["g_x_rest"], 1)
                transpose_x(1)
                pe.wait_ge(e["g_wa_ready"], 1)
                pe.wait_ge(e["g_o_stacked"], 2)
                query_product(0, 0, other_hl)
                pe.wait_ge(e["g_y2_ready"], 1)
                query_product(0, 1, other_hl)

            @block.scalar
            def _(act):
                for half in range(2):
                    x_high(act, half)
                for half in range(2):
                    act.wait_ge(e["g_y_ready"], half + 1)
                    query_high(0, half)

            @block.vector
            def _(dve):
                for half in range(2):
                    x_rest(dve, half)
                for half in range(2):
                    dve.wait_ge(e["g_yr_ready"], half + 1)
                    query_rest(0, half)
        nc.all_engine_barrier(sems_to_clear=numbers(e))

        def element(b, first=False, last=False):
            before = 0 if first else 1
            LATER = 2 + before

            def unit(h):
                return h + before if not isinstance(h, int) or h >= 2 else h

            OUT = 2
            END = unit(HEADS - 1)
            FINAL = END + 1
            def program(run, loop):
                run(0, 0, "head" if before else None, 1, -1)
                run(1, 1, "head", 2 if first else "out", 0)
                if not first:
                    run(OUT, "out", "head", 2, 1)
                run(LATER, 2, "head" if first else "out", 3, 1)
                with loop(0, (HEADS - 4) // 2) as pair:
                    run(2 * pair + 3 + before, 2 * pair + 3, "head", 2 * pair + 4, 2 * pair + 2, k=1, looped=True)
                    run(2 * pair + 4 + before, 2 * pair + 4, "head", 2 * pair + 5, 2 * pair + 3, k=0, looped=True)
                run(END, HEADS - 1, "head", None, HEADS - 2)

            def parity(h, k):
                return h % 2 if isinstance(h, int) else k

            with nc.Block() as block:

                @block.sync
                def _(sp):
                    if not first:
                        sp.dma_start(x_again[:, :, :], xin[b - 1]).then_inc(e["g_r_loaded"], 16)
                    if not last:
                        sp.wait_ge(e["g_v_rest"], 1)
                        load_x(sp, b + 1)
                    if not first:
                        sp.wait_ge(e["g_y_done"], 1)
                        sp.dma_start(xout[b - 1], y[:, :, :]).then_inc(e["g_stored"], 16)
                    if last:
                        sp.dma_start(x_again[:, :, :], xin[b]).then_inc(e["g_r_loaded"], 16)
                        sp.wait_ge(e["g_y_done"], 2)
                        sp.dma_start(xout[b], y[:, :, :]).then_inc(e["g_stored"], 16)
                    if not first:
                        sp.wait_ge(e["g_stored"], 32 if last else 16)

                @block.gpsimd
                def _(pool):
                    def wait_turn(number, signal, count):
                        pool.wait_ge(signal, count)
                        nc.gpsimd.tensor_tensor(pool_waiter[:, :], ident[:, 0:1], ident[:, 0:1], ALU.add).then_inc(e["g_turn"], 1)
                        pool.wait_ge(e["g_turn"], number)

                    def load_A(h, k):
                        nc.gpsimd.tensor_copy(A_cur[k][:, :, :], A_table[:, h, :, :]).then_inc(e["g_wa_ready"], 1)

                    def load_W(h, k):
                        nc.gpsimd.tensor_copy(W_cur[k][:, :], W_table[:, h, :]).then_inc(e["g_ww_ready"], 1)

                    def run(u, h, came, behind, h_before, k=0, looped=False):
                        k = parity(h, k) if not is_out(h) else None
                        for i in range(NT):
                            if i == 0 and not is_out(h) and (looped or 1 <= h):
                                if looped:
                                    wait_turn(2 * h - 5, e["g_y_ready"], 2 * h - 2)
                                elif h >= 2:
                                    pool.wait_ge(e["g_y_ready"], 2 * h - 2)
                                if looped or h + 1 < HEADS:
                                    load_A(h + 1, 1 - k)
                                elif not last:
                                    load_A(0, 1 - k)
                            if i == 3 and not is_out(h) and (looped or h >= 1):
                                done = 2 * h - 2 + 2 * before
                                if looped:
                                    wait_turn(2 * h - 4, e["g_hp_ready"], done)
                                elif done > 0:
                                    pool.wait_ge(e["g_hp_ready"], done)
                                load_W(h, k)
                            if i == 4 and is_out(behind):
                                pool.wait_ge(e["g_h_rest"], 1)
                                stack_other(pool, 0, e["g_ww_ready"], 2)

                    nc.gpsimd.tensor_copy(moving_hl[:, :], other_hl[:, :].bitcast(F32)).then_inc(e["g_main_hl"], 1)
                    load_A(1, 1)
                    load_W(0, 0)
                    program(run, pool.Fori)
                    if not last:
                        pool.wait_ge(e["g_x_rest"], 2)
                        stack_other(pool, before, e["g_ww_ready"], HEADS)
                    if not first:
                        pool.wait_ge(e["g_var_ready"], 1)
                        nc.gpsimd.tensor_tensor(rstd[:, :], var[:, :], minus_half[:, :], ALU.pow).then_inc(e["g_rstd_ready"], 1)
                    if last:
                        pool.wait_ge(e["g_h_rest"], 2)
                        stack_other(pool, 1, e["g_rstd_ready"], 1)
                        pool.wait_ge(e["g_var_ready"], 2)
                        nc.gpsimd.tensor_tensor(rstd[:, :], var[:, :], minus_half[:, :], ALU.pow).then_inc(e["g_rstd_ready"], 1)

                @block.tensor
                def _(pe):
                    def score(u, h, i, k):
                        n = 8 * u + i
                        if not isinstance(n, int) or n >= 2:
                            pe.wait_ge(e["g_m_ready"], n - 1)
                        if is_out(h):
                            queries, high, low = other_hl, other_hi, other_lo
                        else:
                            queries, high, low = query[k], moving_hi, moving_lo
                            if i % 4 == 0 and not (isinstance(h, int) and h == 0):
                                pe.wait_ge(e["g_y2_ready"], 2 * h - 1 + i // 4)
                        for m in range(2):
                            cols = slice(m * HN, (m + 1) * HN)
                            rows = slice(i * P, (i + 1) * P)
                            nc.tensor.matmul(ps_s[i % 2][:, cols], ident_bf[:, :], fence[:, i, cols], start=True, stop=False)
                            nc.tensor.matmul(ps_s[i % 2][:, cols], queries[:, rows], high[:, cols], start=False, stop=False)
                            mm = nc.tensor.matmul(ps_s[i % 2][:, cols], queries[:, rows], low[:, cols], start=False, stop=True)
                        mm.then_inc(e["g_s_ready"], 1)

                    def transpose(u, i):
                        n = 8 * u + i
                        pe.wait_ge(e["g_p_ready"], n + 1)
                        for a in range(2):
                            if not isinstance(n, int) or n >= 1:
                                pe.wait_ge(e["g_lo_ready"], 2 * n + a - 1)
                            for j in range(4):
                                m = 4 * a + j
                                mm = nc.tensor.transpose(ps_t[a][:, j * P:(j + 1) * P],
                                                         tile[i % SLOTS][:, m * P:(m + 1) * P], ident[:, :])
                            mm.then_inc(e["g_pt_ready"], 1)

                    def mix(u, h, half, chunk):
                        values = other_value if is_out(h) else value_hl
                        if chunk == 0:
                            pe.wait_ge(e["g_lo_ready"], 16 * u + 8 * half + 8)
                            if not (isinstance(u, int) and 2 * u + half + before == 0):
                                pe.wait_ge(e["g_ut_ready"], 2 * u + half + before)
                        for j in range(3 * chunk, min(3 * chunk + 3, NT)):
                            nc.tensor.matmul(ps_u[:, :], values[:, j, :], pt_hi[half][:, j, :], start=(j == 0), stop=False)
                            mm = nc.tensor.matmul(ps_u[:, :], values[:, j, :], pt_lo[half][:, j, :], start=False, stop=(j == NT - 1))
                        if chunk == 2:
                            mm.then_inc(e["g_u_ready"], 1)

                    def spread_inverse(u, half):
                        if u is not None:
                            pe.wait_ge(e["g_ri_ready"], 2 * u + half + 1)
                        for j in range(4):
                            i = 4 * half + j
                            mm = nc.tensor.matmul(ps_x[:, j * P:(j + 1) * P], row_inv[:, i:i + 1].broadcast_to([P, P]), ident[:, :],
                                                  start=True, stop=True)
                        mm.then_inc(e["g_rb_ready"], 1)

                    def project(h, half, k):
                        if not (isinstance(h, int) and h < 0):
                            pe.wait_ge(e["g_ww_ready"], h + 1)
                        pe.wait_ge(e["g_un_ready"], 2 * (h + before) + half + 1)
                        nc.tensor.matmul(ps_x[:, :], W_cur[k][:, 0:P], mixed_n[:, :], start=True, stop=True).then_inc(e["g_cat_ready"], 1)

                    def project_out(h, half, k):
                        pe.wait_ge(e["g_v_ready"], 2 * (h + before) + half + 1)
                        nc.tensor.matmul(ps_x[:, :], W_cur[k][:, P:2 * P], cat[:, :], start=True, stop=True).then_inc(e["g_hp_ready"], 1)

                    def out_rows(u, half):
                        pe.wait_ge(e["g_ut_ready"], 2 * u + half + 1 + before)
                        for j in range(4):
                            mm = nc.tensor.matmul(ps_x[:, j * C:(j + 1) * C], mixed[:, j * P:(j + 1) * P], ident2[:, :],
                                                  start=True, stop=True)
                        mm.then_inc(e["g_o_ready"], 1)

                    def transpose_hidden(half):
                        for j in range(4):
                            i = 4 * half + j
                            mm = nc.tensor.transpose(ps_x[:, j * P:(j + 1) * P], other_hl[:, i * P:(i + 1) * P].bitcast(F32), ident[:, :])
                        mm.then_inc(e["g_hT_ready"], 1)

                    def run(u, h, came, behind, h_before, k=0, looped=False):
                        k = parity(h, k) if not is_out(h) else 0
                        kb = (1 - k) if not is_out(h) and not is_int(h, 2) else 1
                        kn = (1 - k) if not is_out(h) else 0
                        q = 2 * (h_before + before)
                        start_of_element = isinstance(u, int) and u == 0
                        for i in range(NT):
                            transpose(u, i)
                            if i + AHEAD < NT:
                                score(u, h, i + AHEAD, k)
                            elif behind is not None:
                                score(u + 1, behind, i + AHEAD - NT, kn)
                            if i >= 5:
                                mix(u, h, 0, i - 5)
                            elif 1 <= i <= 3 and not start_of_element:
                                mix(u - 1, "out" if came == "out" else h_before, 1, i - 1)

                            if i == 0 and came == "head":
                                if u is not None and not start_of_element:
                                    if isinstance(q, int) and q == 0:
                                        pe.wait_ge(e["g_y2_ready"], 2)
                                    else:
                                        pe.wait_ge(e["g_hacc_ready"], q)
                                    if looped:
                                        if not first:
                                            pe.wait_ge(e["g_o_used"], 2)
                                spread_inverse(None if start_of_element else u - 1, 0)
                            if i == 0 and came == "out":
                                pe.wait_ge(e["g_hacc_ready"], q + 2)
                                out_rows(u - 1, 0)
                            if i == 1 and came == "head":
                                project(h_before, 0, kb)
                            if i == 2 and came == "head":
                                project_out(h_before, 0, kb)
                            if i == 3:
                                if came == "head":
                                    pe.wait_ge(e["g_hacc_ready"], q + 1)
                                elif came == "out":
                                    pe.wait_ge(e["g_o_used"], 1)
                                if is_out(behind):
                                    pe.wait_ge(e["g_o_stacked"], 2)
                                    transpose_hidden(0)
                                elif behind is not None:
                                    pe.wait_ge(e["g_wa_ready"], behind)
                                    if start_of_element:
                                        pe.wait_ge(e["g_main_hl"], 1)
                                    query_product(kn, 0, moving_hl)
                                elif not last:
                                    pe.wait_ge(e["g_x_loaded"], 32)
                                    transpose_x(0)
                            if i == 4:
                                if is_out(behind):
                                    pe.wait_ge(e["g_hT_copied"], 1)
                                    transpose_hidden(1)
                                elif behind is not None:
                                    pe.wait_ge(e["g_y2_ready"], 2 * behind - 1)
                                    query_product(kn, 1, moving_hl)
                                elif not last:
                                    pe.wait_ge(e["g_x_rest"], 1)
                                    transpose_x(1)
                            if i == 5 and came is not None:
                                if is_out(behind):
                                    pe.wait_ge(e["g_hT_copied"], 2)
                                elif behind is not None:
                                    pe.wait_ge(e["g_y2_ready"], 2 * behind)
                                elif not last:
                                    pe.wait_ge(e["g_x_rest"], 2)
                                if came == "head":
                                    spread_inverse(None if start_of_element else u - 1, 1)
                                else:
                                    out_rows(u - 1, 1)
                            if i == 6 and came == "head":
                                project(h_before, 1, kb)
                            if i == 7 and came == "head":
                                project_out(h_before, 1, kb)

                    pe.wait_ge(e["g_main_hi"], 1)
                    pe.wait_ge(e["g_main_lo"], 1)
                    pe.wait_ge(e["g_v_rest"], 1)
                    for i in range(AHEAD):
                        score(0, 0, i, 0)
                    program(run, pe.Fori)
                    collected = 2 * (HEADS - 1 + before)
                    if not last:
                        pe.wait_ge(e["g_wa_ready"], NEXT)
                        pe.wait_ge(e["g_o_stacked"], 2 if first else 4)
                        pe.wait_ge(e["g_hacc_ready"], collected)
                        query_product(0, 0, other_hl)
                        pe.wait_ge(e["g_y2_ready"], 2 * NEXT - 1)
                        query_product(0, 1, other_hl)
                        for chunk in range(3):
                            mix(END, HEADS - 1, 1, chunk)
                    else:
                        for half in range(2):
                            if half == 1:
                                for chunk in range(3):
                                    mix(END, HEADS - 1, 1, chunk)
                            pe.wait_ge(e["g_hacc_ready"], collected + half)
                            spread_inverse(END, half)
                            project(HEADS - 1, half, 1)
                            project_out(HEADS - 1, half, 1)
                        pe.wait_ge(e["g_hacc_ready"], collected + 2)
                        pe.wait_ge(e["g_o_stacked"], 4)
                        for i in range(2):
                            score(FINAL, "out", i, 0)
                        transpose_hidden(0)
                        pe.wait_ge(e["g_hT_copied"], 3)
                        transpose_hidden(1)
                        for i in range(NT):
                            transpose(FINAL, i)
                            if i + AHEAD < NT:
                                score(FINAL, "out", i + AHEAD, 0)
                            if i == 5:
                                pe.wait_ge(e["g_hT_copied"], 4)
                            if i >= 5:
                                mix(FINAL, "out", 0, i - 5)
                        for half in range(2):
                            if half == 1:
                                for chunk in range(3):
                                    mix(FINAL, "out", 1, chunk)
                                pe.wait_ge(e["g_o_used"], 3)
                            out_rows(FINAL, half)

                @block.scalar
                def _(act):
                    def exponentials(u, i):
                        act.wait_ge(e["g_t_ready"], 8 * u + i + 1)
                        k = i % SLOTS
                        nc.scalar.activation(tile[k][:, :], tile[k][:, :], ACT.Exp, bias=neg_max[k][:, :],
                                             accum_out=row_sum[:, i:i + 1]).then_inc(e["g_p_ready"], 1)

                    def high(u, i):
                        n = 8 * u + i
                        half, j = i // 4, i % 4
                        for a in range(2):
                            if j == 0 and a == 0 and not (isinstance(u, int) and u == 0):
                                act.wait_ge(e["g_u_ready"], 2 * u - 1 + half)
                            act.wait_ge(e["g_pt_ready"], 2 * n + a + 1)
                            nc.scalar.activation(pt_hi[half][:, 4 * a:4 * a + 4, j * P:(j + 1) * P],
                                                 ps_t[a][:, :].rearrange("p (m n) -> p m n", n=P), ACT.Copy).then_inc(e["g_hi_ready"], 1)

                    def take_mixed(u, half):
                        act.wait_ge(e["g_u_ready"], 2 * u + half + 1)
                        nc.scalar.activation(mixed[:, :], ps_u[:, :], ACT.Copy).then_inc(e["g_ut_ready"], 1)

                    def add_bias(h, half, k):
                        act.wait_ge(e["g_cat_ready"], 2 * (h + before) + half + 1)
                        nc.scalar.activation(cat[:, :], ps_x[:, :], ACT.Identity, bias=W_cur[k][:, 2 * P:2 * P + 1]).then_inc(e["g_vb_ready"], 1)

                    def round_queries(h, half, k):
                        act.wait_ge(e["g_y_ready"], 2 * h - 1 + half)
                        query_high(k, half)

                    def run(u, h, came, behind, h_before, k=0, looped=False):
                        k = parity(h, k) if not is_out(h) else 0
                        kb = (1 - k) if not is_out(h) and not is_int(h, 2) else 1
                        kn = (1 - k) if not is_out(h) else 0
                        start_of_element = isinstance(u, int) and u == 0
                        for i in range(NT):
                            high(u, i)
                            if i + 1 < NT:
                                exponentials(u, i + 1)
                            elif behind is not None:
                                exponentials(u + 1, 0)
                            if i == 0 and came is not None and not start_of_element:
                                take_mixed(u - 1, 0)
                            if i == 0 and is_out(behind):
                                act.wait_ge(e["g_hacc_ready"], 2)
                                nc.scalar.activation(other_hi[:, :], hidden[:, :], ACT.Copy).then_inc(e["g_h_high"], 1)
                            if i == 1 and came == "head":
                                add_bias(h_before, 0, kb)
                            if i == 3:
                                if behind is None and not last:
                                    x_high(act, 0)
                                elif behind is not None and not is_out(behind):
                                    round_queries(behind, 0, kn)
                            if i == 3 and behind is None and not first:
                                act.wait_ge(e["g_norm"], 6)
                                nc.scalar.activation(sq[:, :, :], y[:, :, :], ACT.Square).then_inc(e["g_square"], 1)
                            if i == 4 and came is not None:
                                if start_of_element:
                                    act.wait_ge(e["g_un_ready"], 1)
                                    nc.scalar.activation(mixed[:, :], ps_u[:, :], ACT.Copy).then_inc(e["g_ut_ready"], 1)
                                else:
                                    take_mixed(u - 1, 1)
                            if i == 4:
                                if behind is None and not last:
                                    x_high(act, 1)
                                elif behind is not None and not is_out(behind):
                                    round_queries(behind, 1, kn)
                            if i == 6 and came == "head":
                                add_bias(h_before, 1, kb)

                    nc.scalar.activation(moving_hi[:, :], other_hi[:, :].bitcast(F32), ACT.Copy).then_inc(e["g_main_hi"], 1)
                    exponentials(0, 0)
                    program(run, act.Fori)
                    take_mixed(END, 0)
                    if not last:
                        round_queries(NEXT, 0, 0)
                        round_queries(NEXT, 1, 0)
                    else:
                        add_bias(HEADS - 1, 0, 1)
                        take_mixed(END, 1)
                        add_bias(HEADS - 1, 1, 1)
                        act.wait_ge(e["g_hacc_ready"], 2 * (HEADS + before))
                        nc.scalar.activation(other_hi[:, :], hidden[:, :], ACT.Copy).then_inc(e["g_h_high"], 1)
                        exponentials(FINAL, 0)
                        for i in range(NT):
                            high(FINAL, i)
                            if i + 1 < NT:
                                exponentials(FINAL, i + 1)
                        for half in range(2):
                            if half == 1:
                                act.wait_ge(e["g_o_ready"], 3)
                            take_mixed(FINAL, half)
                        act.wait_ge(e["g_norm"], 12)
                        nc.scalar.activation(sq[:, :, :], y[:, :, :], ACT.Square).then_inc(e["g_square"], 1)

                @block.vector
                def _(dve):
                    def mask_and_max(u, i):
                        n = 8 * u + i
                        k = i % SLOTS
                        if not isinstance(n, int) or n >= SLOTS:
                            dve.wait_ge(e["g_pt_ready"], 2 * n - 2 * SLOTS + 2)
                        dve.wait_ge(e["g_s_ready"], n + 1)
                        nc.vector.memset(waiter[:, :], 0.0)
                        nc.vector.tensor_tensor_reduce(out=tile[k][:, :], in0=ps_s[i % 2][:, :], in1=graph[:, i, :],
                                                       scale=1.0, scalar=LOWEST, op0=ALU.mult, op1=ALU.max,
                                                       accum_out=row_max[k][:, :]).then_inc(e["g_m_ready"], 1)
                        dve.wait_ge(e["g_m_ready"], n + 1)
                        nc.vector.tensor_scalar(neg_max[k][:, :], row_max[k][:, :], -1.0, None, ALU.mult).then_inc(e["g_t_ready"], 1)

                    def rest(u, i):
                        n = 8 * u + i
                        half, j = i // 4, i % 4
                        for a in range(2):
                            dve.wait_ge(e["g_hi_ready"], 2 * n + a + 1)
                            into = (slice(None), slice(4 * a, 4 * a + 4), slice(j * P, (j + 1) * P))
                            nc.vector.tensor_tensor(pt_lo[half][into], ps_t[a][:, :].rearrange("p (m n) -> p m n", n=P),
                                                    pt_hi[half][into].bitcast(F32), ALU.subtract).then_inc(e["g_lo_ready"], 1)

                    def inverse(u, half, spread):
                        dve.wait_ge(e["g_p_ready"], 8 * u + 4 * half + 4)
                        if spread is not None:
                            dve.wait_ge(e["g_rb_ready"], spread)
                        cols = slice(4 * half, 4 * half + 4)
                        nc.vector.reciprocal(row_inv[:, cols], row_sum[:, cols]).then_inc(e["g_ri_ready"], 1)

                    def scale_mixed(u, h, half):
                        if u is not None:
                            dve.wait_ge(e["g_ut_ready"], 2 * u + half + 1 + before)
                        elif half == 1:
                            dve.wait_ge(e["g_ut_ready"], 1)
                        dve.wait_ge(e["g_rb_ready"], 2 * (h + before) + half + 1)
                        nc.vector.tensor_tensor(mixed_n[:, :], mixed[:, :], ps_x[:, :], ALU.mult).then_inc(e["g_un_ready"], 1)

                    def leaky(h, half):
                        dve.wait_ge(e["g_vb_ready"], 2 * (h + before) + half + 1)
                        nc.vector.scalar_tensor_tensor(cat[:, :], cat[:, :], 0.01, cat[:, :], ALU.mult, ALU.max).then_inc(e["g_v_ready"], 1)

                    def collect(h, half):
                        count = 2 * (h + before) + half + 1
                        cols = slice(half * HN, (half + 1) * HN)
                        dve.wait_ge(e["g_hp_ready"], count)
                        if isinstance(h, int) and h == 0:
                            nc.vector.tensor_copy(hidden[:, cols], ps_x[:, :]).then_inc(e["g_hacc_ready"], 1)
                            return
                        if not (isinstance(h, int) and h < 0):
                            dve.wait_ge(e["g_hacc_ready"], count - 2)
                        nc.vector.tensor_tensor(hidden[:, cols], hidden[:, cols], ps_x[:, :], ALU.add).then_inc(e["g_hacc_ready"], 1)

                    def rest_of_queries(h, half, k):
                        dve.wait_ge(e["g_yr_ready"], 2 * h - 1 + half)
                        query_rest(k, half)

                    def split_hidden(number):
                        dve.wait_ge(e["g_h_high"], number)
                        nc.vector.tensor_tensor(other_lo[:, :], hidden[:, :], other_hi[:, :].bitcast(F32), ALU.subtract).then_inc(e["g_h_rest"], 1)

                    def hidden_rows(number, half):
                        dve.wait_ge(e["g_hT_ready"], number)
                        nc.vector.tensor_copy(other_value[:, 4 * half:4 * half + 4, :],
                                              ps_x[:, :].rearrange("p (t c) -> p t c", c=P)).then_inc(e["g_hT_copied"], 1)

                    def out_half(u, number, half):
                        tiles = slice(4 * half, 4 * half + 4)
                        dve.wait_ge(e["g_ri_ready"], 2 * u + half + 1)
                        dve.wait_ge(e["g_o_ready"], number)
                        nc.vector.tensor_tensor(y[:, tiles, :], ps_x[:, 0:4 * C].rearrange("p (t c) -> p t c", c=C),
                                                row_inv[:, tiles].unsqueeze(2).broadcast_to([P, 4, C]), ALU.mult).then_inc(e["g_o_used"], 1)

                    def spread(v):
                        return v[:, :].unsqueeze(2).broadcast_to([P, NT, C])

                    def norm(step, turn):
                        count = 6 * turn + step
                        if step == 0:
                            dve.wait_ge(e["g_o_used"], 2 * turn + 2)
                            ins = nc.vector.tensor_tensor(y[:, :, :], y[:, :, :], b_out_row[:, :].unsqueeze(1).broadcast_to([P, NT, C]), ALU.add)
                        elif step < 6:
                            dve.wait_ge(e["g_norm"], count)
                        if step == 1:
                            ins = nc.vector.scalar_tensor_tensor(y[:, :, :], y[:, :, :], 0.01, y[:, :, :], ALU.mult, ALU.max)
                        if step == 2:
                            dve.wait_ge(e["g_r_loaded"], 16 * turn + 16)
                            ins = nc.vector.tensor_tensor(y[:, :, :], y[:, :, :], x_again[:, :, :], ALU.add)
                        if step == 3:
                            ins = nc.vector.tensor_reduce(mean[:, :], y[:, :, :], AX.X, ALU.add)
                        if step == 4:
                            ins = nc.vector.tensor_scalar(mean[:, :], mean[:, :], 1.0 / C, None, ALU.mult)
                        if step == 5:
                            ins = nc.vector.tensor_tensor(y[:, :, :], y[:, :, :], spread(mean), ALU.subtract)
                        if step < 6:
                            ins.then_inc(e["g_norm"], 1)
                        if step == 6:
                            dve.wait_ge(e["g_square"], turn + 1)
                            nc.vector.tensor_reduce(var[:, :], sq[:, :, :], AX.X, ALU.add).then_inc(e["g_v_high"], 1)
                            dve.wait_ge(e["g_v_high"], 2 + turn)
                            nc.vector.tensor_scalar(var[:, :], var[:, :], 1.0 / C, EPS, ALU.mult, ALU.add).then_inc(e["g_var_ready"], 1)
                        if step == 7:
                            dve.wait_ge(e["g_rstd_ready"], turn + 1)
                            nc.vector.tensor_tensor(y[:, :, :], y[:, :, :], spread(rstd), ALU.mult).then_inc(e["g_y_done"], 1)

                    def run(u, h, came, behind, h_before, k=0, looped=False):
                        k = parity(h, k) if not is_out(h) else 0
                        kn = (1 - k) if not is_out(h) else 0
                        start_of_element = isinstance(u, int) and u == 0
                        from_unit = None if start_of_element else u - 1
                        for i in range(NT):
                            if i + 1 < NT:
                                mask_and_max(u, i + 1)
                            elif behind is not None:
                                mask_and_max(u + 1, 0)
                            rest(u, i)
                            if i == 1 and is_out(behind):
                                split_hidden(1)
                            if came == "head":
                                if i == 0 or i == 5:
                                    scale_mixed(from_unit, h_before, i // 5)
                                if i == 1 or i == 6:
                                    leaky(h_before, i // 6)
                                if i == 2 or i == 7:
                                    collect(h_before, i // 7)
                            if came == "out":
                                if i == 0 or i == 5:
                                    out_half(u - 1, 1 + i // 5, i // 5)
                                if i == 6:
                                    norm(0, 0)
                                if i == 7:
                                    norm(1, 0)
                            if i == 3 or i == 7:
                                inverse(u, i // 4, 2 * (h_before + before) + i // 4 + 1 if came == "head" else None)
                            if i == 3 or i == 4:
                                if is_out(behind):
                                    hidden_rows(i - 2, i - 3)
                                elif behind is not None:
                                    rest_of_queries(behind, i - 3, kn)
                                elif not last:
                                    x_rest(dve, i - 3)
                            if behind is None and not first:
                                if i <= 2:
                                    norm(2 + i, 0)
                                if i == 3:
                                    norm(5, 0)
                                if i == 5:
                                    norm(6, 0)

                    nc.vector.tensor_copy(moving_lo[:, :], other_lo[:, :].bitcast(F32)).then_inc(e["g_main_lo"], 1)
                    nc.vector.tensor_copy(value_hl[:, :, 0:C], x_rows[:, :, 0:C]).then_inc(e["g_v_high"], 1)
                    dve.wait_ge(e["g_v_high"], 1)
                    nc.vector.tensor_tensor(value_hl[:, :, C:P], x_rows[:, :, C:P], value_hl[:, :, 0:C].bitcast(F32),
                                            ALU.subtract).then_inc(e["g_v_rest"], 1)
                    mask_and_max(0, 0)
                    program(run, dve.Fori)
                    if not last:
                        rest_of_queries(NEXT, 0, 0)
                        rest_of_queries(NEXT, 1, 0)
                    if not first:
                        norm(7, 0)
                    if last:
                        for half in range(2):
                            scale_mixed(END, HEADS - 1, half)
                            leaky(HEADS - 1, half)
                            collect(HEADS - 1, half)
                        split_hidden(2)
                        mask_and_max(FINAL, 0)
                        hidden_rows(3, 0)
                        hidden_rows(4, 1)
                        for i in range(NT):
                            if i + 1 < NT:
                                mask_and_max(FINAL, i + 1)
                            rest(FINAL, i)
                            if i == 3 or i == 7:
                                inverse(FINAL, i // 4, 2 * (HEADS - 1 + before) + i // 4 + 1)
                        dve.wait_ge(e["g_stored"], 16)
                        for half in range(2):
                            out_half(FINAL, 3 + half, half)
                        for step in range(8):
                            norm(step, 1)
            nc.all_engine_barrier(sems_to_clear=numbers(e))

        element(0, first=True)
        with nc.Fori(1, BATCH - 1) as b:
            element(b)
        element(BATCH - 1, last=True)


def causal_steps(nc, bank, io, adjT_dram, x_in, x_out):
    STEPS = 3
    ctx = ExitStack()
    with ctx:
        def sb(name, shape, dt=F32):
            return ctx.enter_context(nc.sbuf_tensor(name, shape, dt))

        adjT = sb("c_adjT", [P, NT, N])
        ident = sb("c_ident", [P, P])
        w_stage = sb("c_w_stage", [C, 3, P])
        w_diag = sb("c_w_diag", [P, 3, P])
        b1 = sb("c_b1", [P, 1])
        b2 = sb("c_b2", [P, 1])
        b2_row = sb("c_b2_row", [P, P])
        x_rows = sb("c_x_rows", [P, NT, BATCH, C])
        v_rows = sb("c_v_rows", [P, NT, BATCH, C])
        vT = sb("c_vT", [P, PAIRS, N])
        effect = [sb(f"c_effect{k}", [P, N]) for k in range(2)]
        hidden = [sb(f"c_hidden{k}", [P, N]) for k in range(2)]
        sq = sb("c_sq", [P, NT * BATCH, C])
        mean = sb("c_mean", [P, NT * BATCH])
        var = sb("c_var", [P, NT * BATCH])
        rstd = sb("c_rstd", [P, NT * BATCH])
        minus_half = sb("c_minus_half", [P, NT * BATCH])
        ps_e = [ctx.enter_context(nc.psum_tensor(f"c_ps_e{k}", [P, N], F32)) for k in range(2)]
        ps_h = ctx.enter_context(nc.psum_tensor("c_ps_h", [P, N], F32))
        ps_v = ctx.enter_context(nc.psum_tensor("c_ps_v", [P, N], F32))

        def columns(p):
            return v_rows[:, :, 2 * p:2 * p + 2, :]

        setup = events(bank, "c_w_loaded c_adj_loaded c_x_loaded c_v_loaded c_zeroed c_ident_ready c_w_zeroed "
                                "c_wT_ready c_w_ready c_half_ready c_vT_ready c_vT_copied c_intervened")
        with nc.Block() as block:
            e = setup

            @block.sync
            def _(sp):
                xr = x_in.rearrange("b (t p) c -> p t b c", p=P)
                for t in range(NT):
                    sp.dma_start(x_rows[:, t, :, :], xr[:, t, :, :]).then_inc(e["c_x_loaded"], 16)
                    sp.dma_start(v_rows[:, t, :, :], xr[:, t, :, :]).then_inc(e["c_v_loaded"], 16)
                for k in range(2):
                    half = slice(k * C, (k + 1) * C)
                    for i, src in enumerate((io["L2_gnn_W1"][:, 0:C], io["L2_gnn_W1"][:, C:2 * C], io["L2_gnn_W2"])):
                        sp.dma_start(w_stage[:, i, half], src).then_inc(e["c_w_loaded"], 16)
                    sp.dma_start(b1[half, :], io["L2_gnn_b1"].rearrange("(c o) -> c o", o=1)).then_inc(e["c_w_loaded"], 16)
                    sp.dma_start(b2[half, :], io["L2_gnn_b2"].rearrange("(c o) -> c o", o=1)).then_inc(e["c_w_loaded"], 16)
                    sp.dma_start(b2_row[:, half], io["L2_gnn_b2"].partition_broadcast(P)).then_inc(e["c_w_loaded"], 16)
                sp.wait_ge(e["c_v_loaded"], 16 * NT)
                for b in range(BATCH):
                    sp.dma_start(v_rows[0:1, 0, b, :], io["L2_gnn_intervention_value"]).then_inc(e["c_intervened"], 16)
                sp.dma_start(adjT[:, :, :], adjT_dram.rearrange("(t p) n -> p t n", p=P)).then_inc(e["c_adj_loaded"], 16)
                sp.wait_ge(e["c_adj_loaded"], 16)
                sp.wait_ge(e["c_x_loaded"], 16 * NT)

            @block.gpsimd
            def _(pool):
                make_identity(pool, ident, e["c_zeroed"], e["c_ident_ready"], 0)
                nc.gpsimd.memset(w_diag[:, :, :], 0.0).then_inc(e["c_w_zeroed"], 1)
                nc.gpsimd.memset(minus_half[:, :], -0.5).then_inc(e["c_half_ready"], 1)

            @block.tensor
            def _(pe):
                pe.wait_ge(e["c_ident_ready"], 1)
                pe.wait_ge(e["c_w_loaded"], 16 * 12)
                for i in range(3):
                    mm = nc.tensor.transpose(ps_h[:, i * C:(i + 1) * C], w_stage[:, i, :], ident[0:C, 0:C])
                mm.then_inc(e["c_wT_ready"], 1)
                pe.wait_ge(e["c_intervened"], 16 * BATCH)
                for p in range(PAIRS):
                    if p >= 2:
                        pe.wait_ge(e["c_vT_copied"], p - 1)
                    for t in range(NT):
                        mm = nc.tensor.transpose(ps_e[p % 2][:, t * P:(t + 1) * P],
                                                 v_rows[:, t, 2 * p:2 * p + 2, :].rearrange("p b c -> p (b c)"), ident[:, :])
                    mm.then_inc(e["c_vT_ready"], 1)

            @block.vector
            def _(dve):
                dve.wait_ge(e["c_w_zeroed"], 1)
                dve.wait_ge(e["c_wT_ready"], 1)
                for k in range(2):
                    half = slice(k * C, (k + 1) * C)
                    nc.vector.tensor_copy(w_diag[half, :, half], ps_h[half, 0:3 * C].rearrange("p (i c) -> p i c", c=C)).then_inc(e["c_w_ready"], 1)
                for p in range(PAIRS):
                    dve.wait_ge(e["c_vT_ready"], p + 1)
                    nc.vector.tensor_copy(vT[:, p, :], ps_e[p % 2][:, :]).then_inc(e["c_vT_copied"], 1)
        nc.all_engine_barrier(sems_to_clear=numbers(setup))

        e = events(bank, "c_effect_ready c_effect_copied c_hidden_ready c_hidden_copied c_next_ready "
                            "c_next_copied c_rows_ready c_rows_copied c_norm c_var_ready c_rstd_ready c_y_done c_stored")
        with nc.Fori(0, STEPS) as step:
            with nc.Block() as block:

                @block.tensor
                def _(pe):
                    for u in range(PAIRS + 2):
                        if u < PAIRS:
                            if u >= 2:
                                pe.wait_ge(e["c_effect_copied"], u - 1)
                            for m in range(2):
                                cols = slice(m * HN, (m + 1) * HN)
                                for t in range(NT):
                                    mm = nc.tensor.matmul(ps_e[u % 2][:, cols], v_rows[:, t, 2 * u:2 * u + 2, :].rearrange("p b c -> p (b c)"),
                                                          adjT[:, t, cols], start=(t == 0), stop=(t == NT - 1))
                            mm.then_inc(e["c_effect_ready"], 1)
                        if u >= 2:
                            p = u - 2
                            pe.wait_ge(e["c_hidden_copied"], p + 1)
                            if p >= 1:
                                pe.wait_ge(e["c_rows_copied"], p)
                            for m in range(2):
                                cols = slice(m * HN, (m + 1) * HN)
                                mm = nc.tensor.matmul(ps_v[:, cols], w_diag[:, 2, :], hidden[p % 2][:, cols], start=True, stop=True)
                            mm.then_inc(e["c_next_ready"], 1)
                            pe.wait_ge(e["c_next_copied"], p + 1)
                            for t in range(NT):
                                mm = nc.tensor.matmul(ps_v[:, t * P:(t + 1) * P], hidden[p % 2][:, t * P:(t + 1) * P], w_diag[:, 2, :],
                                                      start=True, stop=True)
                            mm.then_inc(e["c_rows_ready"], 1)
                        if 1 <= u <= PAIRS:
                            p = u - 1
                            pe.wait_ge(e["c_effect_copied"], p + 1)
                            if p >= 1:
                                pe.wait_ge(e["c_hidden_copied"], p)
                            for m in range(2):
                                cols = slice(m * HN, (m + 1) * HN)
                                nc.tensor.matmul(ps_h[:, cols], w_diag[:, 0, :], vT[:, p, cols], start=True, stop=False)
                                mm = nc.tensor.matmul(ps_h[:, cols], w_diag[:, 1, :], effect[p % 2][:, cols], start=False, stop=True)
                            mm.then_inc(e["c_hidden_ready"], 1)

                @block.scalar
                def _(act):
                    for p in range(PAIRS):
                        act.wait_ge(e["c_hidden_ready"], p + 1)
                        if p >= 2:
                            act.wait_ge(e["c_rows_ready"], p - 1)
                        nc.scalar.activation(hidden[p % 2][:, :], ps_h[:, :], ACT.Relu, bias=b1[:, :]).then_inc(e["c_hidden_copied"], 1)
                        act.wait_ge(e["c_next_ready"], p + 1)
                        nc.scalar.activation(vT[:, p, :], ps_v[:, :], ACT.Identity, bias=b2[:, :]).then_inc(e["c_next_copied"], 1)

                @block.vector
                def _(dve):
                    def take_effect(p):
                        dve.wait_ge(e["c_effect_ready"], p + 1)
                        if p >= 2:
                            dve.wait_ge(e["c_hidden_ready"], p - 1)
                        nc.vector.tensor_copy(effect[p % 2][:, :], ps_e[p % 2][:, :]).then_inc(e["c_effect_copied"], 1)

                    take_effect(0)
                    take_effect(1)
                    for p in range(PAIRS):
                        if p + 2 < PAIRS:
                            take_effect(p + 2)
                        dve.wait_ge(e["c_rows_ready"], p + 1)
                        nc.vector.tensor_tensor(columns(p).rearrange("p t b c -> p t (b c)"), ps_v[:, :].rearrange("p (t c) -> p t c", c=P),
                                                b2_row[:, :].unsqueeze(1).broadcast_to([P, NT, P]), ALU.add).then_inc(e["c_rows_copied"], 1)
            nc.all_engine_barrier(sems_to_clear=numbers(e))

        with nc.Block() as block:
            v_all = v_rows[:, :, :, :].rearrange("p t b c -> p (t b) c")

            @block.vector
            def _(dve):
                done = 0

                def link(ins):
                    nonlocal done
                    done += 1
                    ins.then_inc(e["c_norm"], 1)
                    dve.wait_ge(e["c_norm"], done)

                link(nc.vector.tensor_tensor(v_all, v_all, x_rows[:, :, :, :].rearrange("p t b c -> p (t b) c"), ALU.add))
                layer_norm_rows(nc, dve, link, v_all, sq[:, :, :], mean[:, :], var[:, :], rstd[:, :],
                                e["c_var_ready"], e["c_rstd_ready"], e["c_y_done"])

            @block.gpsimd
            def _(pool):
                pool.wait_ge(e["c_var_ready"], 1)
                nc.gpsimd.tensor_tensor(rstd[:, :], var[:, :], minus_half[:, :], ALU.pow).then_inc(e["c_rstd_ready"], 1)

            @block.sync
            def _(sp):
                sp.wait_ge(e["c_y_done"], 1)
                for t in range(NT):
                    sp.dma_start(x_out.rearrange("b (t p) c -> p t b c", p=P)[:, t, :, :], v_rows[:, t, :, :]).then_inc(e["c_stored"], 16)
                sp.wait_ge(e["c_stored"], 16 * NT)
        nc.all_engine_barrier(sems_to_clear=numbers(e))


def adaptive_chebyshev(nc, bank, io, adjT_dram, x_in, x_out):
    D = io["L3_gnn_node_embeddings"].shape[1]
    ctx = ExitStack()
    with ctx:
        def sb(name, shape, dt=F32):
            return ctx.enter_context(nc.sbuf_tensor(name, shape, dt))

        adjT = sb("k_adjT", [P, NT, N])
        aptT = sb("k_aptT", [P, NT, N])
        ident = sb("k_ident", [P, P])
        embed = sb("k_embed", [P, NT, D])
        embedT = sb("k_embedT", [D, N])
        pool_w = sb("k_pool_w", [P, 2, D, C])
        pool_b = sb("k_pool_b", [D, C])
        bias = sb("k_bias", [P, NT, C])
        g01 = sb("k_g01", [P, NT, BATCH, 2, C])
        g23 = sb("k_g23", [P, NT, BATCH, 2, C])
        relu = sb("k_relu", [P, N])
        probs = [sb(f"k_probs{k}", [P, N]) for k in range(2)]
        row_max = sb("k_row_max", [P, NT])
        row_sum = sb("k_row_sum", [P, NT])
        row_inv = sb("k_row_inv", [P, NT])
        stage = [sb(f"k_stage{k}", [P, 2, BATCH, P]) for k in range(2)]
        gT = [sb(f"k_gT{k}", [P, 2, P]) for k in range(2)]
        mixed = [probs[0], probs[1]]
        y = sb("k_y", [P, 2, BATCH, C])
        sq = sb("k_sq", [P, 2 * BATCH, C])
        mean = sb("k_mean", [P, 2 * BATCH])
        var = sb("k_var", [P, 2 * BATCH])
        rstd = sb("k_rstd", [P, 2 * BATCH])
        minus_half = sb("k_minus_half", [P, 2 * BATCH])
        ps_a = [ctx.enter_context(nc.psum_tensor(f"k_ps_a{k}", [P, N], F32)) for k in range(2)]
        ps_b = [ctx.enter_context(nc.psum_tensor(f"k_ps_b{k}", [P, HN], F32)) for k in range(2)]

        setup = events(bank, "k_adj_loaded k_x_loaded k_e_loaded k_w_loaded k_zeroed k_ident_ready k_half_ready "
                                "k_eT_ready k_eT_copied k_bias_ready k_bias_copied k_s_ready k_relu_ready k_max_ready "
                                "k_p_ready k_pt_ready k_pt_copied k_inv_ready k_x1_ready k_x1_copied k_x2_ready "
                                "k_x2_copied k_x3_ready k_x3_copied")
        with nc.Block() as block:
            e = setup

            @block.sync
            def _(sp):
                sp.dma_start(embed[:, :, :], io["L3_gnn_node_embeddings"].rearrange("(t p) d -> p t d", p=P)).then_inc(e["k_e_loaded"], 16)
                for t in range(NT):
                    sp.dma_start(g01[:, t, :, 0, :], x_in.rearrange("b (t p) c -> p t b c", p=P)[:, t, :, :]).then_inc(e["k_x_loaded"], 16)
                sp.dma_start(adjT[:, :, :], adjT_dram.rearrange("(t p) n -> p t n", p=P)).then_inc(e["k_adj_loaded"], 16)
                for k in range(4):
                    sp.dma_start(pool_w[(k % 2) * C:(k % 2 + 1) * C, k // 2, :, :],
                                 io["L3_gnn_weights_pool"][:, k, :, :].rearrange("d i o -> i d o")).then_inc(e["k_w_loaded"], 16)
                sp.dma_start(pool_b[:, :], io["L3_gnn_bias_pool"]).then_inc(e["k_w_loaded"], 16)
                sp.wait_ge(e["k_w_loaded"], 16 * 5)

            @block.gpsimd
            def _(pool):
                make_identity(pool, ident, e["k_zeroed"], e["k_ident_ready"], 0)
                nc.gpsimd.memset(minus_half[:, :], -0.5).then_inc(e["k_half_ready"], 1)

            @block.tensor
            def _(pe):
                pe.wait_ge(e["k_ident_ready"], 1)
                pe.wait_ge(e["k_e_loaded"], 16)
                for t in range(NT):
                    mm = nc.tensor.transpose(ps_a[0][0:D, t * P:(t + 1) * P], embed[:, t, :], ident[:, :])
                mm.then_inc(e["k_eT_ready"], 1)
                pe.wait_ge(e["k_eT_copied"], 1)
                pe.wait_ge(e["k_w_loaded"], 16 * 5)
                for t in range(NT):
                    mm = nc.tensor.matmul(ps_b[0][:, t * C:(t + 1) * C], embedT[:, t * P:(t + 1) * P], pool_b[:, :], start=True, stop=True)
                mm.then_inc(e["k_bias_ready"], 1)
                for t in range(NT + 1):
                    if t < NT:
                        if t >= 1:
                            pe.wait_ge(e["k_relu_ready"], t)
                        for m in range(2):
                            cols = slice(m * HN, (m + 1) * HN)
                            mm = nc.tensor.matmul(ps_a[0][:, cols], embedT[:, t * P:(t + 1) * P], embedT[:, cols], start=True, stop=True)
                        mm.then_inc(e["k_s_ready"], 1)
                    if t >= 1:
                        pe.wait_ge(e["k_p_ready"], t)
                        if t >= 2:
                            pe.wait_ge(e["k_pt_copied"], t - 1)
                        for s in range(NT):
                            mm = nc.tensor.transpose(ps_a[1][:, s * P:(s + 1) * P], probs[(t - 1) % 2][:, s * P:(s + 1) * P], ident[:, :])
                        mm.then_inc(e["k_pt_ready"], 1)

                def apply(matrixT, source, ready, copied, before):
                    for t in range(NT):
                        if before + t >= 2:
                            pe.wait_ge(*copied(t))
                        for s in range(NT):
                            mm = nc.tensor.matmul(ps_b[t % 2][:, :], matrixT[:, s, t * P:(t + 1) * P], source(s),
                                                  start=(s == 0), stop=(s == NT - 1))
                        mm.then_inc(ready, 1)

                pe.wait_ge(e["k_adj_loaded"], 16)
                pe.wait_ge(e["k_x_loaded"], 16 * NT)
                pe.wait_ge(e["k_bias_copied"], 1)
                apply(adjT, lambda s: g01[:, s, :, 0, :], e["k_x1_ready"], lambda t: (e["k_x1_copied"], t - 1), 0)
                pe.wait_ge(e["k_x1_copied"], NT)
                apply(adjT, lambda s: g01[:, s, :, 1, :], e["k_x2_ready"], lambda t: (e["k_x2_copied"], t - 1), 0)
                pe.wait_ge(e["k_x2_copied"], NT)
                pe.wait_ge(e["k_pt_copied"], NT)
                apply(aptT, lambda s: g01[:, s, :, 0, :], e["k_x3_ready"], lambda t: (e["k_x3_copied"], t - 1), 0)

            @block.scalar
            def _(act):
                act.wait_ge(e["k_eT_ready"], 1)
                nc.scalar.activation(embedT[:, :], ps_a[0][0:D, :], ACT.Copy).then_inc(e["k_eT_copied"], 1)
                for t in range(NT):
                    act.wait_ge(e["k_s_ready"], t + 1)
                    if t >= 1:
                        act.wait_ge(e["k_p_ready"], t)
                    nc.scalar.activation(relu[:, :], ps_a[0][:, :], ACT.Relu).then_inc(e["k_relu_ready"], 1)
                    act.wait_ge(e["k_max_ready"], t + 1)
                    if t >= 2:
                        act.wait_ge(e["k_pt_ready"], t - 1)
                    nc.scalar.activation(probs[t % 2][:, :], relu[:, :], ACT.Exp, bias=row_max[:, t:t + 1],
                                         accum_out=row_sum[:, t:t + 1]).then_inc(e["k_p_ready"], 1)
                for t in range(NT):
                    act.wait_ge(e["k_x1_ready"], t + 1)
                    nc.scalar.activation(g01[:, t, :, 1, :], ps_b[t % 2][:, :].rearrange("p (b c) -> p b c", c=C), ACT.Copy).then_inc(e["k_x1_copied"], 1)
                act.wait_ge(e["k_inv_ready"], 1)
                for t in range(NT):
                    act.wait_ge(e["k_x3_ready"], t + 1)
                    nc.scalar.activation(g23[:, t, :, 1, :], ps_b[t % 2][:, :].rearrange("p (b c) -> p b c", c=C), ACT.Copy,
                                         scale=row_inv[:, t:t + 1]).then_inc(e["k_x3_copied"], 1)

            @block.vector
            def _(dve):
                dve.wait_ge(e["k_bias_ready"], 1)
                nc.vector.tensor_copy(bias[:, :, :], ps_b[0][:, :].rearrange("p (t c) -> p t c", c=C)).then_inc(e["k_bias_copied"], 1)
                for t in range(NT):
                    dve.wait_ge(e["k_relu_ready"], t + 1)
                    nc.vector.tensor_reduce(row_max[:, t:t + 1], relu[:, :], AX.X, ALU.max, negate=True).then_inc(e["k_max_ready"], 1)
                    if t >= 1:
                        dve.wait_ge(e["k_pt_ready"], t)
                        nc.vector.tensor_copy(aptT[:, :, (t - 1) * P:t * P], ps_a[1][:, :].rearrange("p (s n) -> p s n", n=P)).then_inc(e["k_pt_copied"], 1)
                dve.wait_ge(e["k_pt_ready"], NT)
                nc.vector.tensor_copy(aptT[:, :, (NT - 1) * P:NT * P], ps_a[1][:, :].rearrange("p (s n) -> p s n", n=P)).then_inc(e["k_pt_copied"], 1)
                dve.wait_ge(e["k_p_ready"], NT)
                nc.vector.reciprocal(row_inv[:, :], row_sum[:, :]).then_inc(e["k_inv_ready"], 1)
                for t in range(NT):
                    dve.wait_ge(e["k_x2_ready"], t + 1)
                    nc.vector.scalar_tensor_tensor(g23[:, t, :, 0, :], ps_b[t % 2][:, :].rearrange("p (b c) -> p b c", c=C), 2.0,
                                                   g01[:, t, :, 0, :], ALU.mult, ALU.subtract).then_inc(e["k_x2_copied"], 1)
        nc.all_engine_barrier(sems_to_clear=numbers(setup))

        e = events(bank, "k_staged k_gT_ready k_gT_copied k_z_ready k_z_scaled k_sum_ready k_norm k_var_ready "
                            "k_rstd_ready k_y_done k_stored")
        UNITS = 2 * BATCH
        yT = x_out.rearrange("b (t p) c -> t p b c", p=P)
        with nc.Fori(0, NT // 2) as turn:
            with nc.Block() as block:

                @block.gpsimd
                def _(pool):
                    for k in range(2):
                        nc.gpsimd.tensor_copy(stage[k][:, 0, :, :], g01[:, 2 * turn + k, :, :, :].rearrange("p b k c -> p b (k c)")).then_inc(e["k_staged"], 1)
                        nc.gpsimd.tensor_copy(stage[k][:, 1, :, :], g23[:, 2 * turn + k, :, :, :].rearrange("p b k c -> p b (k c)")).then_inc(e["k_staged"], 1)
                    pool.wait_ge(e["k_var_ready"], 1)
                    nc.gpsimd.tensor_tensor(rstd[:, :], var[:, :], minus_half[:, :], ALU.pow).then_inc(e["k_rstd_ready"], 1)

                @block.tensor
                def _(pe):
                    for u in range(UNITS + 1):
                        if u < UNITS:
                            k, b = u // BATCH, u % BATCH
                            pe.wait_ge(e["k_staged"], 2 * k + 2)
                            if u >= 2:
                                pe.wait_ge(e["k_gT_copied"], u - 1)
                            for q in range(2):
                                mm = nc.tensor.transpose(ps_b[u % 2][:, q * P:(q + 1) * P], stage[k][:, q, b, :], ident[:, :])
                            mm.then_inc(e["k_gT_ready"], 1)
                        if u >= 1:
                            w = u - 1
                            pe.wait_ge(e["k_gT_copied"], w + 1)
                            if w >= 2:
                                pe.wait_ge(e["k_z_scaled"], w - 1)
                            for m in range(2):
                                cols = slice(m * HN, (m + 1) * HN)
                                for q in range(2):
                                    mm = nc.tensor.matmul(ps_a[w % 2][:, cols], gT[w % 2][:, q, :],
                                                          pool_w[:, q, m * D // 2:(m + 1) * D // 2, :].rearrange("p d o -> p (d o)"),
                                                          start=(q == 0), stop=(q == 1))
                            mm.then_inc(e["k_z_ready"], 1)

                @block.scalar
                def _(act):
                    for u in range(UNITS):
                        act.wait_ge(e["k_gT_ready"], u + 1)
                        if u >= 2:
                            act.wait_ge(e["k_z_ready"], u - 1)
                        nc.scalar.activation(gT[u % 2][:, :, :], ps_b[u % 2][:, 0:2 * P].rearrange("p (q n) -> p q n", n=P), ACT.Copy).then_inc(e["k_gT_copied"], 1)

                @block.vector
                def _(dve):
                    for u in range(UNITS):
                        k, b = u // BATCH, u % BATCH
                        dve.wait_ge(e["k_z_ready"], u + 1)
                        if u >= 2:
                            dve.wait_ge(e["k_sum_ready"], u - 1)
                        nc.vector.tensor_tensor(mixed[u % 2][:, :].rearrange("p (d o) -> p d o", o=C),
                                                ps_a[u % 2][:, :].rearrange("p (d o) -> p d o", o=C),
                                                embed[:, 2 * turn + k, :].unsqueeze(2).broadcast_to([P, D, C]), ALU.mult).then_inc(e["k_z_scaled"], 1)
                        dve.wait_ge(e["k_z_scaled"], u + 1)
                        nc.vector.tensor_reduce(y[:, k, b, :], mixed[u % 2][:, :].rearrange("p (d o) -> p o d", o=C), AX.X, ALU.add).then_inc(e["k_sum_ready"], 1)
                    done = 0

                    def link(ins):
                        nonlocal done
                        done += 1
                        ins.then_inc(e["k_norm"], 1)
                        dve.wait_ge(e["k_norm"], done)

                    dve.wait_ge(e["k_sum_ready"], UNITS)
                    for k in range(2):
                        link(nc.vector.tensor_tensor(y[:, k, :, :], y[:, k, :, :],
                                                     bias[:, 2 * turn + k, :].unsqueeze(1).broadcast_to([P, BATCH, C]), ALU.add))
                        link(nc.vector.tensor_tensor(y[:, k, :, :], y[:, k, :, :], g01[:, 2 * turn + k, :, 0, :], ALU.add))
                    layer_norm_rows(nc, dve, link, y[:, :, :, :].rearrange("p k b c -> p (k b) c"), sq[:, :, :], mean[:, :], var[:, :],
                                    rstd[:, :], e["k_var_ready"], e["k_rstd_ready"], e["k_y_done"])

                @block.sync
                def _(sp):
                    sp.wait_ge(e["k_y_done"], 1)
                    for k in range(2):
                        sp.dma_start(yT[2 * turn + k], y[:, k, :, :]).then_inc(e["k_stored"], 16)
                    sp.wait_ge(e["k_stored"], 32)
            nc.all_engine_barrier(sems_to_clear=numbers(e))


def adjacency_network(nc, io, out):
    adjT = nc.dram_tensor("adjT", (N, N), F32, kind="Internal").ap()
    x1, x2, x3 = (nc.dram_tensor(f"x{i}", (BATCH, N, C), F32, kind="Internal").ap() for i in (1, 2, 3))
    with ExitStack() as ctx:
        bank = [ctx.enter_context(nc.semaphore(f"signal{i}")) for i in range(60)]
        transpose_adjacency(nc, bank, io, adjT)
        hypergraph_attention(nc, bank, io, adjT, io["x"], x1)
        multi_head_gat(nc, bank, io, x1, x2)
        causal_steps(nc, bank, io, adjT, x2, x3)
        adaptive_chebyshev(nc, bank, io, adjT, x3, out)


_INS = ['x', 'adj', 'L0_gnn_H', 'L0_gnn_W', 'L0_gnn_W_ind', 'L0_gnn_a_node', 'L0_gnn_a_gn', 'L0_gnn_a_ge',
        'L0_gnn_fcW', 'L0_gnn_fcb', 'L0_gnn_av', 'L1_gnn_Wh', 'L1_gnn_bh', 'L1_gnn_W_out', 'L1_gnn_b_out',
        'L2_gnn_intervention_value', 'L2_gnn_W1', 'L2_gnn_b1', 'L2_gnn_W2', 'L2_gnn_b2',
        'L3_gnn_node_embeddings', 'L3_gnn_weights_pool', 'L3_gnn_bias_pool']


def kernel(**inputs):
    import numpy as _np
    import concourse.bacc as _bacc
    from concourse import mybir as _mybir
    from concourse.bass_utils import run_bass_kernel_spmd as _run

    nc = _bacc.Bacc("TRN2", target_bir_lowering=False, num_devices=1)
    arrays, io = {}, {}
    for name in _INS:
        a = _np.ascontiguousarray(inputs[name])
        arrays[f"in_{name}"] = a
        io[name] = nc.dram_tensor(f"in_{name}", a.shape, _mybir.dt.from_np(a.dtype), kind="ExternalInput").ap()
    out = nc.dram_tensor("out_0", (BATCH, N, C), F32, kind="ExternalOutput").ap()
    adjacency_network(nc, io, out)
    r = _run(nc, [arrays], core_ids=[0])
    return r.results[0]["out_0"]
```

```python
import concourse.bass as bass
from concourse import mybir
from contextlib import ExitStack

F32 = mybir.dt.float32
F32R = mybir.dt.float32r
I32 = mybir.dt.int32
BF16 = mybir.dt.bfloat16
ALU = mybir.AluOpType
ACT = mybir.ActivationFunctionType
AX = mybir.AxisListType

P = 128
BATCH, N, C = 8, 1024, 64
NT = N // P
HN = N // 2
HEADS, HC = 8, 128
EDGES = 64
PAIRS = BATCH // 2
MASKED = -1.0e16
NEG = -1.0e9
EPS = 1.0e-5
LOWEST = -3.0e38


def events(bank, names):
    names = names.split()
    assert len(names) <= len(bank)
    return dict(zip(names, bank))


def numbers(sems):
    every = [s.num for s in sems.values()]
    assert every == list(range(every[0], every[0] + len(every)))
    return range(every[0], every[0] + len(every))


def make_identity(pool, tile, zeroed, ready, before):
    pool.memset(tile[:, :], 0.0).then_inc(zeroed, 1)
    pool.wait_ge(zeroed, before + 1)
    pool.affine_select(out=tile[:, :], in_=tile[:, :], compare_op=ALU.not_equal, fill=1.0, base=0,
                       pattern=[[-1, tile.shape[1]]], channel_multiplier=1).then_inc(ready, 1)


def layer_norm_rows(nc, dve, link, y, sq, mean, var, rstd, var_ready, rstd_ready, done):
    groups = y.shape[1]

    def spread(v):
        return v.unsqueeze(2).broadcast_to([P, groups, C])

    link(nc.vector.tensor_reduce(mean, y, AX.X, ALU.add))
    link(nc.vector.tensor_scalar(mean, mean, 1.0 / C, None, ALU.mult))
    link(nc.vector.tensor_tensor(y, y, spread(mean), ALU.subtract))
    link(nc.vector.tensor_tensor(sq, y, y, ALU.mult))
    link(nc.vector.tensor_reduce(var, sq, AX.X, ALU.add))
    nc.vector.tensor_scalar(var, var, 1.0 / C, EPS, ALU.mult, ALU.add).then_inc(var_ready, 1)
    dve.wait_ge(rstd_ready, 1)
    nc.vector.tensor_tensor(y, y, spread(rstd), ALU.mult).then_inc(done, 1)


def transpose_adjacency(nc, bank, io, adjT_dram, weighted):
    ctx = ExitStack()
    with ctx:
        adj = ctx.enter_context(nc.sbuf_tensor("a_adj", [P, NT, N], F32))
        adjT = ctx.enter_context(nc.sbuf_tensor("a_adjT", [P, NT, N], F32))
        ident = ctx.enter_context(nc.sbuf_tensor("a_ident", [P, P], F32))
        ones = ctx.enter_context(nc.sbuf_tensor("a_ones", [P, P], F32))
        odd = ctx.enter_context(nc.sbuf_tensor("a_odd", [P, N], F32))
        odd_edges = ctx.enter_context(nc.sbuf_tensor("a_odd_edges", [P, NT], F32))
        odd_all = ctx.enter_context(nc.sbuf_tensor("a_odd_all", [P, 1], F32))
        ps = [ctx.enter_context(nc.psum_tensor(f"a_ps{k}", [P, N], F32)) for k in range(4)]
        e = events(bank, " ".join(f"a_loaded{t}" for t in range(NT)) + " a_zeroed a_ident_ready a_transposed a_copied_even a_copied_odd a_stored "
                   "a_ones_ready a_odd_ready a_counted a_total_ready a_total_summed")
        with nc.Block() as block:

            @block.sync
            def _(sp):
                for t in range(NT):
                    sp.dma_start(adj[:, t, :], io["adj"][t * P:(t + 1) * P, :]).then_inc(e[f"a_loaded{t}"], 16)
                for s in range(NT):
                    cols = slice(s * P, (s + 1) * P)
                    sp.wait_ge(e["a_copied_even" if s % 2 == 0 else "a_copied_odd"], s // 2 + 1)
                    sp.dma_start(adjT_dram.rearrange("(t p) n -> p t n", p=P)[:, :, cols], adjT[:, :, cols]).then_inc(e["a_stored"], 16)
                sp.wait_ge(e["a_stored"], 16 * NT)

            @block.gpsimd
            def _(pool):
                make_identity(pool, ident, e["a_zeroed"], e["a_ident_ready"], 0)

            @block.tensor
            def _(pe):
                pe.wait_ge(e["a_ident_ready"], 1)
                for s in range(NT):
                    pe.wait_ge(e[f"a_loaded{s}"], 16)
                    if s >= 4:
                        pe.wait_ge(e["a_copied_even" if s % 2 == 0 else "a_copied_odd"], s // 2 - 1)
                    for t in range(NT):
                        mm = nc.tensor.transpose(ps[s % 4][:, t * P:(t + 1) * P], adj[:, s, t * P:(t + 1) * P], ident[:, :])
                    mm.then_inc(e["a_transposed"], 1)
                pe.wait_ge(e["a_ones_ready"], 1)
                pe.wait_ge(e["a_counted"], NT)
                pe.wait_ge(e["a_copied_even"], NT // 2)
                nc.tensor.matmul(ps[0][:, 0:NT], ones[:, :], odd_edges[:, :], start=True, stop=True).then_inc(e["a_total_ready"], 1)

            @block.vector
            def _(dve):
                nc.vector.memset(ones[:, :], 1.0).then_inc(e["a_ones_ready"], 1)
                for s in range(NT):
                    dve.wait_ge(e[f"a_loaded{s}"], 16)
                    if s >= 1:
                        dve.wait_ge(e["a_counted"], s)
                    nc.vector.scalar_tensor_tensor(odd[:, :], adj[:, s, :], 0.0, adj[:, s, :], ALU.not_equal, ALU.not_equal).then_inc(e["a_odd_ready"], 1)
                    dve.wait_ge(e["a_odd_ready"], s + 1)
                    nc.vector.tensor_reduce(odd_edges[:, s:s + 1], odd[:, :], AX.X, ALU.add).then_inc(e["a_counted"], 1)
                    if s % 2 == 0:
                        dve.wait_ge(e["a_transposed"], s + 1)
                        nc.vector.tensor_copy(adjT[:, :, s * P:(s + 1) * P], ps[s % 4][:, :].rearrange("p (t n) -> p t n", n=P)).then_inc(e["a_copied_even"], 1)
                dve.wait_ge(e["a_total_ready"], 1)
                nc.vector.tensor_reduce(odd_all[:, :], ps[0][:, 0:NT], AX.X, ALU.add).then_inc(e["a_total_summed"], 1)
                dve.wait_ge(e["a_total_summed"], 1)
                nc.vector.tensor_scalar(weighted[:, :], odd_all[:, :], 0.0, None, ALU.is_gt)

            @block.scalar
            def _(act):
                for s in range(1, NT, 2):
                    act.wait_ge(e["a_transposed"], s + 1)
                    nc.scalar.activation(adjT[:, :, s * P:(s + 1) * P], ps[s % 4][:, :].rearrange("p (t n) -> p t n", n=P), ACT.Copy).then_inc(e["a_copied_odd"], 1)
        nc.all_engine_barrier(sems_to_clear=numbers(e))


def hypergraph_attention(nc, bank, io, adjT_dram, x_in, x_out):
    UNROLL = 4
    ctx = ExitStack()
    with ctx:
        def sb(name, shape, dt=F32):
            return ctx.enter_context(nc.sbuf_tensor(name, shape, dt))

        adjT = sb("h_adjT", [P, NT, N])
        inv_degree = sb("h_inv_degree", [P, N])
        ident = sb("h_ident", [P, P])
        ones = sb("h_ones", [P, P])
        pick = sb("h_pick", [P, EDGES, P], BF16)
        W_diag = sb("h_W_diag", [P, P])
        Wind_diag = sb("h_Wind_diag", [P, P])
        vectors = sb("h_vectors", [P, 3])
        spread3 = sb("h_spread3", [P, 3, P])
        fcW = sb("h_fcW", [P, P])
        fcb = sb("h_fcb", [P, 1])
        av = sb("h_av", [P, 1])
        av_half = sb("h_av_half", [P, 1])
        av_all = sb("h_av_all", [P, P])
        av_pair = sb("h_av_pair", [P, 2, 2, P])
        H_rows = sb("h_H_rows", [P, NT, 2, EDGES])
        mask_rows = sb("h_mask_rows", [P, NT, EDGES])
        fence_rows = sb("h_fence_rows", [P, NT, EDGES])
        maskT = sb("h_maskT", [P, N])
        fenceT = sb("h_fenceT", [P, N])
        x_rows = sb("h_x_rows", [P, NT, 2, C])
        xT = sb("h_xT", [P, N])
        hT = sb("h_hT", [P, N])
        half_hT = sb("h_half_hT", [P, N])
        h_rows = sb("h_h_rows", [P, NT, P])
        ind_rows = sb("h_ind_rows", [P, NT, P])
        indT = sb("h_indT", [P, N])
        gate_h = sb("h_gate_h", [P, N])
        logits = sb("h_logits", [P, N])
        alphaT = sb("h_alphaT", [P, NT, P])
        row_max = sb("h_row_max", [P, 1])
        neg_max = sb("h_neg_max", [P, 1])
        row_sum = sb("h_row_sum", [P, 1])
        row_inv = sb("h_row_inv", [P, 1])
        agg_diag = sb("h_agg_diag", [P, P])
        aggT = sb("h_aggT", [P, EDGES])
        edge_table = sb("h_edge_table", [P, EDGES, 4])
        below = sb("h_below", [P, EDGES])
        above = sb("h_above", [P, EDGES])
        he = sb("h_he", [P, EDGES])
        z_edge = sb("h_z_edge", [P, P])
        se_all = sb("h_se_all", [P, 2, EDGES])
        max2 = sb("h_max2", [P, 2 * NT])
        sum2 = sb("h_sum2", [P, 2 * NT])
        inv2 = sb("h_inv2", [P, 2 * NT])
        coef_rows = sb("h_coef_rows", [P, NT, 2, EDGES])
        coef_rest = sb("h_coef_rest", [P, N])
        coef = sb("h_coef", [P, 3, N], BF16)
        edge_now = [sb(f"h_edge_now{k}", [P, 4]) for k in range(UNROLL)]
        pool_waiter = sb("h_pool_waiter", [P, 1])
        diff = [sb(f"h_diff{k}", [P, N]) for k in range(2)]
        gate = [sb(f"h_gate{k}", [P, N]) for k in range(2)]
        shifted = [sb(f"h_shifted{k}", [P, N]) for k in range(2)]
        expv = [sb(f"h_expv{k}", [P, N]) for k in range(2)]
        reluv = [sb(f"h_reluv{k}", [P, N]) for k in range(2)]
        weighted = [sb(f"h_weighted{k}", [P, N]) for k in range(2)]
        mean = sb("h_mean", [P, 2 * NT])
        var = sb("h_var", [P, 2 * NT])
        rstd = sb("h_rstd", [P, 2 * NT])
        minus_half = sb("h_minus_half", [P, 2 * NT])
        ps_c = [ctx.enter_context(nc.psum_tensor(f"h_ps_c{k}", [P, N], F32)) for k in range(2)]
        ps_g = ctx.enter_context(nc.psum_tensor("h_ps_g", [P, N], F32))
        ps_m = ctx.enter_context(nc.psum_tensor("h_ps_m", [P, N], F32))

        def column(v):
            return v.rearrange("(c o) -> c o", o=1)

        setup = events(bank, "h_w_loaded h_adj_loaded h_zeroed h_ident_ready h_w_zeroed h_ones_ready h_half_ready "
                                "h_HT_ready h_deg_ready h_step")
        with nc.Block() as block:
            e = setup
            WEIGHTS = 16 * 14

            @block.sync
            def _(sp):
                sp.wait_ge(e["h_w_zeroed"], 2)
                for k in range(2):
                    half = slice(k * C, (k + 1) * C)
                    sp.dma_start(W_diag[half, half], io["L0_gnn_W"]).then_inc(e["h_w_loaded"], 16)
                    sp.dma_start(Wind_diag[half, half], io["L0_gnn_W_ind"]).then_inc(e["h_w_loaded"], 16)
                    sp.dma_start(fcW[half, :], io["L0_gnn_fcW"]).then_inc(e["h_w_loaded"], 16)
                    for i, name in enumerate(("L0_gnn_a_node", "L0_gnn_a_gn", "L0_gnn_a_ge")):
                        sp.dma_start(vectors[half, i:i + 1], column(io[name])).then_inc(e["h_w_loaded"], 16)
                sp.dma_start(fcb[:, :], column(io["L0_gnn_fcb"])).then_inc(e["h_w_loaded"], 16)
                sp.dma_start(av[:, :], column(io["L0_gnn_av"])).then_inc(e["h_w_loaded"], 16)
                for k in range(2):
                    sp.dma_start(H_rows[:, :, k, :], io["L0_gnn_H"].rearrange("(t p) e -> p t e", p=P)).then_inc(e["h_adj_loaded"], 16)
                sp.dma_start(adjT[:, :, :], adjT_dram.rearrange("(t p) n -> p t n", p=P)).then_inc(e["h_adj_loaded"], 16)

            @block.gpsimd
            def _(pool):
                nc.gpsimd.memset(W_diag[:, :], 0.0).then_inc(e["h_w_zeroed"], 1)
                nc.gpsimd.memset(Wind_diag[:, :], 0.0).then_inc(e["h_w_zeroed"], 1)
                make_identity(pool, ident, e["h_zeroed"], e["h_ident_ready"], 0)
                nc.gpsimd.memset(minus_half[:, :], -0.5).then_inc(e["h_half_ready"], 1)
                nc.gpsimd.memset(agg_diag[:, :], 0.0).then_inc(e["h_half_ready"], 1)
                nc.gpsimd.memset(edge_table[:, :, :], 0.0).then_inc(e["h_half_ready"], 1)

            @block.tensor
            def _(pe):
                pe.wait_ge(e["h_ident_ready"], 1)
                pe.wait_ge(e["h_adj_loaded"], 48)
                for t in range(NT):
                    mm = nc.tensor.transpose(ps_m[:, t * P:(t + 1) * P], H_rows[:, t, :, :].rearrange("p k e -> p (k e)"), ident[:, :])
                mm.then_inc(e["h_HT_ready"], 1)
                pe.wait_ge(e["h_ones_ready"], 1)
                for m in range(2):
                    cols = slice(m * HN, (m + 1) * HN)
                    for t in range(NT):
                        mm = nc.tensor.matmul(ps_g[:, cols], ones[:, :], adjT[:, t, cols], start=(t == 0), stop=(t == NT - 1))
                mm.then_inc(e["h_deg_ready"], 1)

            @block.vector
            def _(dve):
                done = 0

                def link(ins):
                    nonlocal done
                    done += 1
                    ins.then_inc(e["h_step"], 1)
                    dve.wait_ge(e["h_step"], done)

                nc.vector.memset(ones[:, :], 1.0).then_inc(e["h_ones_ready"], 1)
                link(nc.vector.memset(av_pair[:, :, :, :], 0.0))
                link(nc.vector.memset(spread3[:, :, :], 0.0))
                dve.wait_ge(e["h_ones_ready"], 1)
                dve.wait_ge(e["h_w_loaded"], WEIGHTS)
                link(nc.vector.tensor_scalar(vectors[:, 1:3], vectors[:, 1:3], 0.5, None, ALU.mult))
                for i in range(3):
                    for k in range(2):
                        half = slice(k * C, (k + 1) * C)
                        nc.vector.tensor_scalar(spread3[half, i, half], ones[half, 0:C], vectors[half, i:i + 1], None, ALU.mult)
                link(nc.vector.tensor_scalar(av_half[:, :], av[:, :], 0.5, None, ALU.mult))
                nc.vector.tensor_scalar(av_all[:, :], ones[:, :], av[:, :], None, ALU.mult)
                for k in range(2):
                    half = slice(k * C, (k + 1) * C)
                    nc.vector.tensor_scalar(av_pair[:, 0, k, half], ones[:, 0:C], av_half[:, :], -1.0, ALU.mult, ALU.mult)
                    nc.vector.tensor_scalar(av_pair[:, 1, k, half], ones[:, 0:C], av_half[:, :], None, ALU.mult)
                dve.wait_ge(e["h_ident_ready"], 1)
                for k in range(2):
                    nc.vector.tensor_copy(pick[:, :, k * C:(k + 1) * C],
                                          ident[:, k * EDGES:(k + 1) * EDGES].unsqueeze(2).broadcast_to([P, EDGES, C]))
                dve.wait_ge(e["h_adj_loaded"], 48)
                link(nc.vector.tensor_scalar(mask_rows[:, :, :], H_rows[:, :, 0, :], 0.0, None, ALU.is_gt))
                link(nc.vector.tensor_scalar(fence_rows[:, :, :], mask_rows[:, :, :], -1.0, -NEG, ALU.add, ALU.mult))
                dve.wait_ge(e["h_HT_ready"], 1)
                link(nc.vector.tensor_scalar(maskT[:, :], ps_m[:, :], 0.0, None, ALU.is_gt))
                link(nc.vector.tensor_scalar(fenceT[:, :], maskT[:, :], -1.0, -NEG, ALU.add, ALU.mult))
                dve.wait_ge(e["h_deg_ready"], 1)
                link(nc.vector.tensor_scalar(inv_degree[:, :], ps_g[:, :], 1.0, None, ALU.max))
                link(nc.vector.reciprocal(inv_degree[:, :], inv_degree[:, :]))
        nc.all_engine_barrier(sems_to_clear=numbers(setup))

        e = events(bank, "h_x_loaded h_xT_ready h_xT_copied h_hT_ready h_hT_copied h_rows_ready h_rows_copied "
                            "h_irows_ready h_irows_copied h_s_ready h_s_copied h_a_masked h_a_exp h_a_inv h_aT_ready "
                            "h_aT_copied h_agg_ready h_agg_scaled h_aggT_ready h_aggT_copied h_gateh_ready h_gateh_copied "
                            "h_gatee_ready h_gatee_copied h_he_below h_he_exp h_he_ready h_z_ready h_z_tanh h_se_ready "
                            "h_se_copied h_c_shifted h_c_exp h_c_ready h_cT_ready h_c_high h_c_parts h_ind_ready h_ind_copied "
                            "h_half_made h_chain h_norm h_var_ready h_rstd_ready h_y_done h_stored")
        loop = events(bank, "h_edge_copied h_diff_ready h_turn h_gate_ready h_shift_ready h_exp_ready h_relu_ready "
                               "h_f_ready h_w_ready h_spread_ready h_added")
        post = events(bank, "h_g_ready h_za_ready h_za_tanh h_zb_ready h_zb_tanh h_d_ready h_d_tanh h_o_ready "
                               "h_oT_ready h_y_ready h_norm h_var_ready h_rstd_ready h_y_done h_stored")
        x_pairs = x_in.rearrange("(q k) (t p) c -> q k p t c", k=2, p=P)
        y_pairs = x_out.rearrange("(q k) (t p) c -> q k p t c", k=2, p=P)

        y = weighted[0][:, :].rearrange("p (t c) -> p t c", c=C)
        sq = weighted[1][:, :].rearrange("p (t c) -> p t c", c=C)

        def normalise(dve, q, part=None):

            def link(ins, count):
                ins.then_inc(q["h_norm"], 1)
                dve.wait_ge(q["h_norm"], count)

            def spread(v):
                return v[:, :].unsqueeze(2).broadcast_to([P, 2 * NT, C])

            if part != 1:
                link(nc.vector.tensor_reduce(mean[:, :], y, AX.X, ALU.add), 1)
                link(nc.vector.tensor_scalar(mean[:, :], mean[:, :], 1.0 / C, None, ALU.mult), 2)
                link(nc.vector.tensor_tensor(y, y, spread(mean), ALU.subtract), 3)
                link(nc.vector.tensor_tensor(sq, y, y, ALU.mult), 4)
                link(nc.vector.tensor_reduce(var[:, :], sq, AX.X, ALU.add), 5)
                nc.vector.tensor_scalar(var[:, :], var[:, :], 1.0 / C, EPS, ALU.mult, ALU.add).then_inc(q["h_var_ready"], 1)
            if part != 0:
                dve.wait_ge(q["h_rstd_ready"], 1)
                nc.vector.tensor_tensor(y, y, spread(rstd), ALU.mult).then_inc(q["h_y_done"], 1)

        def raise_variance(pool, q):
            pool.wait_ge(q["h_var_ready"], 1)
            nc.gpsimd.tensor_tensor(rstd[:, :], var[:, :], minus_half[:, :], ALU.pow).then_inc(q["h_rstd_ready"], 1)

        def store(sp, q, pair):
            sp.wait_ge(q["h_y_done"], 1)
            for k in range(2):
                sp.dma_start(y_pairs[pair, k], weighted[0][:, :].rearrange("p (t k c) -> p t k c", k=2, c=C)[:, :, k, :]).then_inc(q["h_stored"], 16)
            sp.wait_ge(q["h_stored"], 32)

        def batch_pair(pair, first=False):
            with nc.Block() as block:

                @block.sync
                def _(sp):
                    for k in range(2):
                        sp.dma_start(x_rows[:, :, k, :], x_pairs[pair, k]).then_inc(e["h_x_loaded"], 16)
                    sp.wait_ge(e["h_x_loaded"], 32)
                    if not first:
                        store(sp, e, pair - 1)

                @block.gpsimd
                def _(pool):
                    if not first:
                        raise_variance(pool, e)

                @block.tensor
                def _(pe):
                    def convolve(m):
                        cols = slice(m * HN, (m + 1) * HN)
                        for t in range(NT):
                            mm = nc.tensor.matmul(ps_g[:, cols], ind_rows[:, t, :], adjT[:, t, cols], start=(t == 0), stop=(t == NT - 1))
                        return mm

                    pe.wait_ge(e["h_x_loaded"], 32)
                    for t in range(NT):
                        mm = nc.tensor.transpose(ps_m[:, t * P:(t + 1) * P], x_rows[:, t, :, :].rearrange("p k c -> p (k c)"), ident[:, :])
                    mm.then_inc(e["h_xT_ready"], 1)
                    pe.wait_ge(e["h_xT_copied"], 1)
                    for m in range(2):
                        cols = slice(m * HN, (m + 1) * HN)
                        mm = nc.tensor.matmul(ps_c[0][:, cols], W_diag[:, :], xT[:, cols], start=True, stop=True)
                    mm.then_inc(e["h_hT_ready"], 1)
                    for t in range(NT):
                        mm = nc.tensor.matmul(ps_c[1][:, t * P:(t + 1) * P], xT[:, t * P:(t + 1) * P], W_diag[:, :], start=True, stop=True)
                    mm.then_inc(e["h_rows_ready"], 1)
                    for t in range(NT):
                        mm = nc.tensor.matmul(ps_g[:, t * P:(t + 1) * P], xT[:, t * P:(t + 1) * P], Wind_diag[:, :], start=True, stop=True)
                    mm.then_inc(e["h_irows_ready"], 1)
                    pe.wait_ge(e["h_hT_copied"], 1)
                    for m in range(2):
                        cols = slice(m * HN, (m + 1) * HN)
                        mm = nc.tensor.matmul(ps_m[:, cols], spread3[:, 0, :], hT[:, cols], start=True, stop=True)
                    mm.then_inc(e["h_s_ready"], 1)
                    for m in range(2):
                        cols = slice(m * HN, (m + 1) * HN)
                        mm = nc.tensor.matmul(ps_c[0][:, cols], spread3[:, 1, :], hT[:, cols], start=True, stop=True)
                    mm.then_inc(e["h_gateh_ready"], 1)
                    pe.wait_ge(e["h_irows_copied"], 1)
                    convolve(0)
                    pe.wait_ge(e["h_a_exp"], 1)
                    pe.wait_ge(e["h_rows_copied"], 1)
                    for t in range(NT):
                        mm = nc.tensor.transpose(ps_c[1][:, t * P:(t + 1) * P], logits[:, t * P:(t + 1) * P], ident[:, :])
                    mm.then_inc(e["h_aT_ready"], 1)
                    pe.wait_ge(e["h_aT_copied"], 1)
                    for t in range(NT):
                        mm = nc.tensor.matmul(ps_m[:, 0:P], alphaT[:, t, :], h_rows[:, t, :], start=(t == 0), stop=(t == NT - 1))
                    mm.then_inc(e["h_agg_ready"], 1)
                    pe.wait_ge(e["h_agg_scaled"], 2)
                    nc.tensor.transpose(ps_c[1][:, 0:P], agg_diag[:, :], ident[:, :]).then_inc(e["h_aggT_ready"], 1)
                    pe.wait_ge(e["h_aggT_copied"], 2)
                    nc.tensor.matmul(ps_m[:, 0:EDGES], spread3[:, 2, :], aggT[:, :], start=True, stop=True).then_inc(e["h_gatee_ready"], 1)
                    pe.wait_ge(e["h_he_ready"], 1)
                    for k in range(2):
                        half = slice(k * C, (k + 1) * C)
                        mm = nc.tensor.matmul(ps_c[1][:, k * HN:k * HN + EDGES], fcW[half, :], he[half, :], start=True, stop=True)
                    mm.then_inc(e["h_z_ready"], 1)
                    pe.wait_ge(e["h_z_tanh"], 1)
                    pe.wait_ge(e["h_gatee_copied"], 1)
                    nc.tensor.matmul(ps_m[:, 0:P], av_all[:, :], z_edge[:, :], start=True, stop=True).then_inc(e["h_se_ready"], 1)
                    convolve(1).then_inc(e["h_ind_ready"], 1)
                    pe.wait_ge(e["h_c_ready"], 1)
                    for t in range(NT):
                        mm = nc.tensor.transpose(ps_c[1][:, t * P:(t + 1) * P], coef_rows[:, t, :, :].rearrange("p k e -> p (k e)"), ident[:, :])
                    mm.then_inc(e["h_cT_ready"], 1)

                @block.scalar
                def _(act):
                    act.wait_ge(e["h_xT_ready"], 1)
                    nc.scalar.activation(xT[:, :], ps_m[:, :], ACT.Copy).then_inc(e["h_xT_copied"], 1)
                    act.wait_ge(e["h_rows_ready"], 1)
                    nc.scalar.activation(h_rows[:, :, :], ps_c[1][:, :].rearrange("p (t c) -> p t c", c=P), ACT.Copy).then_inc(e["h_rows_copied"], 1)
                    act.wait_ge(e["h_irows_ready"], 1)
                    nc.scalar.activation(ind_rows[:, :, :], ps_g[:, :].rearrange("p (t c) -> p t c", c=P), ACT.Copy).then_inc(e["h_irows_copied"], 1)
                    act.wait_ge(e["h_s_ready"], 1)
                    nc.scalar.activation(logits[:, :], ps_m[:, :], ACT.Copy).then_inc(e["h_s_copied"], 1)
                    act.wait_ge(e["h_gateh_ready"], 1)
                    nc.scalar.activation(gate_h[:, :], ps_c[0][:, :], ACT.Copy).then_inc(e["h_gateh_copied"], 1)
                    act.wait_ge(e["h_a_masked"], 1)
                    nc.scalar.activation(logits[:, :], logits[:, :], ACT.Exp, bias=neg_max[:, :], accum_out=row_sum[:, :]).then_inc(e["h_a_exp"], 1)
                    act.wait_ge(e["h_aT_ready"], 1)
                    nc.scalar.activation(alphaT[:, :, :], ps_c[1][:, :].rearrange("p (t c) -> p t c", c=P), ACT.Copy).then_inc(e["h_aT_copied"], 1)
                    act.wait_ge(e["h_he_below"], 1)
                    nc.scalar.activation(below[:, :], below[:, :], ACT.Exp).then_inc(e["h_he_exp"], 1)
                    act.wait_ge(e["h_gatee_ready"], 1)
                    nc.scalar.activation(edge_table[:, :, 0], ps_m[:, 0:EDGES], ACT.Copy).then_inc(e["h_gatee_copied"], 1)
                    act.wait_ge(e["h_z_ready"], 1)
                    nc.scalar.activation(z_edge[:, :].rearrange("p (k e) -> p k e", k=2), ps_c[1][:, :].rearrange("p (k e) -> p k e", k=2)[:, :, 0:EDGES], ACT.Tanh, bias=fcb[:, :]).then_inc(e["h_z_tanh"], 1)
                    act.wait_ge(e["h_se_ready"], 1)
                    nc.scalar.activation(se_all[:, :, :], ps_m[:, 0:P].rearrange("p (k e) -> p k e", k=2), ACT.Copy).then_inc(e["h_se_copied"], 1)
                    act.wait_ge(e["h_c_shifted"], 1)
                    nc.scalar.activation(coef_rows[:, :, :, :], coef_rows[:, :, :, :], ACT.Exp).then_inc(e["h_c_exp"], 1)
                    act.wait_ge(e["h_cT_ready"], 1)
                    nc.scalar.activation(coef[:, 0, :], ps_c[1][:, :], ACT.Copy).then_inc(e["h_c_high"], 1)

                @block.vector
                def _(dve):
                    done = 0

                    def link(ins):
                        nonlocal done
                        done += 1
                        ins.then_inc(e["h_chain"], 1)
                        dve.wait_ge(e["h_chain"], done)

                    dve.wait_ge(e["h_hT_ready"], 1)
                    nc.vector.tensor_copy(hT[:, :], ps_c[0][:, :]).then_inc(e["h_hT_copied"], 1)
                    dve.wait_ge(e["h_s_copied"], 1)
                    link(nc.vector.scalar_tensor_tensor(logits[:, :], logits[:, :], 0.2, logits[:, :], ALU.mult, ALU.max))
                    link(nc.vector.tensor_tensor(logits[:, :], logits[:, :], maskT[:, :], ALU.mult))
                    link(nc.vector.tensor_tensor_reduce(out=logits[:, :], in0=logits[:, :], in1=fenceT[:, :], scale=1.0, scalar=LOWEST,
                                                        op0=ALU.add, op1=ALU.max, accum_out=row_max[:, :]))
                    nc.vector.tensor_scalar(neg_max[:, :], row_max[:, :], -1.0, None, ALU.mult).then_inc(e["h_a_masked"], 1)
                    dve.wait_ge(e["h_hT_copied"], 1)
                    nc.vector.tensor_scalar(half_hT[:, :], hT[:, :], 0.5, None, ALU.mult).then_inc(e["h_half_made"], 1)
                    dve.wait_ge(e["h_a_exp"], 1)
                    nc.vector.reciprocal(row_inv[:, :], row_sum[:, :]).then_inc(e["h_a_inv"], 1)
                    if not first:
                        normalise(dve, e, 0)
                    dve.wait_ge(e["h_agg_ready"], 1)
                    dve.wait_ge(e["h_a_inv"], 1)
                    for k in range(2):
                        half = slice(k * C, (k + 1) * C)
                        nc.vector.tensor_scalar(agg_diag[half, half], ps_m[half, half], row_inv[half, :], None, ALU.mult).then_inc(e["h_agg_scaled"], 1)
                    dve.wait_ge(e["h_aggT_ready"], 1)
                    for k in range(2):
                        half = slice(k * C, (k + 1) * C)
                        nc.vector.tensor_copy(aggT[half, :], ps_c[1][half, half]).then_inc(e["h_aggT_copied"], 1)
                    dve.wait_ge(e["h_aggT_copied"], 2)
                    nc.vector.tensor_scalar(below[:, :], aggT[:, :], 0.0, None, ALU.min).then_inc(e["h_he_below"], 1)
                    link(nc.vector.tensor_scalar(above[:, :], aggT[:, :], 0.0, None, ALU.max))
                    link(nc.vector.tensor_copy(edge_table[:, :, 1], aggT[:, :]))
                    link(nc.vector.tensor_scalar(edge_table[:, :, 2], aggT[:, :], 0.5, None, ALU.mult))
                    dve.wait_ge(e["h_he_exp"], 1)
                    nc.vector.scalar_tensor_tensor(he[:, :], below[:, :], -1.0, above[:, :], ALU.add, ALU.add).then_inc(e["h_he_ready"], 1)
                    if not first:
                        normalise(dve, e, 1)
                    dve.wait_ge(e["h_se_copied"], 1)
                    rows = coef_rows[:, :, :, :]
                    for k in range(2):
                        link(nc.vector.tensor_tensor(coef_rows[:, :, k, :], mask_rows[:, :, :],
                                                     se_all[:, k, :].unsqueeze(1).broadcast_to([P, NT, EDGES]), ALU.mult))
                        link(nc.vector.tensor_tensor(coef_rows[:, :, k, :], coef_rows[:, :, k, :], fence_rows[:, :, :], ALU.add))
                    flat = rows.rearrange("p t k e -> p (t k) e")
                    link(nc.vector.tensor_reduce(max2[:, :], flat, AX.X, ALU.max))
                    nc.vector.tensor_tensor(flat, flat, max2[:, :].unsqueeze(2).broadcast_to([P, 2 * NT, EDGES]), ALU.subtract).then_inc(e["h_c_shifted"], 1)
                    dve.wait_ge(e["h_c_exp"], 1)
                    link(nc.vector.tensor_reduce(sum2[:, :], flat, AX.X, ALU.add))
                    link(nc.vector.reciprocal(inv2[:, :], sum2[:, :]))
                    nc.vector.tensor_tensor(flat, flat, inv2[:, :].unsqueeze(2).broadcast_to([P, 2 * NT, EDGES]), ALU.mult).then_inc(e["h_c_ready"], 1)
                    dve.wait_ge(e["h_ind_ready"], 1)
                    nc.vector.tensor_tensor(indT[:, :], ps_g[:, :], inv_degree[:, :], ALU.mult).then_inc(e["h_ind_copied"], 1)
                    dve.wait_ge(e["h_c_high"], 1)
                    link(nc.vector.tensor_tensor(coef_rest[:, :], ps_c[1][:, :], coef[:, 0, :], ALU.subtract))
                    link(nc.vector.tensor_copy(coef[:, 1, :], coef_rest[:, :]))
                    link(nc.vector.tensor_tensor(coef[:, 2, :], coef_rest[:, :], coef[:, 1, :], ALU.subtract))
            nc.all_engine_barrier(sems_to_clear=numbers(e))

            with nc.Block() as block:
                f = loop

                def rounds(eng, step):
                    for j in range(UNROLL):
                        step(j, j)
                    with eng.Fori(1, EDGES // UNROLL - 1) as turn:
                        for j in range(UNROLL):
                            step(UNROLL * turn + j, j)
                    for j in range(UNROLL):
                        step(EDGES - UNROLL + j, j)

                def past(edge, least):
                    return not isinstance(edge, int) or edge >= least

                @block.gpsimd
                def _(pool):
                    nc.gpsimd.tensor_tensor(pool_waiter[:, :], ident[:, 0:1], ident[:, 0:1], ALU.add).then_inc(f["h_turn"], 1)

                    def step(edge, j):
                        if past(edge, UNROLL):
                            pool.wait_ge(f["h_turn"], edge - UNROLL + 1)
                            pool.wait_ge(f["h_relu_ready"], edge - UNROLL + 1)
                            nc.gpsimd.tensor_tensor(pool_waiter[:, :], ident[:, 0:1], ident[:, 0:1], ALU.add).then_inc(f["h_turn"], 1)
                        nc.gpsimd.tensor_copy(edge_now[j][:, :], edge_table[:, edge, :]).then_inc(f["h_edge_copied"], 1)
                        pool.wait_ge(f["h_edge_copied"], edge + 1)
                        if past(edge, 2):
                            pool.wait_ge(f["h_shift_ready"], edge - 1)
                        nc.gpsimd.tensor_tensor(diff[j % 2][:, :], half_hT[:, :], edge_now[j][:, 2:3].broadcast_to([P, N]),
                                                ALU.subtract).then_inc(f["h_diff_ready"], 1)
                    rounds(pool, step)

                @block.scalar
                def _(act):
                    def make_gate(edge, j):
                        act.wait_ge(f["h_edge_copied"], edge + 1)
                        if past(edge, 2):
                            act.wait_ge(f["h_shift_ready"], edge - 1)
                        nc.scalar.activation(gate[j % 2][:, :], gate_h[:, :], ACT.Tanh, bias=edge_now[j % UNROLL][:, 0:1]).then_inc(f["h_gate_ready"], 1)

                    def functions(edge, j):
                        act.wait_ge(f["h_shift_ready"], edge + 1)
                        if past(edge, 2):
                            act.wait_ge(f["h_f_ready"], edge - 1)
                        agg = edge_now[j % UNROLL][:, 1:2]
                        nc.scalar.activation(expv[j % 2][:, :], shifted[j % 2][:, :], ACT.Exp, bias=agg).then_inc(f["h_exp_ready"], 1)
                        nc.scalar.activation(reluv[j % 2][:, :], shifted[j % 2][:, :], ACT.Relu, bias=agg).then_inc(f["h_relu_ready"], 1)

                    def step(edge, j):
                        if not isinstance(edge, int) or edge + 2 < EDGES:
                            make_gate(edge + 2, j + 2)
                        if not isinstance(edge, int) or edge + 1 < EDGES:
                            functions(edge + 1, j + 1)

                    make_gate(0, 0)
                    make_gate(1, 1)
                    functions(0, 0)
                    rounds(act, step)

                @block.vector
                def _(dve):
                    def shift(edge, j):
                        dve.wait_ge(f["h_diff_ready"], edge + 1)
                        dve.wait_ge(f["h_gate_ready"], edge + 1)
                        if past(edge, 2):
                            dve.wait_ge(f["h_relu_ready"], edge - 1)
                        nc.vector.scalar_tensor_tensor(shifted[j % 2][:, :], gate[j % 2][:, :], 1.0, diff[j % 2][:, :],
                                                       ALU.add, ALU.mult).then_inc(f["h_shift_ready"], 1)

                    def step(edge, j):
                        if not isinstance(edge, int) or edge + 1 < EDGES:
                            shift(edge + 1, j + 1)
                        dve.wait_ge(f["h_relu_ready"], edge + 1)
                        nc.vector.scalar_tensor_tensor(reluv[j % 2][:, :], expv[j % 2][:, :], 1.0, reluv[j % 2][:, :],
                                                       ALU.min, ALU.add).then_inc(f["h_w_ready"], 1)
                        dve.wait_ge(f["h_w_ready"], edge + 1)
                        dve.wait_ge(f["h_spread_ready"], edge + 1)
                        if past(edge, 2):
                            dve.wait_ge(f["h_added"], edge - 1)
                        nc.vector.tensor_tensor(weighted[j % 2][:, :], reluv[j % 2][:, :], ps_c[j % 2][:, :], ALU.mult).then_inc(f["h_f_ready"], 1)

                    shift(0, 0)
                    rounds(dve, step)

                @block.tensor
                def _(pe):
                    def spread(edge, j):
                        for m in range(2):
                            cols = slice(m * HN, (m + 1) * HN)
                            for part in range(3):
                                mm = nc.tensor.matmul(ps_c[j % 2][:, cols], pick[:, edge, :], coef[:, part, cols],
                                                      start=(part == 0), stop=(part == 2))
                        mm.then_inc(f["h_spread_ready"], 1)

                    def step(edge, j):
                        pe.wait_ge(f["h_f_ready"], edge + 1)
                        first = isinstance(edge, int) and edge == 0
                        last = isinstance(edge, int) and edge == EDGES - 1
                        for m in range(2):
                            cols = slice(m * HN, (m + 1) * HN)
                            mm = nc.tensor.matmul(ps_g[:, cols], ident[:, :], weighted[j % 2][:, cols], start=first, stop=last)
                        mm.then_inc(f["h_added"], 1)
                        if not isinstance(edge, int) or edge + 2 < EDGES:
                            spread(edge + 2, j + 2)

                    spread(0, 0)
                    spread(1, 1)
                    rounds(pe, step)
            nc.all_engine_barrier(sems_to_clear=numbers(loop))

            with nc.Block() as block:
                q = post
                gT, outT, d_tanh = diff[0], diff[1], gate[0]
                zt = [[shifted[0], shifted[1]], [expv[0], expv[1]]]
                @block.vector
                def _(dve):
                    nc.vector.tensor_scalar(gT[:, :], ps_g[:, :], -1.0, None, ALU.add).then_inc(q["h_g_ready"], 1)
                    dve.wait_ge(q["h_g_ready"], 1)
                    nc.vector.tensor_tensor(outT[:, :], gT[:, :], indT[:, :], ALU.subtract).then_inc(q["h_g_ready"], 1)
                    done = 0

                    def link(ins):
                        nonlocal done
                        done += 1
                        ins.then_inc(q["h_norm"], 1)
                        dve.wait_ge(q["h_norm"], done)

                    dve.wait_ge(q["h_d_tanh"], 1)
                    dve.wait_ge(q["h_g_ready"], 2)
                    link(nc.vector.scalar_tensor_tensor(outT[:, :], d_tanh[:, :], 1.0, outT[:, :], ALU.add, ALU.mult))
                    nc.vector.scalar_tensor_tensor(outT[:, :], outT[:, :], 0.5, indT[:, :], ALU.mult, ALU.add).then_inc(q["h_o_ready"], 1)
                    dve.wait_ge(q["h_oT_ready"], 1)
                    nc.vector.tensor_tensor(y, ps_c[0][:, :].rearrange("p (t c) -> p t c", c=C),
                                            x_rows[:, :, :, :].rearrange("p t k c -> p (t k) c"), ALU.add).then_inc(q["h_y_ready"], 1)

                @block.tensor
                def _(pe):
                    for k in range(2):
                        half = slice(k * C, (k + 1) * C)
                        if k == 1:
                            pe.wait_ge(q["h_za_tanh"], 1)
                        for m in range(2):
                            cols = slice(m * HN, (m + 1) * HN)
                            mm = nc.tensor.matmul(ps_c[0][:, cols], fcW[half, :], indT[half, cols], start=True, stop=True)
                        mm.then_inc(q["h_za_ready"], 1)
                        if k == 0:
                            pe.wait_ge(q["h_g_ready"], 1)
                        else:
                            pe.wait_ge(q["h_zb_tanh"], 1)
                        for m in range(2):
                            cols = slice(m * HN, (m + 1) * HN)
                            mm = nc.tensor.matmul(ps_c[1][:, cols], fcW[half, :], gT[half, cols], start=True, stop=True)
                        mm.then_inc(q["h_zb_ready"], 1)
                    pe.wait_ge(q["h_za_tanh"], 2)
                    pe.wait_ge(q["h_zb_tanh"], 2)
                    for m in range(2):
                        cols = slice(m * HN, (m + 1) * HN)
                        for i in range(4):
                            kind, k = i // 2, i % 2
                            mm = nc.tensor.matmul(ps_m[:, cols], av_pair[:, kind, k, :], zt[kind][k][:, cols], start=(i == 0), stop=(i == 3))
                    mm.then_inc(q["h_d_ready"], 1)
                    pe.wait_ge(q["h_o_ready"], 1)
                    for t in range(NT):
                        mm = nc.tensor.transpose(ps_c[0][:, t * P:(t + 1) * P], outT[:, t * P:(t + 1) * P], ident[:, :])
                    mm.then_inc(q["h_oT_ready"], 1)

                @block.scalar
                def _(act):
                    for k in range(2):
                        act.wait_ge(q["h_za_ready"], k + 1)
                        nc.scalar.activation(zt[0][k][:, :], ps_c[0][:, :], ACT.Tanh, bias=fcb[:, :]).then_inc(q["h_za_tanh"], 1)
                        act.wait_ge(q["h_zb_ready"], k + 1)
                        nc.scalar.activation(zt[1][k][:, :], ps_c[1][:, :], ACT.Tanh, bias=fcb[:, :]).then_inc(q["h_zb_tanh"], 1)
                    act.wait_ge(q["h_d_ready"], 1)
                    nc.scalar.activation(d_tanh[:, :], ps_m[:, :], ACT.Tanh).then_inc(q["h_d_tanh"], 1)
            nc.all_engine_barrier(sems_to_clear=numbers(post))

        batch_pair(0, first=True)
        with nc.Fori(1, PAIRS) as pair:
            batch_pair(pair)
        with nc.Block() as block:

            @block.sync
            def _(sp):
                store(sp, post, PAIRS - 1)

            @block.gpsimd
            def _(pool):
                raise_variance(pool, post)

            @block.vector
            def _(dve):
                normalise(dve, post)
        nc.all_engine_barrier(sems_to_clear=numbers(post))


def multi_head_gat(nc, bank, io, weighted, x_in, x_out):
    ctx = ExitStack()
    with ctx:
        def sb(name, shape, dt=F32):
            return ctx.enter_context(nc.sbuf_tensor(name, shape, dt))

        def pb(name, shape):
            return ctx.enter_context(nc.psum_tensor(name, shape, F32))

        ident = sb("g_ident", [P, P])
        ident2 = sb("g_ident2", [P, C])
        graph = sb("g_graph", [P, NT, N])
        fence = sb("g_fence", [P, NT, N], BF16)
        A_table = sb("g_A_table", [P, HEADS, 2, P], F32R)
        W_table = sb("g_W_table", [P, HEADS, 2 * P + 1])
        b_out_row = sb("g_b_out_row", [P, C])
        A_cur = [sb(f"g_A_cur{k}", [P, 2, P], F32R) for k in range(2)]
        W_cur = [sb(f"g_W_cur{k}", [P, 2 * P + 1]) for k in range(2)]
        x_rows = sb("g_x_rows", [P, NT, 2 * C])
        x_again = sb("g_x_again", [P, NT, C])
        moving_hi = sb("g_moving_hi", [P, N], F32R)
        moving_lo = sb("g_moving_lo", [P, N], F32R)
        moving_hl = sb("g_moving_hl", [P, N], F32R)
        value_hl = sb("g_value_hl", [P, NT, P], F32R)
        query = [sb(f"g_query{k}", [P, N], F32R) for k in range(2)]
        other_hi = sb("g_other_hi", [P, N], F32R)
        other_lo = sb("g_other_lo", [P, N], F32R)
        other_hl = sb("g_other_hl", [P, N], F32R)
        other_value = sb("g_other_value", [P, NT, P], F32R)
        SLOTS = 4
        tile = [sb(f"g_tile{k}", [P, N]) for k in range(SLOTS)]
        row_max = [sb(f"g_row_max{k}", [P, 1]) for k in range(SLOTS)]
        neg_max = [sb(f"g_neg_max{k}", [P, 1]) for k in range(SLOTS)]
        waiter = sb("g_waiter", [P, 1])
        pool_waiter = sb("g_pool_waiter", [P, 1])
        row_sum = sb("g_row_sum", [P, NT])
        row_inv = sb("g_row_inv", [P, NT])
        pt_hi = [sb(f"g_pt_hi{k}", [P, NT, HN], F32R) for k in range(2)]
        pt_lo = [sb(f"g_pt_lo{k}", [P, NT, HN], F32R) for k in range(2)]
        mixed = sb("g_mixed", [P, HN])
        mixed_n = sb("g_mixed_n", [P, HN])
        cat = sb("g_cat", [P, HN])
        hidden = sb("g_hidden", [P, N])
        y = sb("g_y", [P, NT, C])
        sq = x_again
        mean = sb("g_mean", [P, NT])
        var = sb("g_var", [P, NT])
        rstd = sb("g_rstd", [P, NT])
        minus_half = sb("g_minus_half", [P, NT])

        ps_s = [pb(f"g_ps_s{k}", [P, N]) for k in range(2)]
        ps_t = [pb(f"g_ps_t{k}", [P, HN]) for k in range(2)]
        ps_u = pb("g_ps_u", [P, HN])
        ps_x = pb("g_ps_x", [P, HN])

        w_head = tile[2][:, :].rearrange("p (h d) -> p h d", d=HC)
        setup = events(bank, "g_loaded g_zeroed g_ident_ready g_ident2_ready g_graph_zero "
                                "g_fence_ready g_wT_ready g_wT_copied g_A_ready "
                                "g_A_high g_A_rest g_W_packed g_half_ready")
        with nc.Block() as block:
            e = setup

            @block.sync
            def _(sp):
                sp.dma_start(graph[:, :, :], io["adj"].rearrange("(t p) m -> p t m", p=P)).then_inc(e["g_loaded"], 16)
                for k in range(2):
                    half = slice(k * C, (k + 1) * C)
                    sp.dma_start(w_head[half, :, :], io["L1_gnn_Wh"].rearrange("h c d -> c h d")).then_inc(e["g_loaded"], 16)
                    sp.dma_start(W_table[:, :, P + k * C:P + (k + 1) * C],
                                 io["L1_gnn_W_out"].rearrange("(h d) c -> d h c", d=HC)).then_inc(e["g_loaded"], 16)
                sp.dma_start(W_table[:, :, 2 * P:2 * P + 1],
                             io["L1_gnn_bh"].rearrange("h (d o) -> d h o", o=1),
                             allow_slow_non_contiguous=True).then_inc(e["g_loaded"], 16)
                sp.dma_start(b_out_row[:, :], io["L1_gnn_b_out"].partition_broadcast(P)).then_inc(e["g_loaded"], 16)

            @block.gpsimd
            def _(pool):
                make_identity(pool, ident, e["g_zeroed"], e["g_ident_ready"], 0)
                nc.gpsimd.memset(minus_half[:, :], -0.5).then_inc(e["g_half_ready"], 1)

            @block.vector
            def _(dve):
                dve.wait_ge(e["g_ident_ready"], 1)
                nc.vector.tensor_tensor(ident2[:, :], ident[:, 0:C], ident[:, C:2 * C], ALU.add).then_inc(e["g_ident2_ready"], 1)
                dve.wait_ge(e["g_loaded"], 16 * 7)
                for t in range(NT):
                    nc.vector.tensor_scalar(tile[t % 2][:, :], graph[:, t, :], 0.0, None, ALU.is_equal).then_inc(e["g_graph_zero"], 1)
                    dve.wait_ge(e["g_graph_zero"], t + 1)
                    nc.vector.tensor_scalar(fence[:, t, :], tile[t % 2][:, :], MASKED, None, ALU.mult).then_inc(e["g_fence_ready"], 1)
                nc.vector.tensor_copy(W_table[:, :, 0:P], w_head).then_inc(e["g_W_packed"], 1)
                dve.wait_ge(e["g_wT_ready"], 1)
                nc.vector.tensor_copy(tile[0][:, :], ps_s[0][:, :]).then_inc(e["g_wT_copied"], 1)
                dve.wait_ge(e["g_A_ready"], 1)
                for h in range(HEADS):
                    nc.vector.tensor_copy(A_table[:, h, 0, :], ps_s[1][:, h * P:(h + 1) * P]).then_inc(e["g_A_high"], 1)
                    dve.wait_ge(e["g_A_high"], h + 1)
                    nc.vector.tensor_tensor(A_table[:, h, 1, :], ps_s[1][:, h * P:(h + 1) * P],
                                            A_table[:, h, 0, :].bitcast(F32), ALU.subtract).then_inc(e["g_A_rest"], 1)

            @block.tensor
            def _(pe):
                pe.wait_ge(e["g_loaded"], 16 * 7)
                pe.wait_ge(e["g_ident_ready"], 1)
                for h in range(HEADS):
                    mm = nc.tensor.transpose(ps_s[0][:, h * P:(h + 1) * P], w_head[:, h, :], ident[:, :])
                mm.then_inc(e["g_wT_ready"], 1)
                pe.wait_ge(e["g_wT_copied"], 1)
                for h in range(HEADS):
                    wT = tile[0][:, h * P:(h + 1) * P]
                    mm = nc.tensor.matmul(ps_s[1][:, h * P:(h + 1) * P], wT, wT, start=True, stop=True)
                mm.then_inc(e["g_A_ready"], 1)
        nc.all_engine_barrier(sems_to_clear=numbers(setup))

        names = ("g_x_loaded g_r_loaded g_xT_ready g_x_high g_x_rest g_o_stacked g_main_hi g_main_lo g_main_hl g_v_high g_v_rest "
                 "g_s_ready g_g_ready g_m_ready g_t_ready g_p_ready g_pt_ready g_hi_ready g_lo_ready g_u_ready "
                 "g_ut_ready g_ri_ready g_rb_ready g_un_ready g_cat_ready g_vb_ready g_v_ready g_hp_ready "
                 "g_hacc_ready g_y_ready g_yr_ready g_y2_ready g_wa_ready g_ww_ready g_turn "
                 "g_h_high g_h_rest g_hT_ready g_hT_copied g_o_ready g_o_used g_norm g_square g_var_ready g_rstd_ready "
                 "g_y_done g_stored")
        e = events(bank, names)
        AHEAD = 3
        NEXT = HEADS
        xin = x_in.rearrange("b (t p) c -> b p t c", p=P)
        xout = x_out.rearrange("b (t p) c -> b p t c", p=P)

        def is_out(h):
            return isinstance(h, str)

        def is_int(h, number):
            return isinstance(h, int) and h == number

        def load_x(sp, b):
            for k in range(2):
                sp.dma_start(x_rows[:, :, k * C:(k + 1) * C], xin[b]).then_inc(e["g_x_loaded"], 16)

        def transpose_x(half):
            for j in range(4):
                mm = nc.tensor.transpose(ps_x[:, j * P:(j + 1) * P], x_rows[:, 4 * half + j, :], ident[:, :])
            mm.then_inc(e["g_xT_ready"], 1)

        def x_high(act, half):
            act.wait_ge(e["g_xT_ready"], half + 1)
            nc.scalar.activation(other_hi[:, half * HN:(half + 1) * HN], ps_x[:, :], ACT.Copy).then_inc(e["g_x_high"], 1)

        def x_rest(dve, half):
            cols = slice(half * HN, (half + 1) * HN)
            dve.wait_ge(e["g_x_high"], half + 1)
            nc.vector.tensor_tensor(other_lo[:, cols], ps_x[:, :], other_hi[:, cols].bitcast(F32), ALU.subtract).then_inc(e["g_x_rest"], 1)

        def stack_other(pool, turn, prior, prior_count):
            pool.wait_ge(prior, prior_count)
            nc.gpsimd.tensor_copy(other_hl[0:C, :], other_hi[0:C, :].bitcast(F32)).then_inc(e["g_o_stacked"], 1)
            pool.wait_ge(e["g_o_stacked"], 2 * turn + 1)
            nc.gpsimd.tensor_copy(other_hl[C:P, :], other_lo[C:P, :].bitcast(F32)).then_inc(e["g_o_stacked"], 1)
            pool.wait_ge(e["g_o_stacked"], 2 * turn + 2)

        def query_product(k, half, moving):
            cols = slice(half * HN, (half + 1) * HN)
            nc.tensor.matmul(ps_x[:, :], A_cur[k][:, 0, :], moving[:, cols], start=True, stop=False)
            nc.tensor.matmul(ps_x[:, :], A_cur[k][:, 1, :], moving[:, cols], start=False, stop=True).then_inc(e["g_y_ready"], 1)

        def query_high(k, half):
            nc.scalar.activation(query[k][:, half * HN:(half + 1) * HN], ps_x[:, :], ACT.Copy).then_inc(e["g_yr_ready"], 1)

        def query_rest(k, half):
            cols = slice(half * HN, (half + 1) * HN)
            nc.vector.tensor_tensor(query[k][C:P, cols], ps_x[C:P, :], query[k][C:P, cols].bitcast(F32),
                                    ALU.subtract).then_inc(e["g_y2_ready"], 1)

        with nc.Block() as block:

            @block.sync
            def _(sp):
                load_x(sp, 0)

            @block.gpsimd
            def _(pool):
                nc.gpsimd.tensor_copy(A_cur[0][:, :, :], A_table[:, 0, :, :]).then_inc(e["g_wa_ready"], 1)
                pool.wait_ge(e["g_x_rest"], 2)
                stack_other(pool, 0, e["g_wa_ready"], 1)

            @block.tensor
            def _(pe):
                pe.wait_ge(e["g_x_loaded"], 32)
                transpose_x(0)
                pe.wait_ge(e["g_x_rest"], 1)
                transpose_x(1)
                pe.wait_ge(e["g_wa_ready"], 1)
                pe.wait_ge(e["g_o_stacked"], 2)
                query_product(0, 0, other_hl)
                pe.wait_ge(e["g_y2_ready"], 1)
                query_product(0, 1, other_hl)

            @block.scalar
            def _(act):
                for half in range(2):
                    x_high(act, half)
                for half in range(2):
                    act.wait_ge(e["g_y_ready"], half + 1)
                    query_high(0, half)

            @block.vector
            def _(dve):
                for half in range(2):
                    x_rest(dve, half)
                for half in range(2):
                    dve.wait_ge(e["g_yr_ready"], half + 1)
                    query_rest(0, half)
        nc.all_engine_barrier(sems_to_clear=numbers(e))

        def element(b, first=False, last=False):
            before = 0 if first else 1
            LATER = 2 + before

            def unit(h):
                return h + before if not isinstance(h, int) or h >= 2 else h

            OUT = 2
            END = unit(HEADS - 1)
            FINAL = END + 1
            def program(run, loop):
                run(0, 0, "head" if before else None, 1, -1)
                run(1, 1, "head", 2 if first else "out", 0)
                if not first:
                    run(OUT, "out", "head", 2, 1)
                run(LATER, 2, "head" if first else "out", 3, 1)
                with loop(0, (HEADS - 4) // 2) as pair:
                    run(2 * pair + 3 + before, 2 * pair + 3, "head", 2 * pair + 4, 2 * pair + 2, k=1, looped=True)
                    run(2 * pair + 4 + before, 2 * pair + 4, "head", 2 * pair + 5, 2 * pair + 3, k=0, looped=True)
                run(END, HEADS - 1, "head", None, HEADS - 2)

            def parity(h, k):
                return h % 2 if isinstance(h, int) else k

            with nc.Block() as block:

                @block.sync
                def _(sp):
                    if not first:
                        sp.dma_start(x_again[:, :, :], xin[b - 1]).then_inc(e["g_r_loaded"], 16)
                    if not last:
                        sp.wait_ge(e["g_v_rest"], 1)
                        load_x(sp, b + 1)
                    if not first:
                        sp.wait_ge(e["g_y_done"], 1)
                        sp.dma_start(xout[b - 1], y[:, :, :]).then_inc(e["g_stored"], 16)
                    if last:
                        sp.dma_start(x_again[:, :, :], xin[b]).then_inc(e["g_r_loaded"], 16)
                        sp.wait_ge(e["g_y_done"], 2)
                        sp.dma_start(xout[b], y[:, :, :]).then_inc(e["g_stored"], 16)
                    if not first:
                        sp.wait_ge(e["g_stored"], 32 if last else 16)

                @block.gpsimd
                def _(pool):
                    def wait_turn(number, signal, count):
                        pool.wait_ge(signal, count)
                        nc.gpsimd.tensor_tensor(pool_waiter[:, :], ident[:, 0:1], ident[:, 0:1], ALU.add).then_inc(e["g_turn"], 1)
                        pool.wait_ge(e["g_turn"], number)

                    def load_A(h, k):
                        nc.gpsimd.tensor_copy(A_cur[k][:, :, :], A_table[:, h, :, :]).then_inc(e["g_wa_ready"], 1)

                    def load_W(h, k):
                        nc.gpsimd.tensor_copy(W_cur[k][:, :], W_table[:, h, :]).then_inc(e["g_ww_ready"], 1)

                    def run(u, h, came, behind, h_before, k=0, looped=False):
                        k = parity(h, k) if not is_out(h) else None
                        for i in range(NT):
                            if i == 0 and not is_out(h) and (looped or 1 <= h):
                                if looped:
                                    wait_turn(2 * h - 5, e["g_y_ready"], 2 * h - 2)
                                elif h >= 2:
                                    pool.wait_ge(e["g_y_ready"], 2 * h - 2)
                                if looped or h + 1 < HEADS:
                                    load_A(h + 1, 1 - k)
                                elif not last:
                                    load_A(0, 1 - k)
                            if i == 3 and not is_out(h) and (looped or h >= 1):
                                done = 2 * h - 2 + 2 * before
                                if looped:
                                    wait_turn(2 * h - 4, e["g_hp_ready"], done)
                                elif done > 0:
                                    pool.wait_ge(e["g_hp_ready"], done)
                                load_W(h, k)
                            if i == 4 and is_out(behind):
                                pool.wait_ge(e["g_h_rest"], 1)
                                stack_other(pool, 0, e["g_ww_ready"], 2)

                    nc.gpsimd.tensor_copy(moving_hl[:, :], other_hl[:, :].bitcast(F32)).then_inc(e["g_main_hl"], 1)
                    load_A(1, 1)
                    load_W(0, 0)
                    program(run, pool.Fori)
                    if not last:
                        pool.wait_ge(e["g_x_rest"], 2)
                        stack_other(pool, before, e["g_ww_ready"], HEADS)
                    if not first:
                        pool.wait_ge(e["g_var_ready"], 1)
                        nc.gpsimd.tensor_tensor(rstd[:, :], var[:, :], minus_half[:, :], ALU.pow).then_inc(e["g_rstd_ready"], 1)
                    if last:
                        pool.wait_ge(e["g_h_rest"], 2)
                        stack_other(pool, 1, e["g_rstd_ready"], 1)
                        pool.wait_ge(e["g_var_ready"], 2)
                        nc.gpsimd.tensor_tensor(rstd[:, :], var[:, :], minus_half[:, :], ALU.pow).then_inc(e["g_rstd_ready"], 1)

                @block.tensor
                def _(pe):
                    def score(u, h, i, k):
                        n = 8 * u + i
                        if not isinstance(n, int) or n >= 2:
                            pe.wait_ge(e["g_m_ready"], n - 1)
                        if is_out(h):
                            queries, high, low = other_hl, other_hi, other_lo
                        else:
                            queries, high, low = query[k], moving_hi, moving_lo
                            if i % 4 == 0 and not (isinstance(h, int) and h == 0):
                                pe.wait_ge(e["g_y2_ready"], 2 * h - 1 + i // 4)
                        for m in range(2):
                            cols = slice(m * HN, (m + 1) * HN)
                            rows = slice(i * P, (i + 1) * P)
                            nc.tensor.matmul(ps_s[i % 2][:, cols], queries[:, rows], high[:, cols], start=True, stop=False)
                            mm = nc.tensor.matmul(ps_s[i % 2][:, cols], queries[:, rows], low[:, cols], start=False, stop=True)
                        mm.then_inc(e["g_s_ready"], 1)

                    def transpose(u, i):
                        n = 8 * u + i
                        pe.wait_ge(e["g_p_ready"], n + 1)
                        for a in range(2):
                            if not isinstance(n, int) or n >= 1:
                                pe.wait_ge(e["g_lo_ready"], 2 * n + a - 1)
                            for j in range(4):
                                m = 4 * a + j
                                mm = nc.tensor.transpose(ps_t[a][:, j * P:(j + 1) * P],
                                                         tile[i % SLOTS][:, m * P:(m + 1) * P], ident[:, :])
                            mm.then_inc(e["g_pt_ready"], 1)

                    def mix(u, h, half, chunk):
                        values = other_value if is_out(h) else value_hl
                        if chunk == 0:
                            pe.wait_ge(e["g_lo_ready"], 16 * u + 8 * half + 8)
                            if not (isinstance(u, int) and 2 * u + half + before == 0):
                                pe.wait_ge(e["g_ut_ready"], 2 * u + half + before)
                        for j in range(3 * chunk, min(3 * chunk + 3, NT)):
                            nc.tensor.matmul(ps_u[:, :], values[:, j, :], pt_hi[half][:, j, :], start=(j == 0), stop=False)
                            mm = nc.tensor.matmul(ps_u[:, :], values[:, j, :], pt_lo[half][:, j, :], start=False, stop=(j == NT - 1))
                        if chunk == 2:
                            mm.then_inc(e["g_u_ready"], 1)

                    def spread_inverse(u, half):
                        if u is not None:
                            pe.wait_ge(e["g_ri_ready"], 2 * u + half + 1)
                        for j in range(4):
                            i = 4 * half + j
                            mm = nc.tensor.matmul(ps_x[:, j * P:(j + 1) * P], row_inv[:, i:i + 1].broadcast_to([P, P]), ident[:, :],
                                                  start=True, stop=True)
                        mm.then_inc(e["g_rb_ready"], 1)

                    def project(h, half, k):
                        if not (isinstance(h, int) and h < 0):
                            pe.wait_ge(e["g_ww_ready"], h + 1)
                        pe.wait_ge(e["g_un_ready"], 2 * (h + before) + half + 1)
                        nc.tensor.matmul(ps_x[:, :], W_cur[k][:, 0:P], mixed_n[:, :], start=True, stop=True).then_inc(e["g_cat_ready"], 1)

                    def project_out(h, half, k):
                        pe.wait_ge(e["g_v_ready"], 2 * (h + before) + half + 1)
                        nc.tensor.matmul(ps_x[:, :], W_cur[k][:, P:2 * P], cat[:, :], start=True, stop=True).then_inc(e["g_hp_ready"], 1)

                    def out_rows(u, half):
                        pe.wait_ge(e["g_ut_ready"], 2 * u + half + 1 + before)
                        for j in range(4):
                            mm = nc.tensor.matmul(ps_x[:, j * C:(j + 1) * C], mixed[:, j * P:(j + 1) * P], ident2[:, :],
                                                  start=True, stop=True)
                        mm.then_inc(e["g_o_ready"], 1)

                    def transpose_hidden(half):
                        for j in range(4):
                            i = 4 * half + j
                            mm = nc.tensor.transpose(ps_x[:, j * P:(j + 1) * P], other_hl[:, i * P:(i + 1) * P].bitcast(F32), ident[:, :])
                        mm.then_inc(e["g_hT_ready"], 1)

                    def run(u, h, came, behind, h_before, k=0, looped=False):
                        k = parity(h, k) if not is_out(h) else 0
                        kb = (1 - k) if not is_out(h) and not is_int(h, 2) else 1
                        kn = (1 - k) if not is_out(h) else 0
                        q = 2 * (h_before + before)
                        start_of_element = isinstance(u, int) and u == 0
                        for i in range(NT):
                            transpose(u, i)
                            if i + AHEAD < NT:
                                score(u, h, i + AHEAD, k)
                            elif behind is not None:
                                score(u + 1, behind, i + AHEAD - NT, kn)

                            if i == 0 and came == "head":
                                if u is not None and not start_of_element:
                                    if isinstance(q, int) and q == 0:
                                        pe.wait_ge(e["g_y2_ready"], 2)
                                    else:
                                        pe.wait_ge(e["g_hacc_ready"], q)
                                    if looped:
                                        if not first:
                                            pe.wait_ge(e["g_o_used"], 2)
                                spread_inverse(None if start_of_element else u - 1, 0)
                            if i == 0 and came == "out":
                                pe.wait_ge(e["g_hacc_ready"], q + 2)
                                out_rows(u - 1, 0)
                            if i == 1 and came == "head":
                                project(h_before, 0, kb)
                            if i == 2 and came == "head":
                                project_out(h_before, 0, kb)
                            if i == 3:
                                if came == "head":
                                    pe.wait_ge(e["g_hacc_ready"], q + 1)
                                elif came == "out":
                                    pe.wait_ge(e["g_o_used"], 1)
                                if is_out(behind):
                                    pe.wait_ge(e["g_o_stacked"], 2)
                                    transpose_hidden(0)
                                elif behind is not None:
                                    pe.wait_ge(e["g_wa_ready"], behind)
                                    if start_of_element:
                                        pe.wait_ge(e["g_main_hl"], 1)
                                    query_product(kn, 0, moving_hl)
                                elif not last:
                                    pe.wait_ge(e["g_x_loaded"], 32)
                                    transpose_x(0)
                            if i == 4:
                                if is_out(behind):
                                    pe.wait_ge(e["g_hT_copied"], 1)
                                    transpose_hidden(1)
                                elif behind is not None:
                                    pe.wait_ge(e["g_y2_ready"], 2 * behind - 1)
                                    query_product(kn, 1, moving_hl)
                                elif not last:
                                    pe.wait_ge(e["g_x_rest"], 1)
                                    transpose_x(1)
                            if i == 5 and came is not None:
                                if is_out(behind):
                                    pe.wait_ge(e["g_hT_copied"], 2)
                                elif behind is not None:
                                    pe.wait_ge(e["g_y2_ready"], 2 * behind)
                                elif not last:
                                    pe.wait_ge(e["g_x_rest"], 2)
                                if came == "head":
                                    spread_inverse(None if start_of_element else u - 1, 1)
                                else:
                                    out_rows(u - 1, 1)
                            if i == 6 and came == "head":
                                project(h_before, 1, kb)
                            if i == 7 and came == "head":
                                project_out(h_before, 1, kb)
                            if i >= 5:
                                mix(u, h, 0, i - 5)
                            elif 1 <= i <= 3 and not start_of_element:
                                mix(u - 1, "out" if came == "out" else h_before, 1, i - 1)

                    pe.wait_ge(e["g_main_hi"], 1)
                    pe.wait_ge(e["g_main_lo"], 1)
                    pe.wait_ge(e["g_v_rest"], 1)
                    for i in range(AHEAD):
                        score(0, 0, i, 0)
                    program(run, pe.Fori)
                    collected = 2 * (HEADS - 1 + before)
                    if not last:
                        pe.wait_ge(e["g_wa_ready"], NEXT)
                        pe.wait_ge(e["g_o_stacked"], 2 if first else 4)
                        pe.wait_ge(e["g_hacc_ready"], collected)
                        query_product(0, 0, other_hl)
                        pe.wait_ge(e["g_y2_ready"], 2 * NEXT - 1)
                        query_product(0, 1, other_hl)
                        for chunk in range(3):
                            mix(END, HEADS - 1, 1, chunk)
                    else:
                        for half in range(2):
                            if half == 1:
                                for chunk in range(3):
                                    mix(END, HEADS - 1, 1, chunk)
                            pe.wait_ge(e["g_hacc_ready"], collected + half)
                            spread_inverse(END, half)
                            project(HEADS - 1, half, 1)
                            project_out(HEADS - 1, half, 1)
                        pe.wait_ge(e["g_hacc_ready"], collected + 2)
                        pe.wait_ge(e["g_o_stacked"], 4)
                        for i in range(2):
                            score(FINAL, "out", i, 0)
                        transpose_hidden(0)
                        pe.wait_ge(e["g_hT_copied"], 3)
                        transpose_hidden(1)
                        score(FINAL, "out", 2, 0)
                        for i in range(NT):
                            transpose(FINAL, i)
                            if i + AHEAD < NT:
                                score(FINAL, "out", i + AHEAD, 0)
                            if i == 5:
                                pe.wait_ge(e["g_hT_copied"], 4)
                            if i >= 5:
                                mix(FINAL, "out", 0, i - 5)
                        for half in range(2):
                            if half == 1:
                                for chunk in range(3):
                                    mix(FINAL, "out", 1, chunk)
                                pe.wait_ge(e["g_o_used"], 3)
                            out_rows(FINAL, half)

                @block.scalar
                def _(act):
                    def exponentials(u, i):
                        act.wait_ge(e["g_t_ready"], 8 * u + i + 1)
                        k = i % SLOTS
                        nc.scalar.activation(tile[k][:, :], tile[k][:, :], ACT.Exp, bias=neg_max[k][:, :],
                                             accum_out=row_sum[:, i:i + 1]).then_inc(e["g_p_ready"], 1)

                    def high(u, i):
                        n = 8 * u + i
                        half, j = i // 4, i % 4
                        for a in range(2):
                            if j == 0 and a == 0 and not (isinstance(u, int) and u == 0):
                                act.wait_ge(e["g_u_ready"], 2 * u - 1 + half)
                            act.wait_ge(e["g_pt_ready"], 2 * n + a + 1)
                            nc.scalar.activation(pt_hi[half][:, 4 * a:4 * a + 4, j * P:(j + 1) * P],
                                                 ps_t[a][:, :].rearrange("p (m n) -> p m n", n=P), ACT.Copy).then_inc(e["g_hi_ready"], 1)

                    def take_mixed(u, half):
                        act.wait_ge(e["g_u_ready"], 2 * u + half + 1)
                        nc.scalar.activation(mixed[:, :], ps_u[:, :], ACT.Copy).then_inc(e["g_ut_ready"], 1)

                    def add_bias(h, half, k):
                        act.wait_ge(e["g_cat_ready"], 2 * (h + before) + half + 1)
                        nc.scalar.activation(cat[:, :], ps_x[:, :], ACT.Identity, bias=W_cur[k][:, 2 * P:2 * P + 1]).then_inc(e["g_vb_ready"], 1)

                    def round_queries(h, half, k):
                        act.wait_ge(e["g_y_ready"], 2 * h - 1 + half)
                        query_high(k, half)

                    def run(u, h, came, behind, h_before, k=0, looped=False):
                        k = parity(h, k) if not is_out(h) else 0
                        kb = (1 - k) if not is_out(h) and not is_int(h, 2) else 1
                        kn = (1 - k) if not is_out(h) else 0
                        start_of_element = isinstance(u, int) and u == 0
                        for i in range(NT):
                            if i + 1 < NT:
                                exponentials(u, i + 1)
                            elif behind is not None:
                                exponentials(u + 1, 0)
                            high(u, i)
                            if i == 0 and came is not None and not start_of_element:
                                take_mixed(u - 1, 0)
                            if i == 0 and is_out(behind):
                                act.wait_ge(e["g_hacc_ready"], 2)
                                nc.scalar.activation(other_hi[:, :], hidden[:, :], ACT.Copy).then_inc(e["g_h_high"], 1)
                            if i == 1 and came == "head":
                                add_bias(h_before, 0, kb)
                            if i == 3:
                                if behind is None and not last:
                                    x_high(act, 0)
                                elif behind is not None and not is_out(behind):
                                    round_queries(behind, 0, kn)
                            if i == 3 and behind is None and not first:
                                act.wait_ge(e["g_norm"], 6)
                                nc.scalar.activation(sq[:, :, :], y[:, :, :], ACT.Square).then_inc(e["g_square"], 1)
                            if i == 4 and came is not None:
                                if start_of_element:
                                    act.wait_ge(e["g_un_ready"], 1)
                                    nc.scalar.activation(mixed[:, :], ps_u[:, :], ACT.Copy).then_inc(e["g_ut_ready"], 1)
                                else:
                                    take_mixed(u - 1, 1)
                            if i == 4:
                                if behind is None and not last:
                                    x_high(act, 1)
                                elif behind is not None and not is_out(behind):
                                    round_queries(behind, 1, kn)
                            if i == 6 and came == "head":
                                add_bias(h_before, 1, kb)

                    nc.scalar.activation(moving_hi[:, :], other_hi[:, :].bitcast(F32), ACT.Copy).then_inc(e["g_main_hi"], 1)
                    exponentials(0, 0)
                    program(run, act.Fori)
                    take_mixed(END, 0)
                    if not last:
                        round_queries(NEXT, 0, 0)
                        round_queries(NEXT, 1, 0)
                    else:
                        add_bias(HEADS - 1, 0, 1)
                        take_mixed(END, 1)
                        add_bias(HEADS - 1, 1, 1)
                        act.wait_ge(e["g_hacc_ready"], 2 * (HEADS + before))
                        nc.scalar.activation(other_hi[:, :], hidden[:, :], ACT.Copy).then_inc(e["g_h_high"], 1)
                        exponentials(FINAL, 0)
                        for i in range(NT):
                            if i + 1 < NT:
                                exponentials(FINAL, i + 1)
                            high(FINAL, i)
                        for half in range(2):
                            if half == 1:
                                act.wait_ge(e["g_o_ready"], 3)
                            take_mixed(FINAL, half)
                        act.wait_ge(e["g_norm"], 12)
                        nc.scalar.activation(sq[:, :, :], y[:, :, :], ACT.Square).then_inc(e["g_square"], 1)

                @block.vector
                def _(dve):
                    def whole(weights):
                        def mask_and_max(u, i):
                            n = 8 * u + i
                            k = i % SLOTS
                            if not isinstance(n, int) or n >= SLOTS:
                                dve.wait_ge(e["g_pt_ready"], 2 * n - 2 * SLOTS + 2)
                            dve.wait_ge(e["g_s_ready"], n + 1)
                            nc.vector.memset(waiter[:, :], 0.0)
                            if weights:
                                nc.vector.tensor_tensor(ps_s[i % 2][:, :], ps_s[i % 2][:, :], graph[:, i, :], ALU.mult).then_inc(e["g_g_ready"], 1)
                                dve.wait_ge(e["g_g_ready"], n + 1)
                                nc.vector.memset(waiter[:, :], 0.0)
                            nc.vector.tensor_tensor_reduce(out=tile[k][:, :], in0=ps_s[i % 2][:, :], in1=fence[:, i, :],
                                                           scale=1.0, scalar=LOWEST, op0=ALU.add, op1=ALU.max,
                                                           accum_out=row_max[k][:, :]).then_inc(e["g_m_ready"], 1)
                            dve.wait_ge(e["g_m_ready"], n + 1)
                            nc.vector.tensor_scalar(neg_max[k][:, :], row_max[k][:, :], -1.0, None, ALU.mult).then_inc(e["g_t_ready"], 1)

                        def rest(u, i):
                            n = 8 * u + i
                            half, j = i // 4, i % 4
                            for a in range(2):
                                dve.wait_ge(e["g_hi_ready"], 2 * n + a + 1)
                                into = (slice(None), slice(4 * a, 4 * a + 4), slice(j * P, (j + 1) * P))
                                nc.vector.tensor_tensor(pt_lo[half][into], ps_t[a][:, :].rearrange("p (m n) -> p m n", n=P),
                                                        pt_hi[half][into].bitcast(F32), ALU.subtract).then_inc(e["g_lo_ready"], 1)

                        def inverse(u, half, spread):
                            dve.wait_ge(e["g_p_ready"], 8 * u + 4 * half + 4)
                            if spread is not None:
                                dve.wait_ge(e["g_rb_ready"], spread)
                            cols = slice(4 * half, 4 * half + 4)
                            nc.vector.reciprocal(row_inv[:, cols], row_sum[:, cols]).then_inc(e["g_ri_ready"], 1)

                        def scale_mixed(u, h, half):
                            if u is not None:
                                dve.wait_ge(e["g_ut_ready"], 2 * u + half + 1 + before)
                            elif half == 1:
                                dve.wait_ge(e["g_ut_ready"], 1)
                            dve.wait_ge(e["g_rb_ready"], 2 * (h + before) + half + 1)
                            nc.vector.tensor_tensor(mixed_n[:, :], mixed[:, :], ps_x[:, :], ALU.mult).then_inc(e["g_un_ready"], 1)

                        def leaky(h, half):
                            dve.wait_ge(e["g_vb_ready"], 2 * (h + before) + half + 1)
                            nc.vector.scalar_tensor_tensor(cat[:, :], cat[:, :], 0.01, cat[:, :], ALU.mult, ALU.max).then_inc(e["g_v_ready"], 1)

                        def collect(h, half):
                            count = 2 * (h + before) + half + 1
                            cols = slice(half * HN, (half + 1) * HN)
                            dve.wait_ge(e["g_hp_ready"], count)
                            if isinstance(h, int) and h == 0:
                                nc.vector.tensor_copy(hidden[:, cols], ps_x[:, :]).then_inc(e["g_hacc_ready"], 1)
                                return
                            if not (isinstance(h, int) and h < 0):
                                dve.wait_ge(e["g_hacc_ready"], count - 2)
                            nc.vector.tensor_tensor(hidden[:, cols], hidden[:, cols], ps_x[:, :], ALU.add).then_inc(e["g_hacc_ready"], 1)

                        def rest_of_queries(h, half, k):
                            dve.wait_ge(e["g_yr_ready"], 2 * h - 1 + half)
                            query_rest(k, half)

                        def split_hidden(number):
                            dve.wait_ge(e["g_h_high"], number)
                            nc.vector.tensor_tensor(other_lo[:, :], hidden[:, :], other_hi[:, :].bitcast(F32), ALU.subtract).then_inc(e["g_h_rest"], 1)

                        def hidden_rows(number, half):
                            dve.wait_ge(e["g_hT_ready"], number)
                            nc.vector.tensor_copy(other_value[:, 4 * half:4 * half + 4, :],
                                                  ps_x[:, :].rearrange("p (t c) -> p t c", c=P)).then_inc(e["g_hT_copied"], 1)

                        def out_half(u, number, half):
                            tiles = slice(4 * half, 4 * half + 4)
                            dve.wait_ge(e["g_ri_ready"], 2 * u + half + 1)
                            dve.wait_ge(e["g_o_ready"], number)
                            nc.vector.tensor_tensor(y[:, tiles, :], ps_x[:, 0:4 * C].rearrange("p (t c) -> p t c", c=C),
                                                    row_inv[:, tiles].unsqueeze(2).broadcast_to([P, 4, C]), ALU.mult).then_inc(e["g_o_used"], 1)

                        def spread(v):
                            return v[:, :].unsqueeze(2).broadcast_to([P, NT, C])

                        def norm(step, turn):
                            count = 6 * turn + step
                            if step == 0:
                                dve.wait_ge(e["g_o_used"], 2 * turn + 2)
                                ins = nc.vector.tensor_tensor(y[:, :, :], y[:, :, :], b_out_row[:, :].unsqueeze(1).broadcast_to([P, NT, C]), ALU.add)
                            elif step < 6:
                                dve.wait_ge(e["g_norm"], count)
                            if step == 1:
                                ins = nc.vector.scalar_tensor_tensor(y[:, :, :], y[:, :, :], 0.01, y[:, :, :], ALU.mult, ALU.max)
                            if step == 2:
                                dve.wait_ge(e["g_r_loaded"], 16 * turn + 16)
                                ins = nc.vector.tensor_tensor(y[:, :, :], y[:, :, :], x_again[:, :, :], ALU.add)
                            if step == 3:
                                ins = nc.vector.tensor_reduce(mean[:, :], y[:, :, :], AX.X, ALU.add)
                            if step == 4:
                                ins = nc.vector.tensor_scalar(mean[:, :], mean[:, :], 1.0 / C, None, ALU.mult)
                            if step == 5:
                                ins = nc.vector.tensor_tensor(y[:, :, :], y[:, :, :], spread(mean), ALU.subtract)
                            if step < 6:
                                ins.then_inc(e["g_norm"], 1)
                            if step == 6:
                                dve.wait_ge(e["g_square"], turn + 1)
                                nc.vector.tensor_reduce(var[:, :], sq[:, :, :], AX.X, ALU.add).then_inc(e["g_v_high"], 1)
                                dve.wait_ge(e["g_v_high"], 2 + turn)
                                nc.vector.tensor_scalar(var[:, :], var[:, :], 1.0 / C, EPS, ALU.mult, ALU.add).then_inc(e["g_var_ready"], 1)
                            if step == 7:
                                dve.wait_ge(e["g_rstd_ready"], turn + 1)
                                nc.vector.tensor_tensor(y[:, :, :], y[:, :, :], spread(rstd), ALU.mult).then_inc(e["g_y_done"], 1)

                        def run(u, h, came, behind, h_before, k=0, looped=False):
                            k = parity(h, k) if not is_out(h) else 0
                            kn = (1 - k) if not is_out(h) else 0
                            start_of_element = isinstance(u, int) and u == 0
                            from_unit = None if start_of_element else u - 1
                            for i in range(NT):
                                if i + 2 < NT:
                                    mask_and_max(u, i + 2)
                                elif behind is not None:
                                    mask_and_max(u + 1, i + 2 - NT)
                                rest(u, i)
                                if i == 1 and is_out(behind):
                                    split_hidden(1)
                                if came == "head":
                                    if i == 0 or i == 5:
                                        scale_mixed(from_unit, h_before, i // 5)
                                    if i == 1 or i == 6:
                                        leaky(h_before, i // 6)
                                    if i == 2 or i == 7:
                                        collect(h_before, i // 7)
                                if came == "out":
                                    if i == 0 or i == 5:
                                        out_half(u - 1, 1 + i // 5, i // 5)
                                    if i == 6:
                                        norm(0, 0)
                                    if i == 7:
                                        norm(1, 0)
                                if i == 3 or i == 7:
                                    inverse(u, i // 4, 2 * (h_before + before) + i // 4 + 1 if came == "head" else None)
                                if i == 3 or i == 4:
                                    if is_out(behind):
                                        hidden_rows(i - 2, i - 3)
                                    elif behind is not None:
                                        rest_of_queries(behind, i - 3, kn)
                                    elif not last:
                                        x_rest(dve, i - 3)
                                if behind is None and not first:
                                    if i <= 2:
                                        norm(2 + i, 0)
                                    if i == 3:
                                        norm(5, 0)
                                    if i == 5:
                                        norm(6, 0)

                        nc.vector.tensor_copy(moving_lo[:, :], other_lo[:, :].bitcast(F32)).then_inc(e["g_main_lo"], 1)
                        nc.vector.tensor_copy(value_hl[:, :, 0:C], x_rows[:, :, 0:C]).then_inc(e["g_v_high"], 1)
                        dve.wait_ge(e["g_v_high"], 1)
                        nc.vector.tensor_tensor(value_hl[:, :, C:P], x_rows[:, :, C:P], value_hl[:, :, 0:C].bitcast(F32),
                                                ALU.subtract).then_inc(e["g_v_rest"], 1)
                        mask_and_max(0, 0)
                        mask_and_max(0, 1)
                        program(run, dve.Fori)
                        if not last:
                            rest_of_queries(NEXT, 0, 0)
                            rest_of_queries(NEXT, 1, 0)
                        if not first:
                            norm(7, 0)
                        if last:
                            for half in range(2):
                                scale_mixed(END, HEADS - 1, half)
                                leaky(HEADS - 1, half)
                                collect(HEADS - 1, half)
                            split_hidden(2)
                            mask_and_max(FINAL, 0)
                            mask_and_max(FINAL, 1)
                            hidden_rows(3, 0)
                            hidden_rows(4, 1)
                            for i in range(NT):
                                if i + 2 < NT:
                                    mask_and_max(FINAL, i + 2)
                                rest(FINAL, i)
                                if i == 3 or i == 7:
                                    inverse(FINAL, i // 4, 2 * (HEADS - 1 + before) + i // 4 + 1)
                            dve.wait_ge(e["g_stored"], 16)
                            for half in range(2):
                                out_half(FINAL, 3 + half, half)
                            for step in range(8):
                                norm(step, 1)

                    any_weights = dve.value_load(weighted[0:1, 0:1], min_val=0, max_val=1)
                    with dve.If(any_weights == 1):
                        whole(True)
                    with dve.Else():
                        whole(False)
            nc.all_engine_barrier(sems_to_clear=numbers(e))

        element(0, first=True)
        with nc.Fori(1, BATCH - 1) as b:
            element(b)
        element(BATCH - 1, last=True)


def causal_steps(nc, bank, io, adjT_dram, weighted, x_in, x_out):
    STEPS = 3
    ctx = ExitStack()
    with ctx:
        def sb(name, shape, dt=F32):
            return ctx.enter_context(nc.sbuf_tensor(name, shape, dt))

        adjT_short = sb("c_adjT", [P, NT, N], F32R)
        adjT = adjT_short[:, :, :].bitcast(F32)
        ident = sb("c_ident", [P, P])
        w_stage = sb("c_w_stage", [C, 3, P])
        w_diag = sb("c_w_diag", [P, 3, P])
        b1 = sb("c_b1", [P, 1])
        b2 = sb("c_b2", [P, 1])
        b2_row = sb("c_b2_row", [P, P])
        v_high = sb("c_v_high", [P, NT, BATCH, C], F32R)
        v_rest = sb("c_v_rest", [P, NT, BATCH, C], F32R)
        v_rows = sb("c_v_rows", [P, NT, BATCH, C])
        vT = sb("c_vT", [P, PAIRS, N])
        effect = [sb(f"c_effect{k}", [P, N]) for k in range(2)]
        hidden = [sb(f"c_hidden{k}", [P, N]) for k in range(2)]
        x_rows = sb("c_x_rows", [P, NT, BATCH, C])
        sq = sb("c_sq", [P, NT * BATCH, C])
        mean = sb("c_mean", [P, NT * BATCH])
        var = sb("c_var", [P, NT * BATCH])
        rstd = sb("c_rstd", [P, NT * BATCH])
        minus_half = sb("c_minus_half", [P, NT * BATCH])
        ps_e = [ctx.enter_context(nc.psum_tensor(f"c_ps_e{k}", [P, N], F32)) for k in range(2)]
        ps_h = ctx.enter_context(nc.psum_tensor("c_ps_h", [P, N], F32))
        ps_v = ctx.enter_context(nc.psum_tensor("c_ps_v", [P, N], F32))

        def columns(p, v=v_rows):
            return v[:, :, 2 * p:2 * p + 2, :].rearrange("p t b c -> p t (b c)")

        setup = events(bank, "c_w_loaded c_adj_loaded c_v0_loaded c_v_loaded c_zeroed c_ident_ready c_w_zeroed "
                                "c_wT_ready c_w_ready c_half_ready c_vT_ready c_vT_copied c_intervened c_high_ready c_rest_ready")
        with nc.Block() as block:
            e = setup

            @block.sync
            def _(sp):
                xr = x_in.rearrange("b (t p) c -> p t b c", p=P)
                for t in range(NT):
                    sp.dma_start(v_rows[:, t, :, :], xr[:, t, :, :]).then_inc(e["c_v0_loaded" if t == 0 else "c_v_loaded"], 16)
                for k in range(2):
                    half = slice(k * C, (k + 1) * C)
                    for i, src in enumerate((io["L2_gnn_W1"][:, 0:C], io["L2_gnn_W1"][:, C:2 * C], io["L2_gnn_W2"])):
                        sp.dma_start(w_stage[:, i, half], src).then_inc(e["c_w_loaded"], 16)
                    sp.dma_start(b1[half, :], io["L2_gnn_b1"].rearrange("(c o) -> c o", o=1)).then_inc(e["c_w_loaded"], 16)
                    sp.dma_start(b2[half, :], io["L2_gnn_b2"].rearrange("(c o) -> c o", o=1)).then_inc(e["c_w_loaded"], 16)
                    sp.dma_start(b2_row[:, half], io["L2_gnn_b2"].partition_broadcast(P)).then_inc(e["c_w_loaded"], 16)
                sp.wait_ge(e["c_v0_loaded"], 16)
                sp.dma_start(v_rows[0:1, 0, :, :], io["L2_gnn_intervention_value"].unsqueeze(1).broadcast_to([1, BATCH, C])).then_inc(e["c_intervened"], 16)
                sp.dma_start(adjT, adjT_dram.rearrange("(t p) n -> p t n", p=P)).then_inc(e["c_adj_loaded"], 16)
                sp.wait_ge(e["c_adj_loaded"], 16)

            @block.gpsimd
            def _(pool):
                make_identity(pool, ident, e["c_zeroed"], e["c_ident_ready"], 0)
                nc.gpsimd.memset(w_diag[:, :, :], 0.0).then_inc(e["c_w_zeroed"], 1)
                nc.gpsimd.memset(minus_half[:, :], -0.5).then_inc(e["c_half_ready"], 1)
                for p in range(PAIRS):
                    pool.wait_ge(e["c_high_ready"], p + 1)
                    nc.gpsimd.tensor_tensor(columns(p, v_rest), columns(p), columns(p, v_high).bitcast(F32), ALU.subtract).then_inc(e["c_rest_ready"], 1)

            @block.scalar
            def _(act):
                act.wait_ge(e["c_intervened"], 16)
                act.wait_ge(e["c_v_loaded"], 16 * (NT - 1))
                for p in range(PAIRS):
                    nc.scalar.activation(columns(p, v_high), columns(p), ACT.Copy).then_inc(e["c_high_ready"], 1)

            @block.tensor
            def _(pe):
                pe.wait_ge(e["c_ident_ready"], 1)
                pe.wait_ge(e["c_w_loaded"], 16 * 12)
                for i in range(3):
                    mm = nc.tensor.transpose(ps_h[:, i * C:(i + 1) * C], w_stage[:, i, :], ident[0:C, 0:C])
                mm.then_inc(e["c_wT_ready"], 1)
                pe.wait_ge(e["c_intervened"], 16)
                pe.wait_ge(e["c_v_loaded"], 16 * (NT - 1))
                for p in range(PAIRS):
                    if p >= 2:
                        pe.wait_ge(e["c_vT_copied"], p - 1)
                    for t in range(NT):
                        mm = nc.tensor.transpose(ps_e[p % 2][:, t * P:(t + 1) * P],
                                                 v_rows[:, t, 2 * p:2 * p + 2, :].rearrange("p b c -> p (b c)"), ident[:, :])
                    mm.then_inc(e["c_vT_ready"], 1)

            @block.vector
            def _(dve):
                dve.wait_ge(e["c_w_zeroed"], 1)
                dve.wait_ge(e["c_wT_ready"], 1)
                for k in range(2):
                    half = slice(k * C, (k + 1) * C)
                    nc.vector.tensor_copy(w_diag[half, :, half], ps_h[half, 0:3 * C].rearrange("p (i c) -> p i c", c=C)).then_inc(e["c_w_ready"], 1)
                for p in range(PAIRS):
                    dve.wait_ge(e["c_vT_ready"], p + 1)
                    nc.vector.tensor_copy(vT[:, p, :], ps_e[p % 2][:, :]).then_inc(e["c_vT_copied"], 1)
        nc.all_engine_barrier(sems_to_clear=numbers(setup))

        e = events(bank, "c_effect_ready c_effect_copied c_hidden_ready c_hidden_copied c_next_ready "
                            "c_next_copied c_rows_ready c_rows_copied c_high_ready c_rest_ready")
        with nc.Fori(0, STEPS) as step:
            with nc.Block() as block:

                @block.tensor
                def _(pe):
                    def whole(weights):
                        for u in range(PAIRS + 2):
                            if u < PAIRS:
                                if u >= 2:
                                    pe.wait_ge(e["c_effect_copied"], u - 1)
                                for m in range(2):
                                    cols = slice(m * HN, (m + 1) * HN)
                                    for t in range(NT):
                                        if weights:
                                            mm = nc.tensor.matmul(ps_e[u % 2][:, cols], columns(u)[:, t, :], adjT[:, t, cols],
                                                                  start=(t == 0), stop=(t == NT - 1))
                                        else:
                                            nc.tensor.matmul(ps_e[u % 2][:, cols], columns(u, v_high)[:, t, :], adjT_short[:, t, cols],
                                                             start=(t == 0), stop=False)
                                            mm = nc.tensor.matmul(ps_e[u % 2][:, cols], columns(u, v_rest)[:, t, :], adjT_short[:, t, cols],
                                                                  start=False, stop=(t == NT - 1))
                                mm.then_inc(e["c_effect_ready"], 1)
                            if u >= 2:
                                p = u - 2
                                pe.wait_ge(e["c_hidden_copied"], p + 1)
                                if p >= 1:
                                    pe.wait_ge(e["c_rows_copied"], p)
                                for m in range(2):
                                    cols = slice(m * HN, (m + 1) * HN)
                                    mm = nc.tensor.matmul(ps_v[:, cols], w_diag[:, 2, :], hidden[p % 2][:, cols], start=True, stop=True)
                                mm.then_inc(e["c_next_ready"], 1)
                                pe.wait_ge(e["c_next_copied"], p + 1)
                                for t in range(NT):
                                    mm = nc.tensor.matmul(ps_v[:, t * P:(t + 1) * P], hidden[p % 2][:, t * P:(t + 1) * P], w_diag[:, 2, :],
                                                          start=True, stop=True)
                                mm.then_inc(e["c_rows_ready"], 1)
                            if 1 <= u <= PAIRS:
                                p = u - 1
                                pe.wait_ge(e["c_effect_copied"], p + 1)
                                if p >= 1:
                                    pe.wait_ge(e["c_hidden_copied"], p)
                                for m in range(2):
                                    cols = slice(m * HN, (m + 1) * HN)
                                    nc.tensor.matmul(ps_h[:, cols], w_diag[:, 0, :], vT[:, p, cols], start=True, stop=False)
                                    mm = nc.tensor.matmul(ps_h[:, cols], w_diag[:, 1, :], effect[p % 2][:, cols], start=False, stop=True)
                                mm.then_inc(e["c_hidden_ready"], 1)

                    any_weights = pe.value_load(weighted[0:1, 0:1], min_val=0, max_val=1)
                    with pe.If(any_weights == 1):
                        whole(True)
                    with pe.Else():
                        whole(False)

                @block.scalar
                def _(act):
                    def split_high(p):
                        act.wait_ge(e["c_rows_copied"], p + 1)
                        nc.scalar.activation(columns(p, v_high), columns(p), ACT.Copy).then_inc(e["c_high_ready"], 1)

                    for p in range(PAIRS):
                        act.wait_ge(e["c_hidden_ready"], p + 1)
                        if p >= 2:
                            act.wait_ge(e["c_rows_ready"], p - 1)
                        nc.scalar.activation(hidden[p % 2][:, :], ps_h[:, :], ACT.Relu, bias=b1[:, :]).then_inc(e["c_hidden_copied"], 1)
                        act.wait_ge(e["c_next_ready"], p + 1)
                        nc.scalar.activation(vT[:, p, :], ps_v[:, :], ACT.Identity, bias=b2[:, :]).then_inc(e["c_next_copied"], 1)
                        if p >= 1:
                            split_high(p - 1)
                    split_high(PAIRS - 1)

                @block.gpsimd
                def _(pool):
                    for p in range(PAIRS):
                        pool.wait_ge(e["c_high_ready"], p + 1)
                        nc.gpsimd.tensor_tensor(columns(p, v_rest), columns(p), columns(p, v_high).bitcast(F32), ALU.subtract).then_inc(e["c_rest_ready"], 1)

                @block.vector
                def _(dve):
                    def take_effect(p):
                        dve.wait_ge(e["c_effect_ready"], p + 1)
                        if p >= 2:
                            dve.wait_ge(e["c_hidden_ready"], p - 1)
                        nc.vector.tensor_copy(effect[p % 2][:, :], ps_e[p % 2][:, :]).then_inc(e["c_effect_copied"], 1)

                    take_effect(0)
                    take_effect(1)
                    for p in range(PAIRS):
                        if p + 2 < PAIRS:
                            take_effect(p + 2)
                        dve.wait_ge(e["c_rows_ready"], p + 1)
                        nc.vector.tensor_tensor(columns(p), ps_v[:, :].rearrange("p (t c) -> p t c", c=P),
                                                b2_row[:, :].unsqueeze(1).broadcast_to([P, NT, P]), ALU.add).then_inc(e["c_rows_copied"], 1)
            nc.all_engine_barrier(sems_to_clear=numbers(e))

        e = events(bank, " ".join(f"c_x_loaded{k}" for k in range(4)) + " c_norm c_square c_rowvar_ready c_var_ready "
                         "c_rstd_ready c_y_done c_stored")
        PARTS = NT // 2
        GROUPS = 2 * BATCH
        with nc.Block() as block:

            def part(v, k):
                return v[:, 2 * k:2 * k + 2, :, :].rearrange("p t b c -> p (t b) c")

            def of(v, k):
                return v[:, k * GROUPS:(k + 1) * GROUPS]

            def spread(v, k):
                return of(v, k).unsqueeze(2).broadcast_to([P, GROUPS, C])

            @block.vector
            def _(dve):
                def centre(k):
                    dve.wait_ge(e[f"c_x_loaded{k}"], 32)
                    nc.vector.tensor_tensor(part(v_rows, k), part(v_rows, k), part(x_rows, k), ALU.add).then_inc(e["c_norm"], 1)
                    dve.wait_ge(e["c_norm"], 4 * k + 1)
                    nc.vector.tensor_reduce(of(mean, k), part(v_rows, k), AX.X, ALU.add).then_inc(e["c_norm"], 1)
                    dve.wait_ge(e["c_norm"], 4 * k + 2)
                    nc.vector.tensor_scalar(of(mean, k), of(mean, k), 1.0 / C, None, ALU.mult).then_inc(e["c_norm"], 1)
                    dve.wait_ge(e["c_norm"], 4 * k + 3)
                    nc.vector.tensor_tensor(part(v_rows, k), part(v_rows, k), spread(mean, k), ALU.subtract).then_inc(e["c_norm"], 1)

                def variance(k):
                    dve.wait_ge(e["c_square"], k + 1)
                    nc.vector.tensor_reduce(of(var, k), sq[:, k * GROUPS:(k + 1) * GROUPS, :], AX.X, ALU.add).then_inc(e["c_rowvar_ready"], 1)
                    dve.wait_ge(e["c_rowvar_ready"], k + 1)
                    nc.vector.tensor_scalar(of(var, k), of(var, k), 1.0 / C, EPS, ALU.mult, ALU.add).then_inc(e["c_var_ready"], 1)

                for k in range(PARTS):
                    centre(k)
                    if k >= 1:
                        variance(k - 1)
                variance(PARTS - 1)
                dve.wait_ge(e["c_rstd_ready"], PARTS)
                nc.vector.tensor_tensor(part(v_rows, PARTS - 1), part(v_rows, PARTS - 1), spread(rstd, PARTS - 1), ALU.mult).then_inc(e["c_y_done"], 1)

            @block.scalar
            def _(act):
                for k in range(PARTS):
                    act.wait_ge(e["c_norm"], 4 * k + 4)
                    nc.scalar.activation(sq[:, k * GROUPS:(k + 1) * GROUPS, :], part(v_rows, k), ACT.Square).then_inc(e["c_square"], 1)

            @block.gpsimd
            def _(pool):
                for k in range(PARTS):
                    pool.wait_ge(e["c_var_ready"], k + 1)
                    nc.gpsimd.tensor_tensor(of(rstd, k), of(var, k), of(minus_half, k), ALU.pow).then_inc(e["c_rstd_ready"], 1)
                    if k < PARTS - 1:
                        pool.wait_ge(e["c_rstd_ready"], k + 1)
                        nc.gpsimd.tensor_tensor(part(v_rows, k), part(v_rows, k), spread(rstd, k), ALU.mult).then_inc(e["c_y_done"], 1)

            @block.sync
            def _(sp):
                xr = x_in.rearrange("b (t p) c -> p t b c", p=P)
                yr = x_out.rearrange("b (t p) c -> p t b c", p=P)
                for t in range(NT):
                    sp.dma_start(x_rows[:, t, :, :], xr[:, t, :, :]).then_inc(e[f"c_x_loaded{t // 2}"], 16)
                for t in range(NT):
                    sp.wait_ge(e["c_y_done"], t // 2 + 1)
                    sp.dma_start(yr[:, t, :, :], v_rows[:, t, :, :]).then_inc(e["c_stored"], 16)
                sp.wait_ge(e["c_stored"], 16 * NT)
        nc.all_engine_barrier(sems_to_clear=numbers(e))


def adaptive_chebyshev(nc, bank, io, adjT_dram, weighted, x_in, x_out):
    D = io["L3_gnn_node_embeddings"].shape[1]
    ctx = ExitStack()
    with ctx:
        def sb(name, shape, dt=F32):
            return ctx.enter_context(nc.sbuf_tensor(name, shape, dt))

        adjT_short = sb("k_adjT", [P, NT, N], F32R)
        adjT = adjT_short[:, :, :].bitcast(F32)
        aptT = sb("k_aptT", [P, NT, N])
        ident = sb("k_ident", [P, P])
        embed = sb("k_embed", [P, NT, D])
        embedT = sb("k_embedT", [D, N])
        pool_w = sb("k_pool_w", [P, 2, D, C])
        pool_b = sb("k_pool_b", [D, C])
        bias = sb("k_bias", [P, NT, C])
        g01 = sb("k_g01", [P, NT, BATCH, 2, C])
        with nc.sbuf_tensor("k_x_parts", [P, NT, 2, HN], F32R) as x_parts:
            pass
        g23 = sb("k_g23", [P, NT, BATCH, 2, C])
        x1_parts = sb("k_x1_parts", [P, NT, 2, HN], F32R)
        relu = sb("k_relu", [P, N])
        probs = [sb(f"k_probs{k}", [P, N]) for k in range(2)]
        row_max = sb("k_row_max", [P, NT])
        row_sum = sb("k_row_sum", [P, NT])
        row_inv = sb("k_row_inv", [P, NT])
        gT = [sb(f"k_gT{k}", [P, 2, P]) for k in range(2)]
        mixed = [probs[0], probs[1]]
        y = [sb(f"k_y{k}", [P, BATCH, C]) for k in range(3)]
        sq = sb("k_sq", [P, BATCH, C])
        mean = sb("k_mean", [P, BATCH])
        var = sb("k_var", [P, BATCH])
        rstd = sb("k_rstd", [P, BATCH])
        minus_half = sb("k_minus_half", [P, BATCH])
        ps_a = [ctx.enter_context(nc.psum_tensor(f"k_ps_a{k}", [P, N], F32)) for k in range(2)]
        ps_b = [ctx.enter_context(nc.psum_tensor(f"k_ps_b{k}", [P, HN], F32)) for k in range(2)]

        setup = events(bank, "k_adj_loaded k_x_loaded k_e_loaded k_b_loaded k_w_loaded k_zeroed k_ident_ready k_half_ready "
                                "k_eT_ready k_eT_copied k_bias_ready k_bias_copied k_s_ready k_relu_ready k_max_ready "
                                "k_p_ready k_pt_ready k_pt_copied k_inv_ready k_x1_ready k_x1_copied k_x_high k_x_rest k_x1_high k_x1_rest k_x2_ready "
                                "k_x2_copied k_x3_ready k_x3_copied k_gT_ready k_gT_copied k_z_ready k_z_scaled k_sum_ready "
                                "k_norm k_square k_rowvar_ready k_var_ready k_rstd_ready k_y_done k_stored")
        def by_batch(v):
            return v.rearrange("p (b c) -> p b c", c=C)

        UNITS = NT * BATCH
        NORM = 5
        y_tiles = x_out.rearrange("b (t p) c -> t p b c", p=P)
        with nc.Block() as block:
            e = setup

            @block.sync
            def _(sp):
                sp.dma_start(embed[:, :, :], io["L3_gnn_node_embeddings"].rearrange("(t p) d -> p t d", p=P)).then_inc(e["k_e_loaded"], 16)
                sp.dma_start(pool_b[:, :], io["L3_gnn_bias_pool"]).then_inc(e["k_b_loaded"], 16)
                for t in range(NT):
                    sp.dma_start(g01[:, t, :, 0, :], x_in.rearrange("b (t p) c -> p t b c", p=P)[:, t, :, :]).then_inc(e["k_x_loaded"], 16)
                sp.dma_start(adjT, adjT_dram.rearrange("(t p) n -> p t n", p=P)).then_inc(e["k_adj_loaded"], 16)
                for k in range(4):
                    sp.dma_start(pool_w[(k % 2) * C:(k % 2 + 1) * C, k // 2, :, :],
                                 io["L3_gnn_weights_pool"][:, k, :, :].rearrange("d i o -> i d o")).then_inc(e["k_w_loaded"], 16)
                for t in range(NT):
                    sp.wait_ge(e["k_y_done"], t + 1)
                    sp.dma_start(y_tiles[t], y[t % 3][:, :, :]).then_inc(e["k_stored"], 16)
                sp.wait_ge(e["k_stored"], 16 * NT)

            @block.gpsimd
            def _(pool):
                make_identity(pool, ident, e["k_zeroed"], e["k_ident_ready"], 0)
                nc.gpsimd.memset(minus_half[:, :], -0.5).then_inc(e["k_half_ready"], 1)
                pool.wait_ge(e["k_x_loaded"], 16 * NT)
                for t in range(NT):
                    x_t, high, low = g01[:, t, :, 0, :], by_batch(x_parts[:, t, 0, :]), by_batch(x_parts[:, t, 1, :])
                    nc.gpsimd.tensor_copy(high, x_t).then_inc(e["k_x_high"], 1)
                    pool.wait_ge(e["k_x_high"], t + 1)
                    nc.gpsimd.tensor_tensor(low, x_t, high.bitcast(F32), ALU.subtract).then_inc(e["k_x_rest"], 1)
                for t in range(NT):
                    pool.wait_ge(e["k_var_ready"], t + 1)
                    if t == 0:
                        pool.wait_ge(e["k_half_ready"], 1)
                    nc.gpsimd.tensor_tensor(rstd[:, :], var[:, :], minus_half[:, :], ALU.pow).then_inc(e["k_rstd_ready"], 1)

            @block.tensor
            def _(pe):
                pe.wait_ge(e["k_ident_ready"], 1)
                pe.wait_ge(e["k_e_loaded"], 16)
                for t in range(NT):
                    mm = nc.tensor.transpose(ps_a[0][0:D, t * P:(t + 1) * P], embed[:, t, :], ident[:, :])
                mm.then_inc(e["k_eT_ready"], 1)
                pe.wait_ge(e["k_eT_copied"], 1)
                for t in range(NT + 1):
                    if t < NT:
                        if t >= 1:
                            pe.wait_ge(e["k_relu_ready"], t)
                        for m in range(2):
                            cols = slice(m * HN, (m + 1) * HN)
                            mm = nc.tensor.matmul(ps_a[0][:, cols], embedT[:, t * P:(t + 1) * P], embedT[:, cols], start=True, stop=True)
                        mm.then_inc(e["k_s_ready"], 1)
                    if t >= 1:
                        pe.wait_ge(e["k_p_ready"], t)
                        if t >= 2:
                            pe.wait_ge(e["k_pt_copied"], t - 1)
                        for s in range(NT):
                            mm = nc.tensor.transpose(ps_a[1][:, s * P:(s + 1) * P], probs[(t - 1) % 2][:, s * P:(s + 1) * P], ident[:, :])
                        mm.then_inc(e["k_pt_ready"], 1)

                pe.wait_ge(e["k_b_loaded"], 16)
                for t in range(NT):
                    mm = nc.tensor.matmul(ps_b[0][:, t * C:(t + 1) * C], embedT[:, t * P:(t + 1) * P], pool_b[:, :], start=True, stop=True)
                mm.then_inc(e["k_bias_ready"], 1)

                def apply(matrixT, source, ready, copied, before):
                    for t in range(NT):
                        if before + t >= 2:
                            pe.wait_ge(*copied(t))
                        for s in range(NT):
                            mm = nc.tensor.matmul(ps_b[t % 2][:, :], matrixT[:, s, t * P:(t + 1) * P], source(s),
                                                  start=(s == 0), stop=(s == NT - 1))
                        mm.then_inc(ready, 1)

                pe.wait_ge(e["k_adj_loaded"], 16)
                pe.wait_ge(e["k_x_loaded"], 16 * NT)
                pe.wait_ge(e["k_bias_copied"], 1)
                pe.wait_ge(e["k_x_rest"], NT)

                def apply_short(parts, ready, before, copied):
                    for t in range(NT):
                        if before + t >= 2:
                            pe.wait_ge(*copied(t))
                        for s in range(NT):
                            for q in range(2):
                                mm = nc.tensor.matmul(ps_b[t % 2][:, :], adjT_short[:, s, t * P:(t + 1) * P], parts[:, s, q, :],
                                                      start=(s == 0 and q == 0), stop=(s == NT - 1 and q == 1))
                        mm.then_inc(ready, 1)

                any_weights = pe.value_load(weighted[0:1, 0:1], min_val=0, max_val=1)
                with pe.If(any_weights == 1):
                    apply(adjT, lambda s: g01[:, s, :, 0, :], e["k_x1_ready"], lambda t: (e["k_x1_rest"], t - 1), 0)
                    pe.wait_ge(e["k_x1_rest"], NT)
                    apply(adjT, lambda s: g01[:, s, :, 1, :], e["k_x2_ready"], lambda t: (e["k_x2_copied"], t - 1), 0)
                with pe.Else():
                    apply_short(x_parts, e["k_x1_ready"], 0, lambda t: (e["k_x1_rest"], t - 1))
                    pe.wait_ge(e["k_x1_rest"], NT)
                    apply_short(x1_parts, e["k_x2_ready"], 0, lambda t: (e["k_x2_copied"], t - 1))
                pe.wait_ge(e["k_x2_copied"], NT)
                pe.wait_ge(e["k_pt_copied"], NT)
                apply(aptT, lambda s: g01[:, s, :, 0, :], e["k_x3_ready"], lambda t: (e["k_x3_copied"], t - 1), 0)

                pe.wait_ge(e["k_w_loaded"], 16 * 4)
                for u in range(UNITS + 1):
                    if u < UNITS:
                        t, b = divmod(u, BATCH)
                        if u < 2:
                            pe.wait_ge(e["k_x3_copied"], NT - 1 + u)
                        if u >= 2:
                            pe.wait_ge(e["k_gT_copied"], u - 1)
                        for q, pairs in enumerate((g01, g23)):
                            mm = nc.tensor.transpose(ps_b[u % 2][:, q * P:(q + 1) * P], pairs[:, t, b, :, :].rearrange("p k c -> p (k c)"), ident[:, :])
                        mm.then_inc(e["k_gT_ready"], 1)
                    if u >= 1:
                        w = u - 1
                        pe.wait_ge(e["k_gT_copied"], w + 1)
                        if w >= 2:
                            pe.wait_ge(e["k_z_scaled"], w - 1)
                        for m in range(2):
                            cols = slice(m * HN, (m + 1) * HN)
                            for q in range(2):
                                mm = nc.tensor.matmul(ps_a[w % 2][:, cols], gT[w % 2][:, q, :],
                                                      pool_w[:, q, m * D // 2:(m + 1) * D // 2, :].rearrange("p d o -> p (d o)"),
                                                      start=(q == 0), stop=(q == 1))
                        mm.then_inc(e["k_z_ready"], 1)

            @block.scalar
            def _(act):
                act.wait_ge(e["k_eT_ready"], 1)
                nc.scalar.activation(embedT[:, :], ps_a[0][0:D, :], ACT.Copy).then_inc(e["k_eT_copied"], 1)
                for t in range(NT):
                    act.wait_ge(e["k_s_ready"], t + 1)
                    if t >= 1:
                        act.wait_ge(e["k_p_ready"], t)
                    nc.scalar.activation(relu[:, :], ps_a[0][:, :], ACT.Relu).then_inc(e["k_relu_ready"], 1)
                    act.wait_ge(e["k_max_ready"], t + 1)
                    if t >= 2:
                        act.wait_ge(e["k_pt_ready"], t - 1)
                    nc.scalar.activation(probs[t % 2][:, :], relu[:, :], ACT.Exp, bias=row_max[:, t:t + 1],
                                         accum_out=row_sum[:, t:t + 1]).then_inc(e["k_p_ready"], 1)
                for t in range(NT):
                    act.wait_ge(e["k_x1_ready"], t + 1)
                    nc.scalar.activation(g01[:, t, :, 1, :], ps_b[t % 2][:, :].rearrange("p (b c) -> p b c", c=C), ACT.Copy).then_inc(e["k_x1_copied"], 1)
                    nc.scalar.activation(x1_parts[:, t, 0, :], ps_b[t % 2][:, :], ACT.Copy).then_inc(e["k_x1_high"], 1)
                act.wait_ge(e["k_inv_ready"], 1)
                for t in range(NT):
                    act.wait_ge(e["k_x3_ready"], t + 1)
                    nc.scalar.activation(g23[:, t, :, 1, :], ps_b[t % 2][:, :].rearrange("p (b c) -> p b c", c=C), ACT.Copy,
                                         scale=row_inv[:, t:t + 1]).then_inc(e["k_x3_copied"], 1)
                for u in range(UNITS + 3):
                    if u < UNITS:
                        act.wait_ge(e["k_gT_ready"], u + 1)
                        if u >= 2:
                            act.wait_ge(e["k_z_ready"], u - 1)
                        nc.scalar.activation(gT[u % 2][:, :, :], ps_b[u % 2][:, 0:2 * P].rearrange("p (q n) -> p q n", n=P), ACT.Copy).then_inc(e["k_gT_copied"], 1)
                    t = (u - BATCH) // BATCH
                    if u >= BATCH and u % BATCH == 6 or u == UNITS + 2:
                        act.wait_ge(e["k_norm"], NORM * (t + 1))
                        if t >= 1:
                            act.wait_ge(e["k_rowvar_ready"], t)
                        nc.scalar.activation(sq[:, :, :], y[t % 3][:, :, :], ACT.Square).then_inc(e["k_square"], 1)

            @block.vector
            def _(dve):
                for t in range(NT):
                    dve.wait_ge(e["k_relu_ready"], t + 1)
                    nc.vector.tensor_reduce(row_max[:, t:t + 1], relu[:, :], AX.X, ALU.max, negate=True).then_inc(e["k_max_ready"], 1)
                    if t >= 1:
                        dve.wait_ge(e["k_pt_ready"], t)
                        nc.vector.tensor_copy(aptT[:, :, (t - 1) * P:t * P], ps_a[1][:, :].rearrange("p (s n) -> p s n", n=P)).then_inc(e["k_pt_copied"], 1)
                dve.wait_ge(e["k_pt_ready"], NT)
                nc.vector.tensor_copy(aptT[:, :, (NT - 1) * P:NT * P], ps_a[1][:, :].rearrange("p (s n) -> p s n", n=P)).then_inc(e["k_pt_copied"], 1)
                dve.wait_ge(e["k_bias_ready"], 1)
                nc.vector.tensor_copy(bias[:, :, :], ps_b[0][:, :].rearrange("p (t c) -> p t c", c=C)).then_inc(e["k_bias_copied"], 1)
                dve.wait_ge(e["k_p_ready"], NT)
                nc.vector.reciprocal(row_inv[:, :], row_sum[:, :]).then_inc(e["k_inv_ready"], 1)
                for t in range(NT):
                    dve.wait_ge(e["k_x1_copied"], t + 1)
                    dve.wait_ge(e["k_x1_high"], t + 1)
                    nc.vector.tensor_tensor(x1_parts[:, t, 1, :], ps_b[t % 2][:, :], x1_parts[:, t, 0, :].bitcast(F32),
                                            ALU.subtract).then_inc(e["k_x1_rest"], 1)
                for t in range(NT):
                    dve.wait_ge(e["k_x2_ready"], t + 1)
                    nc.vector.scalar_tensor_tensor(g23[:, t, :, 0, :], ps_b[t % 2][:, :].rearrange("p (b c) -> p b c", c=C), 2.0,
                                                   g01[:, t, :, 0, :], ALU.mult, ALU.subtract).then_inc(e["k_x2_copied"], 1)

                def spread(v):
                    return v[:, :].unsqueeze(2).broadcast_to([P, BATCH, C])

                def norm(t, step):
                    yt = y[t % 3]
                    if step == 0:
                        dve.wait_ge(e["k_sum_ready"], BATCH * (t + 1))
                        ins = nc.vector.tensor_tensor(yt[:, :, :], yt[:, :, :], bias[:, t, :].unsqueeze(1).broadcast_to([P, BATCH, C]), ALU.add)
                    elif step < NORM:
                        dve.wait_ge(e["k_norm"], NORM * t + step)
                    if step == 1:
                        ins = nc.vector.tensor_tensor(yt[:, :, :], yt[:, :, :], g01[:, t, :, 0, :], ALU.add)
                    if step == 2:
                        ins = nc.vector.tensor_reduce(mean[:, :], yt[:, :, :], AX.X, ALU.add)
                    if step == 3:
                        ins = nc.vector.tensor_scalar(mean[:, :], mean[:, :], 1.0 / C, None, ALU.mult)
                    if step == 4:
                        ins = nc.vector.tensor_tensor(yt[:, :, :], yt[:, :, :], spread(mean), ALU.subtract)
                    if step < NORM:
                        ins.then_inc(e["k_norm"], 1)
                    if step == 5:
                        dve.wait_ge(e["k_square"], t + 1)
                        if t >= 1:
                            dve.wait_ge(e["k_rstd_ready"], t)
                        nc.vector.tensor_reduce(var[:, :], sq[:, :, :], AX.X, ALU.add).then_inc(e["k_rowvar_ready"], 1)
                        dve.wait_ge(e["k_rowvar_ready"], t + 1)
                        nc.vector.tensor_scalar(var[:, :], var[:, :], 1.0 / C, EPS, ALU.mult, ALU.add).then_inc(e["k_var_ready"], 1)
                    if step == 6:
                        dve.wait_ge(e["k_rstd_ready"], t + 1)
                        nc.vector.tensor_tensor(yt[:, :, :], yt[:, :, :], spread(rstd), ALU.mult).then_inc(e["k_y_done"], 1)

                for u in range(UNITS):
                    t, b = divmod(u, BATCH)
                    dve.wait_ge(e["k_z_ready"], u + 1)
                    if u >= 2:
                        dve.wait_ge(e["k_sum_ready"], u - 1)
                    nc.vector.tensor_tensor(mixed[u % 2][:, :].rearrange("p (d o) -> p d o", o=C),
                                            ps_a[u % 2][:, :].rearrange("p (d o) -> p d o", o=C),
                                            embed[:, t, :].unsqueeze(2).broadcast_to([P, D, C]), ALU.mult).then_inc(e["k_z_scaled"], 1)
                    if b == 0 and t >= 3:
                        dve.wait_ge(e["k_stored"], 16 * (t - 2))
                    dve.wait_ge(e["k_z_scaled"], u + 1)
                    nc.vector.tensor_reduce(y[t % 3][:, b, :], mixed[u % 2][:, :].rearrange("p (d o) -> p o d", o=C), AX.X, ALU.add).then_inc(e["k_sum_ready"], 1)
                    if t >= 1:
                        if b <= 4:
                            norm(t - 1, b)
                        if b == 7:
                            norm(t - 1, 5)
                    if t >= 2 and b == 0:
                        norm(t - 2, 6)
                norm(NT - 2, 6)
                for step in range(7):
                    norm(NT - 1, step)
        nc.all_engine_barrier(sems_to_clear=numbers(setup))


def adjacency_network(nc, io, out):
    adjT = nc.dram_tensor("adjT", (N, N), F32, kind="Internal").ap()
    x1, x2, x3 = (nc.dram_tensor(f"x{i}", (BATCH, N, C), F32, kind="Internal").ap() for i in (1, 2, 3))
    with ExitStack() as ctx:
        bank = [ctx.enter_context(nc.semaphore(f"signal{i}")) for i in range(60)]
        weighted = ctx.enter_context(nc.sbuf_tensor("weighted", [P, 1], I32))
        transpose_adjacency(nc, bank, io, adjT, weighted)
        hypergraph_attention(nc, bank, io, adjT, io["x"], x1)
        multi_head_gat(nc, bank, io, weighted, x1, x2)
        causal_steps(nc, bank, io, adjT, weighted, x2, x3)
        adaptive_chebyshev(nc, bank, io, adjT, weighted, x3, out)


_INS = ['x', 'adj', 'L0_gnn_H', 'L0_gnn_W', 'L0_gnn_W_ind', 'L0_gnn_a_node', 'L0_gnn_a_gn', 'L0_gnn_a_ge',
        'L0_gnn_fcW', 'L0_gnn_fcb', 'L0_gnn_av', 'L1_gnn_Wh', 'L1_gnn_bh', 'L1_gnn_W_out', 'L1_gnn_b_out',
        'L2_gnn_intervention_value', 'L2_gnn_W1', 'L2_gnn_b1', 'L2_gnn_W2', 'L2_gnn_b2',
        'L3_gnn_node_embeddings', 'L3_gnn_weights_pool', 'L3_gnn_bias_pool']


def kernel(**inputs):
    import numpy as _np
    import concourse.bacc as _bacc
    from concourse import mybir as _mybir
    from concourse.bass_utils import run_bass_kernel_spmd as _run

    nc = _bacc.Bacc("TRN2", target_bir_lowering=False, num_devices=1)
    arrays, io = {}, {}
    for name in _INS:
        a = _np.ascontiguousarray(inputs[name])
        arrays[f"in_{name}"] = a
        io[name] = nc.dram_tensor(f"in_{name}", a.shape, _mybir.dt.from_np(a.dtype), kind="ExternalInput").ap()
    out = nc.dram_tensor("out_0", (BATCH, N, C), F32, kind="ExternalOutput").ap()
    adjacency_network(nc, io, out)
    r = _run(nc, [arrays], core_ids=[0])
    return r.results[0]["out_0"]
```
